# Optimizing a Trainium2 kernel written in Bass

```python
import numpy as np
import jax
import jax.numpy as jnp

def _softmax(x, axis=-1):
    return jax.nn.softmax(x, axis=axis)

def _gelu(x):
    return jax.nn.gelu(x, approximate=True)

def _silu(x):
    return jax.nn.silu(x)

def _sigmoid(x):
    return jax.nn.sigmoid(x)

def _layernorm(x, axis=-1, eps=1e-05):
    m = jnp.mean(x, axis=axis, keepdims=True)
    v = jnp.var(x, axis=axis, keepdims=True)
    return (x - m) / jnp.sqrt(v + eps)

def _scatter_add(tgt, idx, src, axis=0):
    return tgt.at[idx].add(src)

def _segment_sum(src, seg, n):
    return jax.ops.segment_sum(src, seg, n)
kernel_name = 'mk_sandwich_d2_jaxref_r8_0ad864'

def setup_inputs(seed: int=0):
    np.random.seed(seed)
    _w = jnp.asarray

    def _L0_attn_setup():
        import jax, jax.numpy as jnp
        import numpy as np
        HIDDEN = 512
        NUM_HEADS = 32
        HEAD_DIM = HIDDEN // NUM_HEADS
        B, S = (2, 128)

        def _alibi_slopes(n):
            start = 2.0 ** (-2.0 ** (-(np.log2(n) - 3)))
            return np.array([start ** (i + 1) for i in range(n)], dtype=np.float32)
        key = jax.random.key(seed)
        k1, k2, k3, k4 = jax.random.split(key, 4)
        hidden_states = jax.random.normal(k1, (B, S, HIDDEN), jnp.float32)
        Wq = jax.random.normal(k2, (HIDDEN, HIDDEN), jnp.float32) * 0.02
        Wkv = jax.random.normal(k3, (HIDDEN, 2 * HEAD_DIM), jnp.float32) * 0.02
        Wo = jax.random.normal(k4, (HIDDEN, HIDDEN), jnp.float32) * 0.02
        return {'hidden_states': hidden_states, 'Wq': Wq, 'Wkv': Wkv, 'Wo': Wo}
    _L0_attn_in = _L0_attn_setup()

    def _L0_ffn_setup():
        import jax, jax.numpy as jnp
        import numpy as np
        key = jax.random.key(seed)
        k = jax.random.split(key, 6)
        x = jax.random.normal(k[0], (4, 256, 512), jnp.float32)
        W = jax.random.normal(k[1], (512, 512), jnp.float32) * 0.02
        bias = jax.random.normal(k[2], (512,), jnp.float32) * 0.02
        A = jax.random.normal(k[3], (16, 16, 512), jnp.float32) * 0.02
        Bf = jax.random.normal(k[4], (16, 512, 16), jnp.float32) * 0.02
        coeffs = jax.random.uniform(k[5], (16,), jnp.float32)
        scales = jnp.full((16,), 0.5, jnp.float32)
        return {'x': x, 'W': W, 'bias': bias, 'A': A, 'Bf': Bf, 'coeffs': coeffs, 'scales': scales}
    _L0_ffn_in = _L0_ffn_setup()

    def _L1_attn_setup():
        import math
        import jax, jax.numpy as jnp
        import numpy as np
        NUM_HEADS = 32
        NUM_KV_HEADS = 8
        HEAD_DIM = 128
        HIDDEN = 512
        ROPE_THETA = 500000.0
        ROPE_FACTOR = 8.0
        HIGH_FF = 4.0
        LOW_FF = 1.0
        ORIG_MAX_POS = 1024

        def _llama3_inv_freq():
            inv = 1.0 / ROPE_THETA ** (np.arange(0, HEAD_DIM, 2, dtype=np.float32) / HEAD_DIM)
            wavelen = 2.0 * np.pi / inv
            low_wl = ORIG_MAX_POS / LOW_FF
            high_wl = ORIG_MAX_POS / HIGH_FF
            inv_scaled = np.where(wavelen > low_wl, inv / ROPE_FACTOR, inv)
            smooth = (ORIG_MAX_POS / wavelen - LOW_FF) / (HIGH_FF - LOW_FF)
            smoothed = (1.0 - smooth) / ROPE_FACTOR * inv + smooth * inv
            is_medium = (wavelen <= low_wl) & (wavelen >= high_wl)
            return jnp.asarray(np.where(is_medium, smoothed, inv_scaled), dtype=jnp.float32)

        def _rotate_half(x):
            h = x.shape[-1] // 2
            return jnp.concatenate([-x[..., h:], x[..., :h]], axis=-1)
        key = jax.random.key(seed)
        ks = jax.random.split(key, 5)
        s = 0.02
        return {'x': jax.random.normal(ks[0], (1, 256, HIDDEN), dtype=jnp.float32), 'Wq': jax.random.normal(ks[1], (NUM_HEADS * HEAD_DIM, HIDDEN), dtype=jnp.float32) * s, 'Wk': jax.random.normal(ks[2], (NUM_KV_HEADS * HEAD_DIM, HIDDEN), dtype=jnp.float32) * s, 'Wv': jax.random.normal(ks[3], (NUM_KV_HEADS * HEAD_DIM, HIDDEN), dtype=jnp.float32) * s, 'Wo': jax.random.normal(ks[4], (HIDDEN, NUM_HEADS * HEAD_DIM), dtype=jnp.float32) * s}
    _L1_attn_in = _L1_attn_setup()

    def _L1_ffn_setup():
        import jax, jax.numpy as jnp
        import numpy as np
        D = 512
        F = 1376
        B, S = (4, 256)
        key = jax.random.key(seed)
        k_x, k_g, k_u, k_d = jax.random.split(key, 4)
        scale = 0.02
        return {'x': jax.random.normal(k_x, (B, S, D), dtype=jnp.float32), 'W_gate': jax.random.normal(k_g, (F, D), dtype=jnp.float32) * scale, 'W_up': jax.random.normal(k_u, (F, D), dtype=jnp.float32) * scale, 'W_down': jax.random.normal(k_d, (D, F), dtype=jnp.float32) * scale}
    _L1_ffn_in = _L1_ffn_setup()
    _d = {'L0_attn_hidden_states': _L0_attn_in['hidden_states'], 'L0_attn_Wq': _L0_attn_in['Wq'], 'L0_attn_Wkv': _L0_attn_in['Wkv'], 'L0_attn_Wo': _L0_attn_in['Wo'], 'L0_ffn_W': _L0_ffn_in['W'], 'L0_ffn_bias': _L0_ffn_in['bias'], 'L0_ffn_A': _L0_ffn_in['A'], 'L0_ffn_Bf': _L0_ffn_in['Bf'], 'L0_ffn_coeffs': _L0_ffn_in['coeffs'], 'L0_ffn_scales': _L0_ffn_in['scales'], 'L1_attn_Wq': _L1_attn_in['Wq'], 'L1_attn_Wk': _L1_attn_in['Wk'], 'L1_attn_Wv': _L1_attn_in['Wv'], 'L1_attn_Wo': _L1_attn_in['Wo'], 'L1_ffn_W_gate': _L1_ffn_in['W_gate'], 'L1_ffn_W_up': _L1_ffn_in['W_up'], 'L1_ffn_W_down': _L1_ffn_in['W_down']}
    _x0 = _d['L0_attn_hidden_states']
    _d['L0_attn_hidden_states'] = jax.random.normal(jax.random.fold_in(jax.random.key(seed), 1), (4, 256, 512), dtype=_x0.dtype)
    del _x0
    return _d

def reference(L0_attn_hidden_states, L0_attn_Wq, L0_attn_Wkv, L0_attn_Wo, L0_ffn_W, L0_ffn_bias, L0_ffn_A, L0_ffn_Bf, L0_ffn_coeffs, L0_ffn_scales, L1_attn_Wq, L1_attn_Wk, L1_attn_Wv, L1_attn_Wo, L1_ffn_W_gate, L1_ffn_W_up, L1_ffn_W_down):

    def _L0_attn_ref(hidden_states, Wq, Wkv, Wo):
        import jax, jax.numpy as jnp
        import numpy as np
        HIDDEN = 512
        NUM_HEADS = 32
        HEAD_DIM = HIDDEN // NUM_HEADS
        B, S = (2, 128)

        def _alibi_slopes(n):
            start = 2.0 ** (-2.0 ** (-(np.log2(n) - 3)))
            return np.array([start ** (i + 1) for i in range(n)], dtype=np.float32)
        b, s, h = hidden_states.shape
        scale = HEAD_DIM ** (-0.5)
        q = (hidden_states @ Wq).reshape(b, s, NUM_HEADS, HEAD_DIM)
        kv = hidden_states @ Wkv
        k, v = (kv[..., :HEAD_DIM], kv[..., HEAD_DIM:])
        scores = jnp.einsum('bqhd,bkd->bhqk', q, k) * scale
        pos = jnp.arange(s)
        slopes = jnp.asarray(_alibi_slopes(NUM_HEADS))
        bias = slopes[:, None, None] * (pos[None, None, :] - pos[None, :, None]).astype(jnp.float32)
        causal = pos[None, :] <= pos[:, None]
        scores = jnp.where(causal[None, None], scores + bias[None], -jnp.inf)
        attn = jax.nn.softmax(scores, axis=-1)
        out = jnp.einsum('bhqk,bkd->bqhd', attn, v).reshape(b, s, h)
        return out @ Wo

    def _L0_ffn_ref(x, W, bias, A, Bf, coeffs, scales):
        import jax, jax.numpy as jnp
        import numpy as np
        out = jnp.einsum('bsd,od->bso', x, W) + bias
        xa = jnp.einsum('bsd,erd->ebsr', x, A)
        w = coeffs * scales
        upd = jnp.einsum('ebsr,eor,e->bso', xa, Bf, w)
        return out + upd

    def _L1_attn_ref(x, Wq, Wk, Wv, Wo):
        import math
        import jax, jax.numpy as jnp
        import numpy as np
        NUM_HEADS = 32
        NUM_KV_HEADS = 8
        HEAD_DIM = 128
        HIDDEN = 512
        ROPE_THETA = 500000.0
        ROPE_FACTOR = 8.0
        HIGH_FF = 4.0
        LOW_FF = 1.0
        ORIG_MAX_POS = 1024

        def _llama3_inv_freq():
            inv = 1.0 / ROPE_THETA ** (np.arange(0, HEAD_DIM, 2, dtype=np.float32) / HEAD_DIM)
            wavelen = 2.0 * np.pi / inv
            low_wl = ORIG_MAX_POS / LOW_FF
            high_wl = ORIG_MAX_POS / HIGH_FF
            inv_scaled = np.where(wavelen > low_wl, inv / ROPE_FACTOR, inv)
            smooth = (ORIG_MAX_POS / wavelen - LOW_FF) / (HIGH_FF - LOW_FF)
            smoothed = (1.0 - smooth) / ROPE_FACTOR * inv + smooth * inv
            is_medium = (wavelen <= low_wl) & (wavelen >= high_wl)
            return jnp.asarray(np.where(is_medium, smoothed, inv_scaled), dtype=jnp.float32)

        def _rotate_half(x):
            h = x.shape[-1] // 2
            return jnp.concatenate([-x[..., h:], x[..., :h]], axis=-1)
        B, T, _ = x.shape
        G = NUM_HEADS // NUM_KV_HEADS
        q = jnp.einsum('bth,oh->bto', x, Wq).reshape(B, T, NUM_HEADS, HEAD_DIM).transpose(0, 2, 1, 3)
        k = jnp.einsum('bth,oh->bto', x, Wk).reshape(B, T, NUM_KV_HEADS, HEAD_DIM).transpose(0, 2, 1, 3)
        v = jnp.einsum('bth,oh->bto', x, Wv).reshape(B, T, NUM_KV_HEADS, HEAD_DIM).transpose(0, 2, 1, 3)
        inv_freq = _llama3_inv_freq()
        pos = jnp.arange(T, dtype=jnp.float32)
        freqs = pos[:, None] * inv_freq[None, :]
        emb = jnp.concatenate([freqs, freqs], axis=-1)
        cos, sin = (jnp.cos(emb), jnp.sin(emb))
        q = q * cos + _rotate_half(q) * sin
        k = k * cos + _rotate_half(k) * sin
        qg = q.reshape(B, NUM_KV_HEADS, G, T, HEAD_DIM)
        scale = 1.0 / math.sqrt(HEAD_DIM)
        scores = jnp.einsum('bkgtd,bksd->bkgts', qg, k) * scale
        causal = jnp.tril(jnp.ones((T, T), dtype=bool))
        scores = jnp.where(causal, scores, -jnp.inf)
        attn = jax.nn.softmax(scores, axis=-1)
        out = jnp.einsum('bkgts,bksd->bkgtd', attn, v)
        out = out.reshape(B, NUM_HEADS, T, HEAD_DIM).transpose(0, 2, 1, 3).reshape(B, T, NUM_HEADS * HEAD_DIM)
        return jnp.einsum('bto,ho->bth', out, Wo)

    def _L1_ffn_ref(x, W_gate, W_up, W_down):
        import jax, jax.numpy as jnp
        import numpy as np
        D = 512
        F = 1376
        B, S = (4, 256)
        out_shape = x.shape[:-1] + (W_down.shape[0],)
        xt = x.reshape(-1, x.shape[-1])
        up = xt @ W_up.T
        gate = jax.nn.silu(xt @ W_gate.T)
        y = gate * up @ W_down.T
        return y.reshape(out_shape)
    x = L0_attn_hidden_states
    x = x + _layernorm(_L0_attn_ref(_layernorm(x, axis=-1), L0_attn_Wq, L0_attn_Wkv, L0_attn_Wo), axis=-1)
    x = x + _layernorm(_L0_ffn_ref(_layernorm(x, axis=-1), L0_ffn_W, L0_ffn_bias, L0_ffn_A, L0_ffn_Bf, L0_ffn_coeffs, L0_ffn_scales), axis=-1)
    x = x + _layernorm(_L1_attn_ref(_layernorm(x, axis=-1), L1_attn_Wq, L1_attn_Wk, L1_attn_Wv, L1_attn_Wo), axis=-1)
    x = x + _layernorm(_L1_ffn_ref(_layernorm(x, axis=-1), L1_ffn_W_gate, L1_ffn_W_up, L1_ffn_W_down), axis=-1)
    return x

_drawn_inputs = setup_inputs


def setup_inputs(seed=0):
    import zlib

    import numpy as np

    out = dict(_drawn_inputs(seed))
    spreads = {'L0_ffn_scales': (0.5, 0.6)}
    factors = {}
    for name, (base, spread) in spreads.items():
        noise = np.random.default_rng([zlib.crc32(name.encode()), seed]).standard_normal(out[name].shape)
        drawn = base * np.exp(spread * noise) if base else spread * noise
        out[name] = jnp.asarray(drawn.astype(out[name].dtype))
    for name, factor in factors.items():
        out[name] = (out[name] * factor).astype(out[name].dtype)
    return out
```

```python
from contextlib import ExitStack

import numpy as np

import concourse.bass as bass
from concourse import mybir

F32 = mybir.dt.float32
F32R = mybir.dt.float32r
F16 = mybir.dt.float16
BF16 = mybir.dt.bfloat16
ALU = mybir.AluOpType
ACT = mybir.ActivationFunctionType

P = 128
NB, TB = 4, 256
BT = TB // P
NT = NB * BT
D = 512
KD = D // P
EPS = 1e-5
MASKED = -1e32

H0, HD0 = 32, 16
HPT = P // HD0
SC0 = HD0 ** -0.5
SLOTS = 4
PROB_SCALE = 2.0 ** 15
NEXP, RANK = 16, 16
ER = NEXP * RANK // P

NG, HG, HD1 = 8, 4, 128
SC1 = HD1 ** -0.5
QW = HG * HD1
GW = QW + 2 * HD1

F = 1376
FT = (F + P - 1) // P

SW = P + 2 * P


def alibi_slopes(n):
    start = 2.0 ** (-2.0 ** (-(np.log2(n) - 3)))
    return np.array([start ** (i + 1) for i in range(n)], dtype=np.float32)


def rope_tables():
    theta, factor, high, low, orig = 500000.0, 8.0, 4.0, 1.0, 1024
    inv = 1.0 / theta ** (np.arange(0, HD1, 2, dtype=np.float32) / HD1)
    wavelen = 2.0 * np.pi / inv
    scaled = np.where(wavelen > orig / low, inv / factor, inv)
    smooth = (orig / wavelen - low) / (high - low)
    smoothed = (1.0 - smooth) / factor * inv + smooth * inv
    medium = (wavelen <= orig / low) & (wavelen >= orig / high)
    inv = np.where(medium, smoothed, scaled).astype(np.float32)
    freqs = (np.arange(TB, dtype=np.float32)[None, :] * inv[:, None]).astype(np.float32)
    cos, sin = np.cos(freqs), np.sin(freqs)
    return (np.concatenate([cos, cos]).astype(np.float32),
            np.concatenate([-sin, sin]).astype(np.float32))


def constants():
    q, c = np.arange(P)[:, None], np.arange(2 * P)[None, :]
    hidden = np.where(c - P > q, np.float32(MASKED), np.float32(0))
    cos, sin = rope_tables()
    return {
        "ident": np.eye(P, dtype=np.float32),
        "causal": hidden.astype(np.float32),
        "distance": (c - (2 * P - 1) + hidden).astype(np.float32),
        "slot_rows": (np.arange(P)[:, None] // HD0 % 2 == np.arange(2)[None, :]).astype(np.float32),
        "cos": cos, "sin": sin,
    }


def stand_apart(engine):
    engine.nop(nofuse=True)


class Norm:

    def __init__(self, name, sb, sem):
        self.six = sb(f"{name}_six", [P, BT, 6], F32)
        self.mv = sb(f"{name}_mv", [P, BT, 2], F32)
        self.var_eps = sb(f"{name}_var_eps", [P, BT], F32)
        self.rstd = sb(f"{name}_rstd", [P, BT], F32)
        self.stats_done = sem(f"{name}_stats_done")
        self.moments_done = sem(f"{name}_moments_done")
        self.var_ready = sem(f"{name}_var_ready")
        self.rstd_ready = sem(f"{name}_rstd_ready")
        self.normed = sem(f"{name}_normed")

    def moments(self, dve, b, source, apart=False):
        for t in range(BT):
            if apart and t == 0:
                stand_apart(dve)
            dve.bn_stats(self.six[:, t, :], source(t)).then_inc(self.stats_done, 1)
        dve.wait_ge(self.stats_done, b * BT + BT)
        stand_apart(dve)
        for t in range(BT):
            dve.bn_aggr(self.mv[:, t, :], self.six[:, t, :]).then_inc(self.moments_done, 1)
        dve.wait_ge(self.moments_done, b * BT + BT)
        dve.tensor_scalar(self.var_eps[:, :], self.mv[:, :, 1], EPS, None, ALU.add)\
           .then_inc(self.var_ready, 1)

    def inverse(self, pool, b, minus_half):
        pool.wait_ge(self.var_ready, b + 1)
        pool.tensor_tensor(self.rstd[:, :], self.var_eps[:, :], minus_half, ALU.pow)\
            .then_inc(self.rstd_ready, 1)

    def apply(self, dve, b, source, target):
        dve.wait_ge(self.rstd_ready, b + 1)
        for t in range(BT):
            dve.tensor_scalar(target(t), source(t), self.mv[:, t, 0:1], self.rstd[:, t:t + 1],
                              ALU.subtract, ALU.mult).then_inc(self.normed, 1)


def split_product(pe, out, left, right, first, last):
    (lh, ll), (rh, rl) = left, right
    pe.matmul(out, lh, rh, start=first, stop=False)
    pe.matmul(out, lh, rl, start=False, stop=False)
    return pe.matmul(out, ll, rh, start=False, stop=last)


def layer0(nc, dram, X, ps, consts):
    ident, minus_half, consts_in = consts["ident"], consts["minus_half"], consts["in"]
    ctx = ExitStack()
    sb = lambda name, shape, dt: ctx.enter_context(nc.sbuf_tensor(name, shape, dt))
    sem = lambda name: nc.semaphore(name).__enter__()

    stage = sb("stage0", [P, KD, D], F32)
    kv_raw = sb("kv_raw0", [P, KD, P + HD0], F32)
    w_eff = sb("w_eff", [P, KD, D], F32)
    a_raw = sb("a_raw", [P, ER, D], F32)
    bf_raw = sb("bf_raw", [P, ER, D], F32)
    gate_w = sb("gate_w", [P, 2, ER], F32)
    gate_p = sb("gate_p", [P, ER], F32)
    bias_b = sb("bias_b", [P, D], F32)
    wq = [sb(f"wq0_{x}", [P, KD, D], F32R) for x in ("hi", "lo")]
    wkv = [sb(f"wkv0_{x}", [P, KD, P + HD0], F32R) for x in ("hi", "lo")]
    wo = [sb(f"wo0_{x}", [P, KD, D], F32R) for x in ("hi", "lo")]
    wf = [sb(f"wf0_{x}", [P, KD, D], F32R) for x in ("hi", "lo")]
    distance = sb("distance", [P, 2 * P], F32)
    slot_rows = sb("slot_rows", [P, 2], F32)
    alibi = sb("alibi", [P, H0, 2 * P], F32)
    tok = sb("tok0", [P, BT, D], F32)
    delta = sb("delta0", [P, BT, D], F32)
    xT = [sb(f"xT0_{x}", [P, KD, TB], F32R) for x in ("hi", "lo")]
    q_slots = sb("q_slots", [P, BT, H0, SLOTS, HD0], F32R)
    qT = sb("qT0", [P, H0 // 2, TB], F32R)
    k_rows = [sb(f"k_rows_{x}", [P, TB], F32R) for x in ("hi", "lo")]
    kT_half = sb("kT_half", [P, TB], F32)
    kT = sb("kT0", [P, TB], F32R)
    v = sb("v0", [P, BT, HD0], F32)
    v_rest = sb("v_rest0", [P, 2, BT, HD0], F32)
    v_parts = sb("v_parts0", [P, 3, BT, HD0], BF16)
    prob = sb("prob0", [P, 4, SW], F32)
    neg_max = sb("neg_max0", [P, 4, 2], F32)
    row_sum = sb("row_sum0", [P, H0, 2], F32)
    row_inv = sb("row_inv0", [P, H0, 2], F32)
    probT = [sb(f"probT0_{x}", [P, 4, SW], F16) for x in ("hi", "lo")]
    fT = [sb(f"fT0_{x}", [P, KD, TB], F32R) for x in ("hi", "lo")]

    ln1, ln2, ln3, ln4 = (Norm(f"ln{n}", sb, sem) for n in (1, 2, 3, 4))

    x_in = [sem(f"x_in{b}") for b in range(NB)]
    wq_in, kv_in, wo_in, wf_in, small_in = (sem(n) for n in ("wq_in", "kv_in", "wo_in", "wf_in", "small_in"))
    wq_hi, wq_lo, wkv_hi, wkv_lo = (sem(n) for n in ("wq_hi", "wq_lo", "wkv_hi", "wkv_lo"))
    wo_hi, wo_lo, wf_hi, wf_lo = (sem(n) for n in ("wo_hi", "wo_lo", "wf_hi", "wf_lo"))
    gate_done, bf_scaled, adapters_done, w_eff_done = (sem(n) for n in ("gate_done", "bf_scaled", "adapters_done", "w_eff_done"))
    alibi_done = sem("alibi_done")
    xT_done, xT_hi, xT_lo = (sem(n) for n in ("xT_done0", "xT_hi0", "xT_lo0"))
    kv_done, k_hi, k_lo, v_out = (sem(n) for n in ("kv_done0", "k_hi0", "k_lo0", "v_out0"))
    kT_halved, kT_out, v_split = (sem(n) for n in ("kT_halved0", "kT_out0", "v_split0"))
    q_done, q_hi, q_lo = (sem(n) for n in ("q_done0", "q_hi0", "q_lo0"))
    qT_done, qT_act, qT_dve = (sem(n) for n in ("qT_done0", "qT_act0", "qT_dve0"))
    s_done, masked, exp_done, pT_done, pT_hi, pv_done, pT_lo = (sem(n) for n in ("s_done0", "masked0", "exp_done0", "pT_done0", "pT_hi0", "pv_done0", "pT_lo0"))
    inv_done, o_out, oT_done, oT_hi, oT_lo = (sem(n) for n in ("inv_done0", "o_out0", "oT_done0", "oT_hi0", "oT_lo0"))
    wo_done, x1_done, x1T_done, x1T_hi, x1T_lo = (sem(n) for n in ("wo_done0", "x1_done0", "x1T_done0", "x1T_hi0", "x1T_lo0"))
    ffn_done, biased, x2_done = (sem(n) for n in ("ffn_done0", "biased0", "x2_done0"))

    slopes = alibi_slopes(H0)

    LAG_T, LAG_HI, LAG_LO, LAG_V = 2, 3, 4, 5
    QG = H0 // 4
    STEPS = H0 + LAG_V
    AT = {"wo": 4, "n2": 6, "x1": 9, "n3": 10, "a3": 13, "x1T": 14, "x1T_out": 15, "ffn": 18, "n4": 20, "x2": 23}

    def q_bank(t):
        return ps[7 - t][:, :].rearrange("p (h a d) -> p h a d", h=H0, a=1).to_broadcast([P, H0, 2, HD0])

    def xrow(b, t):
        return X[:, b * BT + t, :]

    def sync(sp):
        for b in range(NB):
            sp.dma_start(X[:, b * BT:(b + 1) * BT, :], dram["x"].rearrange("(n p) d -> p n d", p=P)[:, b * BT:(b + 1) * BT, :])\
              .then_inc(x_in[b], 16)
            if b == 0:
                sp.dma_start(kv_raw[:, :, :], dram["wkv0"]).then_inc(kv_in, 16)
                sp.dma_start(stage[:, :, :], dram["wq0"].rearrange("(k p) n -> p k n", p=P)).then_inc(wq_in, 16)
        sp.dma_start(w_eff[:, :, :], dram["wf0"].rearrange("(k p) n -> p k n", p=P)).then_inc(wf_in, 16)
        sp.dma_start(a_raw[:, :, :], dram["a0"].rearrange("(k p) n -> p k n", p=P)).then_inc(wf_in, 16)
        sp.dma_start(bf_raw[:, :, :], dram["bf0"].rearrange("(k p) n -> p k n", p=P)).then_inc(wf_in, 16)
        sp.wait_ge(wq_lo, 1)
        sp.dma_start(stage[:, :, :], dram["wo0"].rearrange("(k p) n -> p k n", p=P)).then_inc(wo_in, 16)

    def sync_consts(act):
        act.dma_start(distance[:, :], dram["distance"]).then_inc(small_in, 16)
        act.dma_start(slot_rows[:, :], dram["slot_rows"]).then_inc(small_in, 16)
        act.dma_start(gate_w[:, :, :], dram["gate_w"]).then_inc(small_in, 16)
        act.dma_start(bias_b[:, :], dram["bias0"].partition_broadcast(P)).then_inc(small_in, 16)

    def pool(pl):
        pl.wait_ge(small_in, 64)
        ln1.inverse(pl, 0, minus_half[:, 0:BT])
        for h in range(H0):
            pl.tensor_scalar(alibi[:, h, :], distance[:, :], float(slopes[h]) / SC0, 1.0, ALU.mult, ALU.mult)\
              .then_inc(alibi_done, 1)
        split_v(pl, 0)
        pl.wait_ge(wo_in, 16)
        pl.tensor_scalar(wo[0][:, :, :], stage[:, :, :], 1.0, 1.0, ALU.mult, ALU.mult).then_inc(wo_hi, 1)
        pl.wait_ge(wo_hi, 1)
        pl.tensor_tensor(wo[1][:, :, :], stage[:, :, :], wo[0][:, :, :].bitcast(F32), ALU.subtract).then_inc(wo_lo, 1)
        pl.wait_ge(w_eff_done, KD)
        pl.tensor_scalar(wf[0][:, :, :], w_eff[:, :, :], 1.0, 1.0, ALU.mult, ALU.mult).then_inc(wf_hi, 1)
        pl.wait_ge(wf_hi, 1)
        pl.tensor_tensor(wf[1][:, :, :], w_eff[:, :, :], wf[0][:, :, :].bitcast(F32), ALU.subtract).then_inc(wf_lo, 1)
        with pl.Fori(1, NB) as b:
            ln1.inverse(pl, b, minus_half[:, 0:BT])
            split_v(pl, b)
            tail_inverses(pl, b - 1)
        tail_inverses(pl, NB - 1)

    def split_v(pl, b):
        pl.wait_ge(v_out, b + 1)
        if not isinstance(b, int):
            pl.wait_ge(pv_done, b * H0)
        stand_apart(pl)
        pl.tensor_copy(v_parts[:, 0, :, :], v[:, :, :]).then_inc(v_split, 1)
        for n, (left, rest) in enumerate(((v[:, :, :], v_rest[:, 0, :, :]), (v_rest[:, 0, :, :], v_rest[:, 1, :, :]))):
            pl.wait_ge(v_split, b * 5 + 2 * n + 1)
            pl.tensor_tensor(rest, left, v_parts[:, n, :, :], ALU.subtract).then_inc(v_split, 1)
            pl.wait_ge(v_split, b * 5 + 2 * n + 2)
            stand_apart(pl)
            pl.tensor_copy(v_parts[:, n + 1, :, :], rest).then_inc(v_split, 1)

    def tail_inverses(pl, b):
        ln2.inverse(pl, b, minus_half[:, 0:BT])
        ln3.inverse(pl, b, minus_half[:, 0:BT])
        ln4.inverse(pl, b, minus_half[:, 0:BT])

    def scalar(act):
        sync_consts(act)
        act.wait_ge(kv_in, 16)
        act.activation(wkv[0][:, :, :], kv_raw[:, :, :], ACT.Copy).then_inc(wkv_hi, 1)
        act.wait_ge(wq_in, 16)
        act.activation(wq[0][:, :, :], stage[:, :, :], ACT.Copy).then_inc(wq_hi, 1)
        act_batch(act, 0, False)
        with act.Fori(1, NB) as b:
            act_batch(act, b, True)
        act_tail(act, NB - 1, None)

    def act_batch(act, b, with_tail):
        first = not with_tail
        for t in range(BT):
            act.wait_ge(xT_done, b * BT + t + 1)
            act.activation(xT[0][:, :, t * P:(t + 1) * P], ps[6 + t][:, :].rearrange("p (k n) -> p k n", k=KD),
                           ACT.Copy).then_inc(xT_hi, 1)
        act.wait_ge(kv_done, b + 1)
        if with_tail:
            act.wait_ge(v_split, b * 5)
        act.activation(v[:, :, :], ps[6][:, TB:TB + BT * HD0].rearrange("p (t n) -> p t n", t=BT), ACT.Copy,
                       scale=1.0 / PROB_SCALE).then_inc(v_out, 1)
        act.activation(k_rows[0][:, :], ps[6][:, 0:TB], ACT.Copy).then_inc(k_hi, 1)
        for t in range(BT):
            act.wait_ge(q_done, b * BT + t + 1)
            act.activation(q_slots[:, t, :, 0:2, :], q_bank(t), ACT.Copy).then_inc(q_hi, 1)
        for n in range(0, QG, 2):
            act.wait_ge(qT_done, b * QG + n + 1)
            act.activation(qT[:, 2 * n:2 * n + 2, :], ps[n % 4][:, :].rearrange("p (k n) -> p k n", k=2), ACT.Copy)\
               .then_inc(qT_act, 1)
        if with_tail:
            act.wait_ge(inv_done, b)
        for step in range(STEPS):
            if 0 <= step - LAG_HI < H0:
                h = step - LAG_HI
                act.wait_ge(pT_done, b * H0 + h + 1)
                if not (first and h < 4):
                    act.wait_ge(pv_done, b * H0 + h - 3)
                act.activation(probT[0][:, h % 4, :], ps[2 + h % 2][:, 0:SW], ACT.Copy, scale=PROB_SCALE).then_inc(pT_hi, 1)
            if step < H0:
                h = step
                act.wait_ge(masked, b * (2 * H0) + 2 * h + 2)
                for qb, (c0, c1) in enumerate(((0, P), (P, SW))):
                    act.activation(prob[:, h % 4, c0:c1], prob[:, h % 4, c0:c1], ACT.Exp,
                                   bias=neg_max[:, h % 4, qb:qb + 1], scale=-1.0,
                                   accum_out=row_sum[:, h, qb:qb + 1]).then_inc(exp_done, 1)
            if with_tail:
                act_tail(act, b - 1, step)
        for t in range(BT):
            act.wait_ge(oT_done, b * BT + t + 1)
            act.activation(fT[0][:, :, t * P:(t + 1) * P], ps[6 + t][:, :].rearrange("p (k n) -> p k n", k=KD),
                           ACT.Copy).then_inc(oT_hi, 1)

    def act_tail(act, b, step):
        if step in (AT["x1T_out"], None):
            for t in range(BT):
                act.wait_ge(x1T_done, b * BT + t + 1)
                act.activation(fT[0][:, :, t * P:(t + 1) * P], ps[6 + t][:, :].rearrange("p (k n) -> p k n", k=KD),
                               ACT.Copy).then_inc(x1T_hi, 1)

    def lo_part(dve, hi, lo, source, ready, count, done):
        dve.wait_ge(ready, count)
        dve.tensor_tensor(lo, source, hi.bitcast(F32), ALU.subtract).then_inc(done, 1)

    def vector(dve):
        dve.wait_ge(x_in[0], 16)
        ln1.moments(dve, 0, lambda t: xrow(0, t))
        dve.wait_ge(wkv_hi, 1)
        dve.tensor_tensor(wkv[1][:, :, :], kv_raw[:, :, :], wkv[0][:, :, :].bitcast(F32), ALU.subtract).then_inc(wkv_lo, 1)
        ln1.apply(dve, 0, lambda t: xrow(0, t), lambda t: tok[:, t, :])
        dve.wait_ge(wq_hi, 1)
        dve.tensor_tensor(wq[1][:, :, :], stage[:, :, :], wq[0][:, :, :].bitcast(F32), ALU.subtract).then_inc(wq_lo, 1)
        dve_batch(dve, 0, False)
        for b in range(1, NB):
            dve.wait_ge(x_in[b], 16)
        with dve.Fori(1, NB) as b:
            ln1.moments(dve, b, lambda t: xrow(b, t), True)
            dve.wait_ge(oT_done, b * BT)
            ln1.apply(dve, b, lambda t: xrow(b, t), lambda t: tok[:, t, :])
            dve_batch(dve, b, True)
        dve_tail(dve, NB - 1, None)

    def merge_adapters(dve):
        for k in range(KD):
            dve.wait_ge(adapters_done, k + 1)
            dve.tensor_tensor(w_eff[:, k, :], ps[7 - k % 2][:, :], w_eff[:, k, :], ALU.add).then_inc(w_eff_done, 1)

    def dve_batch(dve, b, with_tail):
        first = not with_tail
        for t in range(BT):
            lo_part(dve, xT[0][:, :, t * P:(t + 1) * P], xT[1][:, :, t * P:(t + 1) * P],
                    ps[6 + t][:, :].rearrange("p (k n) -> p k n", k=KD), xT_hi, b * BT + t + 1, xT_lo)
        lo_part(dve, k_rows[0][:, :], k_rows[1][:, :], ps[6][:, 0:TB], k_hi, b + 1, k_lo)
        if first:
            dve.wait_ge(small_in, 64)
        dve.wait_ge(k_lo, b + 1)
        dve.tensor_scalar(kT_half[:, :], k_rows[0][:, :].bitcast(F32), slot_rows[:, 0:1], None, ALU.mult).then_inc(kT_halved, 1)
        dve.wait_ge(kT_halved, b + 1)
        dve.scalar_tensor_tensor(kT[:, :], k_rows[1][:, :].bitcast(F32), slot_rows[:, 1:2], kT_half[:, :],
                                 ALU.mult, ALU.add).then_inc(kT_out, 1)
        for t in range(BT):
            dve.wait_ge(q_hi, b * BT + t + 1)
            dve.tensor_tensor(q_slots[:, t, :, 2:4, :], q_bank(t), q_slots[:, t, :, 0:2, :].bitcast(F32), ALU.subtract)\
               .then_inc(q_lo, 1)
        for n in range(1, QG, 2):
            dve.wait_ge(qT_done, b * QG + n + 1)
            dve.tensor_copy(qT[:, 2 * n:2 * n + 2, :], ps[n % 4][:, :].rearrange("p (k n) -> p k n", k=2)).then_inc(qT_dve, 1)
        if not with_tail:
            dve.wait_ge(wf_in, 48)
            dve.tensor_tensor(gate_p[:, :], gate_w[:, 0, :], gate_w[:, 1, :], ALU.mult).then_inc(gate_done, 1)
            dve.wait_ge(gate_done, 1)
            for r in range(ER):
                dve.tensor_scalar(bf_raw[:, r, :], bf_raw[:, r, :], gate_p[:, r:r + 1], None, ALU.mult).then_inc(bf_scaled, 1)
        for step in range(STEPS):
            if 0 <= step - LAG_LO < H0:
                h = step - LAG_LO
                dve.wait_ge(pT_hi, b * H0 + h + 1)
                dve.scalar_tensor_tensor(probT[1][:, h % 4, :], ps[2 + h % 2][:, 0:SW], PROB_SCALE, probT[0][:, h % 4, :],
                                         ALU.mult, ALU.subtract).then_inc(pT_lo, 1)
            if step < H0:
                h = step
                dve.wait_ge(s_done, b * H0 + h + 1)
                if first:
                    dve.wait_ge(alibi_done, h + 1)
                if not (first and h < 4):
                    dve.wait_ge(pT_done, b * H0 + h - 3)
                stand_apart(dve)
                for qb, (c0, c1) in enumerate(((0, P), (P, SW))):
                    dve.tensor_tensor_reduce(prob[:, h % 4, c0:c1], ps[h % 2][:, c0:c1], alibi[:, h, 2 * P - (c1 - c0):2 * P],
                                             -SC0, 3e38, ALU.add, ALU.min, neg_max[:, h % 4, qb:qb + 1]).then_inc(masked, 1)
            if not with_tail and step == 6:
                merge_adapters(dve)
            if with_tail:
                dve_tail(dve, b - 1, step)
        dve.wait_ge(exp_done, b * (2 * H0) + 2 * H0)
        dve.reciprocal(row_inv[:, :, :], row_sum[:, :, :]).then_inc(inv_done, 1)
        dve.wait_ge(inv_done, b + 1)
        dve.wait_ge(pv_done, b * H0 + H0)
        if with_tail:
            dve.wait_ge(x1T_done, b * BT)
        for t in range(BT):
            dve.tensor_tensor(tok[:, t, :].rearrange("p (h d) -> p h d", h=H0),
                              ps[4 + t][:, :].rearrange("p (h d) -> p h d", h=H0),
                              row_inv[:, :, t:t + 1].to_broadcast([P, H0, HD0]), ALU.mult).then_inc(o_out, 1)
        for t in range(BT):
            lo_part(dve, fT[0][:, :, t * P:(t + 1) * P], fT[1][:, :, t * P:(t + 1) * P],
                    ps[6 + t][:, :].rearrange("p (k n) -> p k n", k=KD), oT_hi, b * BT + t + 1, oT_lo)

    def add_delta(dve, b, norm, done):
        dve.wait_ge(norm.normed, b * BT + BT)
        for t in range(BT):
            dve.tensor_tensor(xrow(b, t), xrow(b, t), delta[:, t, :], ALU.add).then_inc(done, 1)

    def dve_tail(dve, b, step):
        if step in (AT["n2"], None):
            dve.wait_ge(wo_done, b * BT + BT)
            ln2.moments(dve, b, lambda t: ps[6 + t][:, :])
        if step in (AT["x1"], None):
            ln2.apply(dve, b, lambda t: ps[6 + t][:, :], lambda t: delta[:, t, :])
            add_delta(dve, b, ln2, x1_done)
        if step in (AT["n3"], None):
            dve.wait_ge(x1_done, b * BT + BT)
            ln3.moments(dve, b, lambda t: xrow(b, t), True)
        if step in (AT["a3"], None):
            if step is None:
                dve.wait_ge(oT_done, NB * BT)
            else:
                dve.wait_ge(xT_done, b * BT + 2 * BT)
            ln3.apply(dve, b, lambda t: xrow(b, t), lambda t: tok[:, t, :])
        if step in (AT["x1T_out"], None):
            for t in range(BT):
                lo_part(dve, fT[0][:, :, t * P:(t + 1) * P], fT[1][:, :, t * P:(t + 1) * P],
                        ps[6 + t][:, :].rearrange("p (k n) -> p k n", k=KD), x1T_hi, b * BT + t + 1, x1T_lo)
        if step in (AT["n4"], None):
            for t in range(BT):
                dve.wait_ge(ffn_done, b * BT + t + 1)
                dve.tensor_tensor(delta[:, t, :], ps[6 + t][:, :], bias_b[:, :], ALU.add).then_inc(biased, 1)
            dve.wait_ge(biased, b * BT + BT)
            ln4.moments(dve, b, lambda t: delta[:, t, :])
        if step in (AT["x2"], None):
            ln4.apply(dve, b, lambda t: delta[:, t, :], lambda t: delta[:, t, :])
            add_delta(dve, b, ln4, x2_done)

    def tensor(pe):
        pe_batch(pe, 0, False)
        with pe.Fori(1, NB) as b:
            pe_batch(pe, b, True)
        pe_tail(pe, NB - 1, None)

    def transpose_tok(pe, t, done):
        for k in range(KD):
            last = pe.transpose(ps[6 + t][:, k * P:(k + 1) * P], tok[:, t, k * P:(k + 1) * P], ident[:, :])
        last.then_inc(done, 1)

    def pe_batch(pe, b, with_tail):
        first = not with_tail
        pe.wait_ge(consts_in, 16)
        for t in range(BT):
            pe.wait_ge(ln1.normed, b * BT + t + 1)
            if with_tail:
                pe.wait_ge(oT_lo, b * BT)
            transpose_tok(pe, t, xT_done)
        if not with_tail:
            pe.wait_ge(wkv_lo, 1)
        pe.wait_ge(xT_lo, b * BT + BT)
        for k in range(KD):
            split_product(pe, ps[6][:, 0:TB], (wkv[0][:, k, 0:P], wkv[1][:, k, 0:P]),
                          (xT[0][:, k, :], xT[1][:, k, :]), k == 0, k == KD - 1)
        for t in range(BT):
            for k in range(KD):
                last = split_product(pe, ps[6][:, TB + t * HD0:TB + (t + 1) * HD0],
                                     (xT[0][:, k, t * P:(t + 1) * P], xT[1][:, k, t * P:(t + 1) * P]),
                                     (wkv[0][:, k, P:P + HD0], wkv[1][:, k, P:P + HD0]), k == 0, k == KD - 1)
        last.then_inc(kv_done, 1)
        if not with_tail:
            pe.wait_ge(wq_lo, 1)
        for t in range(BT):
            if t == 1:
                pe.wait_ge(k_lo, b + 1)
                pe.wait_ge(v_out, b + 1)
            for k in range(KD):
                last = split_product(pe, ps[7 - t][:, :], (xT[0][:, k, t * P:(t + 1) * P], xT[1][:, k, t * P:(t + 1) * P]),
                                     (wq[0][:, k, :], wq[1][:, k, :]), k == 0, k == KD - 1)
            last.then_inc(q_done, 1)
        if with_tail:
            pe.wait_ge(masked, b * (2 * H0))
            pe.wait_ge(pT_lo, b * H0)
        pe.wait_ge(q_lo, b * BT + BT)
        for n in range(QG):
            if n >= 4:
                pe.wait_ge((qT_act, qT_dve)[n % 2], b * (QG // 2) + n // 2 - 1)
            for c in range(4):
                pair, t = 2 * n + c // 2, c % 2
                last = pe.transpose(ps[n % 4][:, c * P:(c + 1) * P],
                                    q_slots[:, t, 2 * pair:2 * pair + 2, :, :].rearrange("p h s d -> p (h s d)").bitcast(F32), ident[:, :])
            last.then_inc(qT_done, 1)
        for step in range(STEPS):
            if step < H0:
                h = step
                rows = slice(64 * (h % 2), 64 * (h % 2) + 64)
                if h == 0:
                    pe.wait_ge(kT_out, b + 1)
                    pe.wait_ge(qT_act, b * (QG // 2) + QG // 2)
                    pe.wait_ge(qT_dve, b * (QG // 2) + QG // 2)
                if h >= 2:
                    pe.wait_ge(masked, b * (2 * H0) + 2 * (h - 1))
                pe.matmul(ps[h % 2][:, 0:P], qT[rows, h // 2, 0:P], kT[rows, 0:P], start=True, stop=True)
                pe.matmul(ps[h % 2][:, P:SW], qT[rows, h // 2, P:TB], kT[rows, :], start=True, stop=True).then_inc(s_done, 1)
            if 0 <= step - LAG_T < H0:
                h = step - LAG_T
                pe.wait_ge(exp_done, b * (2 * H0) + 2 * h + 2)
                if not (first and h < 2):
                    pe.wait_ge(pT_lo, b * H0 + h - 1)
                for n in range(3):
                    last = pe.transpose(ps[2 + h % 2][:, n * P:(n + 1) * P], prob[:, h % 4, n * P:(n + 1) * P], ident[:, :])
                last.then_inc(pT_done, 1)
            if 0 <= step - LAG_V < H0:
                h = step - LAG_V
                pe.wait_ge(pT_lo, b * H0 + h + 1)
                if h == 0:
                    pe.wait_ge(v_split, b * 5 + 5)
                    if with_tail:
                        pe.wait_ge(o_out, b * BT)
                cols = slice(h * HD0, (h + 1) * HD0)
                for qb, kb, c in ((0, 0, 0), (1, 0, P), (1, 1, 2 * P)):
                    for part in range(2):
                        for n in range(3):
                            last = pe.matmul(ps[4 + qb][:, cols], probT[part][:, h % 4, c:c + P], v_parts[:, n, kb, :],
                                             start=(kb == 0 and part == 0 and n == 0), stop=(kb == qb and part == 1 and n == 2))
                last.then_inc(pv_done, 1)
            if not with_tail and step == 6:
                pe.wait_ge(bf_scaled, ER)
                pe.wait_ge(q_lo, 2)
                for k in range(KD):
                    if k >= 2:
                        pe.wait_ge(w_eff_done, k - 1)
                    for r in range(ER):
                        last = pe.matmul(ps[7 - k % 2][:, :], a_raw[:, r, k * P:(k + 1) * P], bf_raw[:, r, :],
                                         start=(r == 0), stop=(r == ER - 1))
                    last.then_inc(adapters_done, 1)
            if with_tail:
                pe_tail(pe, b - 1, step)
        for t in range(BT):
            pe.wait_ge(o_out, b * BT + t + 1)
            if with_tail:
                pe.wait_ge(biased, b * BT)
            else:
                pe.wait_ge(w_eff_done, KD)
            transpose_tok(pe, t, oT_done)

    def pe_tail(pe, b, step):
        if step in (AT["wo"], None):
            pe.wait_ge(wo_lo, 1)
            pe.wait_ge(oT_lo, b * BT + BT)
            pe.wait_ge(q_lo, b * 2 + 4 if step is not None else NB * 2)
            for t in range(BT):
                for k in range(KD):
                    last = split_product(pe, ps[6 + t][:, :], (fT[0][:, k, t * P:(t + 1) * P], fT[1][:, k, t * P:(t + 1) * P]),
                                         (wo[0][:, k, :], wo[1][:, k, :]), k == 0, k == KD - 1)
                last.then_inc(wo_done, 1)
        if step in (AT["x1T"], None):
            for t in range(BT):
                pe.wait_ge(ln3.normed, b * BT + t + 1)
                transpose_tok(pe, t, x1T_done)
        if step in (AT["ffn"], None):
            pe.wait_ge(wf_lo, 1)
            pe.wait_ge(x1T_lo, b * BT + BT)
            for t in range(BT):
                for k in range(KD):
                    last = split_product(pe, ps[6 + t][:, :], (fT[0][:, k, t * P:(t + 1) * P], fT[1][:, k, t * P:(t + 1) * P]),
                                         (wf[0][:, k, :], wf[1][:, k, :]), k == 0, k == KD - 1)
                last.then_inc(ffn_done, 1)

    ctx.close()
    return {"sync": sync, "sync_consts": sync_consts, "pool": pool, "scalar": scalar, "vector": vector,
            "tensor": tensor, "done": x2_done, "done_count": NT}


class WideNorm:

    def __init__(self, sb, sem):
        self.six = sb("wide_six", [P, NT, 6], F32)
        self.mv = sb("wide_mv", [P, NT, 2], F32)
        self.var_eps = sb("wide_var_eps", [P, NT], F32)
        self.rstd = sb("wide_rstd", [P, NT], F32)
        self.stats_done = sem("wide_stats_done")
        self.moments_done = sem("wide_moments_done")
        self.var_ready = sem("wide_var_ready")
        self.rstd_ready = sem("wide_rstd_ready")
        self.normed = sem("wide_normed")

    def moments(self, dve, use, source):
        if use:
            dve.wait_ge(self.normed, use * NT)
        for t in range(NT):
            dve.bn_stats(self.six[:, t, :], source(t)).then_inc(self.stats_done, 1)
            if t:
                dve.wait_ge(self.stats_done, use * NT + t)
                dve.bn_aggr(self.mv[:, t - 1, :], self.six[:, t - 1, :]).then_inc(self.moments_done, 1)
        dve.wait_ge(self.stats_done, use * NT + NT)
        dve.bn_aggr(self.mv[:, NT - 1, :], self.six[:, NT - 1, :]).then_inc(self.moments_done, 1)
        dve.wait_ge(self.moments_done, use * NT + NT)
        dve.tensor_scalar(self.var_eps[:, :], self.mv[:, :, 1], EPS, None, ALU.add).then_inc(self.var_ready, 1)

    def inverse(self, pool, use, minus_half):
        pool.wait_ge(self.var_ready, use + 1)
        pool.tensor_tensor(self.rstd[:, :], self.var_eps[:, :], minus_half, ALU.pow).then_inc(self.rstd_ready, 1)

    def apply(self, dve, use, t, source, target):
        if t == 0:
            dve.wait_ge(self.rstd_ready, use + 1)
        dve.tensor_scalar(target, source, self.mv[:, t, 0:1], self.rstd[:, t:t + 1],
                          ALU.subtract, ALU.mult).then_inc(self.normed, 1)


def past(count, n):
    return not isinstance(count, int) or count >= n


class Transposer:

    RING = 4

    def __init__(self, sb, sem, norm, X, XT, ps, ident):
        self.norm, self.X, self.XT, self.ps, self.ident = norm, X, XT, ps, ident
        self.tok = sb("turn_tok", [P, self.RING, D], F32)
        self.turned = sem("turned")
        self.hi_out = sem("turn_hi_out")
        self.lo_out = sem("turn_lo_out")

    def vector(self, dve, time, use):
        X, XT = self.X, self.XT
        self.norm.moments(dve, use, lambda t: X[:, t, :])
        for t in range(NT + self.RING):
            if t >= self.RING:
                n = t - self.RING
                dve.wait_ge(self.hi_out, time * NT + n + 1)
                dve.tensor_tensor(XT[1][:, :, n * P:(n + 1) * P], self.ps[n][:, :].rearrange("p (k n) -> p k n", k=KD),
                                  XT[0][:, :, n * P:(n + 1) * P].bitcast(F32), ALU.subtract).then_inc(self.lo_out, 1)
            if t < NT:
                self.norm.apply(dve, use, t, X[:, t, :], self.tok[:, t % self.RING, :])

    def scalar(self, act, time):
        for t in range(NT):
            act.wait_ge(self.turned, time * NT + t + 1)
            act.activation(self.XT[0][:, :, t * P:(t + 1) * P], self.ps[t][:, :].rearrange("p (k n) -> p k n", k=KD),
                           ACT.Copy).then_inc(self.hi_out, 1)

    def tensor(self, pe, time, use):
        for t in range(NT):
            pe.wait_ge(self.norm.normed, use * NT + t + 1)
            for k in range(KD):
                last = pe.transpose(self.ps[t][:, k * P:(k + 1) * P], self.tok[:, t % self.RING, k * P:(k + 1) * P],
                                    self.ident[:, :])
            last.then_inc(self.turned, 1)


def layer1_attention(nc, dram, XT, acc, ps, consts, acc_zero, xt_ready, room):
    ident = consts["ident"]
    ctx = ExitStack()
    sb = lambda name, shape, dt: ctx.enter_context(nc.sbuf_tensor(name, shape, dt))
    sem = lambda name: nc.semaphore(name).__enter__()
    pair = lambda name, shape: [sb(f"{name}_{x}", shape, F32R) for x in ("hi", "lo")]

    cos, sin = sb("cos1", [P, TB], F32), sb("sin1", [P, TB], F32)
    causal = sb("causal1", [P, 2 * P], F32)
    w_raw = sb("w_raw1", [P, KD, GW], F32)
    wo_raw = sb("wo_raw1", [P, HG, D], F32)
    w = pair("w1", [P, KD, GW])
    wo = pair("wo1", [P, HG, D])
    prob = sb("prob1", [P, HG, SW], F32)
    neg_max = sb("neg_max1", [P, HG, 2], F32)
    row_sum = sb("row_sum1", [P, HG, 2], F32)
    row_inv = sb("row_inv1", [P, HG, 2], F32)
    pT = pair("pT1", [P, HG, SW])
    oT = pair("oT1", [P, HG, TB])
    k_sum, k_rot = sb("k_sum1", [P, TB], F32), sb("k_rot1", [P, TB], F32)
    q_sum, q_rot = sb("q_sum1", [P, 2, TB], F32), sb("q_rot1", [P, 2, TB], F32)
    vT = sb("vT1", [P, TB], F32)
    q = [pair(f"q1_{n}", [P, HG, TB]) for n in range(2)]
    k = [pair(f"k1_{n}", [P, TB]) for n in range(2)]
    v = [pair(f"v1_{n}", [P, BT, HD1]) for n in range(2)]

    tables_in, w_in, wo_in = sem("tables_in"), sem("w_in1"), sem("wo_in1")
    kvw_hi, qw_hi, kvw_lo, qw_lo, wo_hi, wo_lo = (sem(n) for n in ("kvw_hi", "qw_hi", "kvw_lo", "qw_lo", "wo_hi1", "wo_lo1"))
    s_done, masked, exp_done, inv_done, normed = (sem(n) for n in ("s_done1", "masked1", "exp_done1", "inv_done1", "normed1"))
    pT_done, pT_hi, pT_lo = (sem(n) for n in ("pT_done1", "pT_hi1", "pT_lo1"))
    kv_done, vT_out, v_turned, v_hi, v_lo = (sem(n) for n in ("kv_done1", "vT_out1", "v_turned1", "v_hi1", "v_lo1"))
    k_halves, k_sin, k_cos, k_added, k_hi, k_lo = (sem(n) for n in ("k_halves", "k_sin", "k_cos", "k_added", "k_hi1", "k_lo1"))
    q_done, q_halves, q_sin, q_cos, q_added, q_hi, q_lo = (sem(n) for n in ("q_done1", "q_halves", "q_sin", "q_cos", "q_added", "q_hi1", "q_lo1"))
    pv_done, o_hi, o_lo, wo_done, added = (sem(n) for n in ("pv_done1", "o_hi1", "o_lo1", "wo_done1", "added1"))

    BS, BP, BO, BM = (0, 1), (2, 3), 4, (5, 6, 7)
    KC, VC, QC = 0, HD1, 2 * HD1
    half = HD1 // 2

    def heads(bank):
        return ps[bank][:, :].rearrange("p (h n) -> p h n", h=2)

    def over_pair(table):
        return table[:, :].rearrange("p (a n) -> p a n", a=1).to_broadcast([P, 2, TB])

    def over_groups(engine, step):
        for b in range(NB):
            step(0, b, b > 0, True)
        with engine.Fori(1, NG - 1) as g:
            for b in range(NB):
                step(g, b, True, True)
        for b in range(NB):
            step(NG - 1, b, True, b < NB - 1)

    def sync(sp):
        sp.wait_ge(*room)
        sp.dma_start(cos[:, :], dram["cos"]).then_inc(tables_in, 16)
        sp.dma_start(sin[:, :], dram["sin"]).then_inc(tables_in, 16)
        sp.dma_start(causal[:, :], dram["causal"]).then_inc(tables_in, 16)
        sp.dma_start(w_raw[:, :, :], dram["w1"][0]).then_inc(w_in, 16)
        sp.dma_start(wo_raw[:, :, :], dram["wo1"][0]).then_inc(wo_in, 16)
        with sp.Fori(1, NG) as g:
            sp.wait_ge(kvw_lo, g)
            sp.wait_ge(qw_lo, g)
            sp.dma_start(w_raw[:, :, :], dram["w1"][g]).then_inc(w_in, 16)
            sp.wait_ge(wo_lo, g)
            sp.dma_start(wo_raw[:, :, :], dram["wo1"][g]).then_inc(wo_in, 16)

    def project_kv(pe, u, b):
        if past(u, 1):
            pe.wait_ge(v_lo, u)
        xs = slice(b * TB, (b + 1) * TB)
        for c0, o in ((KC, 0), (VC, TB)):
            for n in range(KD):
                last = split_product(pe, ps[BM[0]][:, o:o + TB], (w[0][:, n, c0:c0 + HD1], w[1][:, n, c0:c0 + HD1]),
                                     (XT[0][:, n, xs], XT[1][:, n, xs]), n == 0, n == KD - 1)
        last.then_inc(kv_done, 1)

    def project_q(pe, u, b, p):
        if past(u, 3):
            pe.wait_ge(added, (u - 3) * 2 + p + 1)
        elif u:
            pe.wait_ge(q_cos, (u - 1) * 2 + p + 1)
        xs = slice(b * TB, (b + 1) * TB)
        for h in (2 * p, 2 * p + 1):
            c0 = QC + h * HD1
            for n in range(KD):
                last = split_product(pe, ps[BM[1 + p]][:, (h % 2) * TB:(h % 2 + 1) * TB],
                                     (w[0][:, n, c0:c0 + HD1], w[1][:, n, c0:c0 + HD1]),
                                     (XT[0][:, n, xs], XT[1][:, n, xs]), n == 0, n == KD - 1)
        last.then_inc(q_done, 1)

    def turn_v(pe, u, b):
        pe.wait_ge(vT_out, u + 1)
        pe.wait_ge(k_cos, u + 1)
        for t in range(BT):
            last = pe.transpose(ps[BM[0]][:, t * P:(t + 1) * P], vT[:, t * P:(t + 1) * P], ident[:, :])
        last.then_inc(v_turned, 1)

    def scores(pe, u, b, h):
        n = b % 2
        if h == 0:
            pe.wait_ge(k_lo, u + 1)
        if h % 2 == 0:
            pe.wait_ge(q_lo, u * 2 + h // 2 + 1)
        if (h >= 2 or past(u, 1)):
            pe.wait_ge(masked, u * 8 + 2 * (h - 1))
        for qs, ks, cols in ((slice(0, P), slice(0, P), slice(0, P)), (slice(P, TB), slice(0, TB), slice(P, SW))):
            last = split_product(pe, ps[BS[h % 2]][:, cols], (q[n][0][:, h, qs], q[n][1][:, h, qs]),
                                 (k[n][0][:, ks], k[n][1][:, ks]), True, True)
        last.then_inc(s_done, 1)

    def turn_prob(pe, u, b, h):
        pe.wait_ge(normed, u * 8 + 2 * h + 2)
        if (h >= 2 or past(u, 1)):
            pe.wait_ge(pT_lo, u * HG + h - 1)
        for n in range(3):
            last = pe.transpose(ps[BP[h % 2]][:, n * P:(n + 1) * P], prob[:, h, n * P:(n + 1) * P], ident[:, :])
        last.then_inc(pT_done, 1)

    def prob_v(pe, u, b, p):
        n = b % 2
        pe.wait_ge(pT_lo, u * HG + 2 * p + 2)
        if p == 0:
            pe.wait_ge(v_lo, u + 1)
        if (p or past(u, 1)):
            pe.wait_ge(o_lo, u * 2 + p)
        hs = slice(2 * p, 2 * p + 2)
        for kb, cols, qs in ((0, slice(0, 2 * P), slice(0, TB)), (1, slice(2 * P, SW), slice(P, TB))):
            last = split_product(pe, heads(BO)[:, :, qs], (v[n][0][:, kb, :], v[n][1][:, kb, :]),
                                 (pT[0][:, hs, cols], pT[1][:, hs, cols]), kb == 0, kb == 1)
        last.then_inc(pv_done, 1)

    def project_out(pe, u, b, t):
        if t == 0:
            pe.wait_ge(o_lo, u * 2 + 2)
        for h in range(HG):
            last = split_product(pe, ps[BM[1 + t]][:, :], (oT[0][:, h, t * P:(t + 1) * P], oT[1][:, h, t * P:(t + 1) * P]),
                                 (wo[0][:, h, :], wo[1][:, h, :]), h == 0, h == HG - 1)
        last.then_inc(wo_done, 1)

    U = NG * NB

    def tensor(pe):
        pe.wait_ge(*xt_ready)
        pe.wait_ge(kvw_lo, 1)
        project_kv(pe, 0, 0)
        pe.wait_ge(qw_lo, 1)
        project_q(pe, 0, 0, 0)
        project_q(pe, 0, 0, 1)
        turn_v(pe, 0, 0)

        def step(g, b, before, after):
            u, nb, pb = g * NB + b, (b + 1) % NB, (b - 1) % NB
            scores(pe, u, b, 0)
            scores(pe, u, b, 1)
            if before:
                prob_v(pe, u - 1, pb, 1)
            if after:
                if nb == 0:
                    pe.wait_ge(kvw_lo, g + 2)
                project_kv(pe, u + 1, nb)
            scores(pe, u, b, 2)
            scores(pe, u, b, 3)
            if after:
                if nb == 0:
                    pe.wait_ge(qw_lo, g + 2)
                project_q(pe, u + 1, nb, 0)
                project_q(pe, u + 1, nb, 1)
            turn_prob(pe, u, b, 0)
            turn_prob(pe, u, b, 1)
            if after:
                turn_v(pe, u + 1, nb)
            if before:
                wait_q_left(pe, u, after)
                if pb == 0:
                    pe.wait_ge(wo_lo, g + 1)
                project_out(pe, u - 1, pb, 0)
            turn_prob(pe, u, b, 2)
            turn_prob(pe, u, b, 3)
            if before:
                project_out(pe, u - 1, pb, 1)
            prob_v(pe, u, b, 0)

        over_groups(pe, step)
        prob_v(pe, U - 1, NB - 1, 1)
        pe.wait_ge(added, U * 2 - 2)
        project_out(pe, U - 1, NB - 1, 0)
        project_out(pe, U - 1, NB - 1, 1)

    def wait_q_left(pe, u, after):
        pe.wait_ge(q_cos, u * 2 + 4 if after else u * 2 + 2)

    def act_weights(act, g):
        act.wait_ge(w_in, g * 16 + 16)
        if past(g, 1):
            act.wait_ge(q_done, g * (2 * NB))
        act.activation(w[0][:, :, 0:QC], w_raw[:, :, 0:QC], ACT.Copy).then_inc(kvw_hi, 1)
        act.activation(w[0][:, :, QC:GW], w_raw[:, :, QC:GW], ACT.Copy).then_inc(qw_hi, 1)

    def act_wo(act, g):
        act.wait_ge(wo_in, g * 16 + 16)
        if past(g, 1):
            act.wait_ge(wo_done, g * (2 * NB))
        act.activation(wo[0][:, :, :], wo_raw[:, :, :], ACT.Copy).then_inc(wo_hi, 1)

    def swap_halves(act, target, source, done):
        act.activation(target[0:half], source[half:HD1], ACT.Copy).then_inc(done, 1)
        act.activation(target[half:HD1], source[0:half], ACT.Copy).then_inc(done, 1)

    def act_kv(act, u, b):
        act.wait_ge(kv_done, u + 1)
        if past(u, 1):
            act.wait_ge(k_added, u)
            act.wait_ge(v_turned, u)
        act.activation(vT[:, :], ps[BM[0]][:, TB:2 * TB], ACT.Copy).then_inc(vT_out, 1)
        swap_halves(act, k_rot, ps[BM[0]][:, 0:TB], k_halves)

    def act_k_hi(act, u, b):
        act.wait_ge(k_added, u + 1)
        act.activation(k[b % 2][0][:, :], k_sum[:, :], ACT.Copy).then_inc(k_hi, 1)

    def act_q(act, u, b, p):
        act.wait_ge(q_done, u * 2 + p + 1)
        if (p or past(u, 1)):
            act.wait_ge(q_added, u * 2 + p)
        swap_halves(act, q_rot, heads(BM[1 + p]), q_halves)

    def act_q_hi(act, u, b, p):
        act.wait_ge(q_added, u * 2 + p + 1)
        act.activation(q[b % 2][0][:, 2 * p:2 * p + 2, :], q_sum[:, :, :], ACT.Copy).then_inc(q_hi, 1)

    def act_v_hi(act, u, b):
        act.wait_ge(v_turned, u + 1)
        act.activation(v[b % 2][0][:, :, :], ps[BM[0]][:, 0:TB].rearrange("p (t n) -> p t n", t=BT), ACT.Copy).then_inc(v_hi, 1)

    def act_exp(act, u, b, h):
        act.wait_ge(masked, u * 8 + 2 * h + 2)
        if past(u, 1):
            act.wait_ge(inv_done, u * 2)
        for qb, (c0, c1) in enumerate(((0, P), (P, SW))):
            act.activation(prob[:, h, c0:c1], prob[:, h, c0:c1], ACT.Exp, bias=neg_max[:, h, qb:qb + 1], scale=-1.0,
                           accum_out=row_sum[:, h, qb:qb + 1]).then_inc(exp_done, 1)

    def act_pT(act, u, b, h):
        act.wait_ge(pT_done, u * HG + h + 1)
        act.activation(pT[0][:, h, :], ps[BP[h % 2]][:, 0:SW], ACT.Copy).then_inc(pT_hi, 1)

    def act_o(act, u, b, p):
        act.wait_ge(pv_done, u * 2 + p + 1)
        act.activation(oT[0][:, 2 * p:2 * p + 2, :], heads(BO), ACT.Copy).then_inc(o_hi, 1)

    def scalar(act):
        act_weights(act, 0)
        act_kv(act, 0, 0)
        act_k_hi(act, 0, 0)
        act_q(act, 0, 0, 0)
        act_q_hi(act, 0, 0, 0)
        act_q(act, 0, 0, 1)
        act_q_hi(act, 0, 0, 1)
        act_v_hi(act, 0, 0)
        act_wo(act, 0)

        def step(g, b, before, after):
            u, nb, pb = g * NB + b, (b + 1) % NB, (b - 1) % NB
            act_exp(act, u, b, 0)
            act_exp(act, u, b, 1)
            if before:
                act_o(act, u - 1, pb, 1)
            if b == 1 and past(g, 1):
                act_wo(act, g)
            if after:
                act_kv(act, u + 1, nb)
            act_exp(act, u, b, 2)
            act_exp(act, u, b, 3)
            if after:
                act_k_hi(act, u + 1, nb)
                act_q(act, u + 1, nb, 0)
                act_q_hi(act, u + 1, nb, 0)
                act_q(act, u + 1, nb, 1)
            act_pT(act, u, b, 0)
            act_pT(act, u, b, 1)
            if after:
                act_q_hi(act, u + 1, nb, 1)
                act_v_hi(act, u + 1, nb)
            if b == 2 and not (isinstance(g, int) and g == NG - 1):
                act_weights(act, g + 1)
            act_pT(act, u, b, 2)
            act_pT(act, u, b, 3)
            act_o(act, u, b, 0)

        over_groups(act, step)
        act_o(act, U - 1, NB - 1, 1)

    def dve_kvw(dve, g):
        dve.wait_ge(kvw_hi, g + 1)
        dve.tensor_tensor(w[1][:, :, 0:QC], w_raw[:, :, 0:QC], w[0][:, :, 0:QC].bitcast(F32), ALU.subtract).then_inc(kvw_lo, 1)

    def dve_k_cos(dve, u, b):
        dve.wait_ge(k_halves, u * 2 + 2)
        if past(u, 1):
            dve.wait_ge(k_lo, u)
        dve.tensor_tensor(k_sum[:, :], ps[BM[0]][:, 0:TB], cos[:, :], ALU.mult).then_inc(k_cos, 1)

    def dve_k_add(dve, u, b):
        dve.wait_ge(k_sin, u + 1)
        dve.wait_ge(k_cos, u + 1)
        dve.tensor_tensor(k_sum[:, :], k_sum[:, :], k_rot[:, :], ALU.add).then_inc(k_added, 1)

    def dve_k_lo(dve, u, b):
        dve.wait_ge(k_hi, u + 1)
        dve.tensor_tensor(k[b % 2][1][:, :], k_sum[:, :], k[b % 2][0][:, :].bitcast(F32), ALU.subtract).then_inc(k_lo, 1)

    def dve_q_cos(dve, u, b, p):
        dve.wait_ge(q_halves, u * 4 + 2 * p + 2)
        if (p or past(u, 1)):
            dve.wait_ge(q_lo, u * 2 + p)
        dve.tensor_tensor(q_sum[:, :, :], heads(BM[1 + p]), over_pair(cos), ALU.mult).then_inc(q_cos, 1)

    def dve_q_add(dve, u, b, p):
        dve.wait_ge(q_sin, u * 2 + p + 1)
        dve.wait_ge(q_cos, u * 2 + p + 1)
        dve.tensor_tensor(q_sum[:, :, :], q_sum[:, :, :], q_rot[:, :, :], ALU.add).then_inc(q_added, 1)

    def dve_q_lo(dve, u, b, p):
        dve.wait_ge(q_hi, u * 2 + p + 1)
        dve.tensor_tensor(q[b % 2][1][:, 2 * p:2 * p + 2, :], q_sum[:, :, :],
                          q[b % 2][0][:, 2 * p:2 * p + 2, :].bitcast(F32), ALU.subtract).then_inc(q_lo, 1)

    def dve_v_lo(dve, u, b):
        dve.wait_ge(v_hi, u + 1)
        dve.tensor_tensor(v[b % 2][1][:, :, :], ps[BM[0]][:, 0:TB].rearrange("p (t n) -> p t n", t=BT),
                          v[b % 2][0][:, :, :].bitcast(F32), ALU.subtract).then_inc(v_lo, 1)

    def dve_mask(dve, u, b, h):
        dve.wait_ge(s_done, u * HG + h + 1)
        if past(u, 1):
            dve.wait_ge(pT_done, (u - 1) * HG + h + 1)
        stand_apart(dve)
        for qb, (c0, c1) in enumerate(((0, P), (P, SW))):
            dve.tensor_tensor_reduce(prob[:, h, c0:c1], ps[BS[h % 2]][:, c0:c1], causal[:, 2 * P - (c1 - c0):2 * P],
                                     -SC1, 3e38, ALU.add, ALU.min, neg_max[:, h, qb:qb + 1]).then_inc(masked, 1)

    def dve_inverse(dve, u, b, p):
        dve.wait_ge(exp_done, u * 8 + 4 * p + 4)
        if past(u, 1):
            dve.wait_ge(normed, (u - 1) * 8 + 4 * p + 4)
        stand_apart(dve)
        dve.reciprocal(row_inv[:, 2 * p:2 * p + 2, :], row_sum[:, 2 * p:2 * p + 2, :]).then_inc(inv_done, 1)

    def dve_pT(dve, u, b, h):
        dve.wait_ge(pT_hi, u * HG + h + 1)
        dve.tensor_tensor(pT[1][:, h, :], ps[BP[h % 2]][:, 0:SW], pT[0][:, h, :].bitcast(F32), ALU.subtract).then_inc(pT_lo, 1)

    def dve_o(dve, u, b, p):
        dve.wait_ge(o_hi, u * 2 + p + 1)
        dve.tensor_tensor(oT[1][:, 2 * p:2 * p + 2, :], heads(BO), oT[0][:, 2 * p:2 * p + 2, :].bitcast(F32),
                          ALU.subtract).then_inc(o_lo, 1)

    def dve_add(dve, u, b, t):
        dve.wait_ge(wo_done, u * 2 + t + 1)
        row = acc[:, b * BT + t, :]
        dve.tensor_tensor(row, row, ps[BM[1 + t]][:, :], ALU.add).then_inc(added, 1)

    def vector(dve):
        dve.wait_ge(tables_in, 48)
        dve.wait_ge(acc_zero, 1)
        dve_kvw(dve, 0)
        dve_k_cos(dve, 0, 0)
        dve_k_add(dve, 0, 0)
        dve_k_lo(dve, 0, 0)
        for p in range(2):
            dve_q_cos(dve, 0, 0, p)
            dve_q_add(dve, 0, 0, p)
            dve_q_lo(dve, 0, 0, p)
        dve_v_lo(dve, 0, 0)

        def step(g, b, before, after):
            u, nb, pb = g * NB + b, (b + 1) % NB, (b - 1) % NB
            dve_mask(dve, u, b, 0)
            dve_mask(dve, u, b, 1)
            if before:
                dve_o(dve, u - 1, pb, 1)
            if after:
                dve_k_cos(dve, u + 1, nb)
            dve_inverse(dve, u, b, 0)
            dve_mask(dve, u, b, 2)
            dve_mask(dve, u, b, 3)
            if after:
                dve_k_add(dve, u + 1, nb)
                dve_k_lo(dve, u + 1, nb)
            dve_inverse(dve, u, b, 1)
            if after:
                for p in range(2):
                    dve_q_cos(dve, u + 1, nb, p)
                    dve_q_add(dve, u + 1, nb, p)
                    if p == 0:
                        dve_q_lo(dve, u + 1, nb, p)
            dve_pT(dve, u, b, 0)
            dve_pT(dve, u, b, 1)
            if after:
                dve_q_lo(dve, u + 1, nb, 1)
                dve_v_lo(dve, u + 1, nb)
            if b == 2 and not (isinstance(g, int) and g == NG - 1):
                dve_kvw(dve, g + 1)
            if before:
                dve_add(dve, u - 1, pb, 0)
            dve_pT(dve, u, b, 2)
            dve_pT(dve, u, b, 3)
            if before:
                dve_add(dve, u - 1, pb, 1)
            dve_o(dve, u, b, 0)

        over_groups(dve, step)
        dve_o(dve, U - 1, NB - 1, 1)
        dve_add(dve, U - 1, NB - 1, 0)
        dve_add(dve, U - 1, NB - 1, 1)

    def pool_qw(pl, g):
        pl.wait_ge(qw_hi, g + 1)
        pl.tensor_tensor(w[1][:, :, QC:GW], w_raw[:, :, QC:GW], w[0][:, :, QC:GW].bitcast(F32), ALU.subtract).then_inc(qw_lo, 1)

    def pool_wo(pl, g):
        pl.wait_ge(wo_hi, g + 1)
        pl.tensor_tensor(wo[1][:, :, :], wo_raw[:, :, :], wo[0][:, :, :].bitcast(F32), ALU.subtract).then_inc(wo_lo, 1)

    def pool_k(pl, u, b):
        pl.wait_ge(k_halves, u * 2 + 2)
        pl.tensor_tensor(k_rot[:, :], k_rot[:, :], sin[:, :], ALU.mult).then_inc(k_sin, 1)

    def pool_q(pl, u, b, p):
        pl.wait_ge(q_halves, u * 4 + 2 * p + 2)
        pl.tensor_tensor(q_rot[:, :, :], q_rot[:, :, :], over_pair(sin), ALU.mult).then_inc(q_sin, 1)

    def pool_norm(pl, u, b, p):
        pl.wait_ge(inv_done, u * 2 + p + 1)
        stand_apart(pl)
        for h in (2 * p, 2 * p + 1):
            for qb, (c0, c1) in enumerate(((0, P), (P, SW))):
                pl.tensor_scalar(prob[:, h, c0:c1], prob[:, h, c0:c1], row_inv[:, h, qb:qb + 1], 1.0, ALU.mult, ALU.mult)\
                  .then_inc(normed, 1)

    def pool(pl):
        pl.wait_ge(tables_in, 48)
        pool_qw(pl, 0)
        pool_k(pl, 0, 0)
        pool_q(pl, 0, 0, 0)
        pool_q(pl, 0, 0, 1)
        pool_wo(pl, 0)

        def step(g, b, before, after):
            u, nb, pb = g * NB + b, (b + 1) % NB, (b - 1) % NB
            if b == 1 and past(g, 1):
                pool_wo(pl, g)
            if after:
                pool_k(pl, u + 1, nb)
            pool_norm(pl, u, b, 0)
            if after:
                pool_q(pl, u + 1, nb, 0)
            pool_norm(pl, u, b, 1)
            if after:
                pool_q(pl, u + 1, nb, 1)
            if b == 2 and not (isinstance(g, int) and g == NG - 1):
                pool_qw(pl, g + 1)

        over_groups(pl, step)

    ctx.close()
    return {"sync": sync, "pool": pool, "scalar": scalar, "vector": vector, "tensor": tensor,
            "done": added, "done_count": U * 2}


def finish_sublayer(dve, norm, use, summed, X, acc):
    norm.moments(dve, use, lambda t: acc[:, t, :])
    for t in range(NT + 1):
        if t < NT:
            norm.apply(dve, use, t, acc[:, t, :], acc[:, t, :])
        if t:
            dve.wait_ge(norm.normed, use * NT + t)
            dve.tensor_tensor(X[:, t - 1, :], X[:, t - 1, :], acc[:, t - 1, :], ALU.add).then_inc(summed, 1)


def swiglu(nc, dram, XT, acc, ps, acc_zero, xt_ready, room):
    ctx = ExitStack()
    sb = lambda name, shape, dt: ctx.enter_context(nc.sbuf_tensor(name, shape, dt))
    sem = lambda name: nc.semaphore(name).__enter__()
    GU, W = KD * 2 * P, KD * 2 * P + D
    C = 2
    TC = NT // C * P

    raw = [sb(f"ffn_raw{n}", [P, W], F32) for n in range(2)]
    w = [[sb(f"ffn_w{n}_{x}", [P, W], F32R) for x in ("hi", "lo")] for n in range(2)]
    act_gate = sb("act_gate", [P, C, TC], F32)
    h32 = sb("h32", [P, C, TC], F32)
    h = [[sb(f"h{n}_{x}", [P, C, TC], F32R) for x in ("hi", "lo")] for n in range(2)]

    raw_in = [sem(f"ffn_raw_in{n}") for n in range(2)]
    gu_hi, gu_lo, dw_hi, dw_lo = (sem(n) for n in ("gu_hi", "gu_lo", "dw_hi", "dw_lo"))
    gate_done, up_done, gate_out, h_done, h_hi, h_lo = (sem("ffn_" + n) for n in ("gate_done", "up_done", "gate_out", "h_done", "h_hi", "h_lo"))
    down_done, down_added = sem("down_done"), sem("down_added")

    def over_tiles(engine, step):
        for f in range(3):
            step(f, f % 2)
        with engine.Fori(1, (FT - 1) // 2) as i:
            step(2 * i + 1, 1)
            step(2 * i + 2, 0)

    def sync(sp):
        sp.wait_ge(*room)
        for f in range(2):
            sp.dma_start(raw[f][:, :], dram["ffn_w"][f]).then_inc(raw_in[f], 16)
        with sp.Fori(1, (FT - 1) // 2) as i:
            for n in range(2):
                sp.wait_ge(dw_lo, 2 * i + n - 1)
                sp.dma_start(raw[n][:, :], dram["ffn_w"][2 * i + n]).then_inc(raw_in[n], 16)
        sp.wait_ge(dw_lo, FT - 2)
        sp.dma_start(raw[(FT - 1) % 2][:, :], dram["ffn_w"][FT - 1]).then_inc(raw_in[(FT - 1) % 2], 16)

    def tensor(pe):
        def step(f, n):
            pe.wait_ge(gu_lo, f + 1)
            for c in range(C):
                for up, done in ((0, gate_done), (1, up_done)):
                    if past(f, 1):
                        pe.wait_ge(h_done, (f - 1) * C + c + 1)
                    for k in range(KD):
                        cols = slice(k * 2 * P + up * P, k * 2 * P + up * P + P)
                        xs = slice(c * TC, (c + 1) * TC)
                        last = split_product(pe, ps[2 * c + up][:, :], (w[n][0][:, cols], w[n][1][:, cols]),
                                             (XT[0][:, k, xs], XT[1][:, k, xs]), k == 0, k == KD - 1)
                    last.then_inc(done, 1)
            if past(f, 1):
                down(f - 1, 1 - n)

        def down(f, n):
            pe.wait_ge(dw_lo, f + 1)
            for t in range(NT):
                c, ts = t // (NT // C), slice(t % (NT // C) * P, (t % (NT // C) + 1) * P)
                if t % (NT // C) == 0:
                    pe.wait_ge(h_lo, f * C + c + 1)
                if t >= 4 or past(f, 1):
                    pe.wait_ge(down_added, f * NT + t - 3)
                last = split_product(pe, ps[4 + t % 4][:, :], (h[n][0][:, c, ts], h[n][1][:, c, ts]),
                                     (w[n][0][:, GU:W], w[n][1][:, GU:W]), True, True)
                last.then_inc(down_done, 1)

        pe.wait_ge(*xt_ready)
        over_tiles(pe, step)
        down(FT - 1, (FT - 1) % 2)

    def scalar(act):
        def step(f, n):
            for c in range(C):
                act.wait_ge(gate_done, f * C + c + 1)
                if past(f, 1):
                    act.wait_ge(h_done, (f - 1) * C + c + 1)
                act.activation(act_gate[:, c, :], ps[2 * c][:, :], ACT.Silu).then_inc(gate_out, 1)
            for c in range(C):
                act.wait_ge(h_done, f * C + c + 1)
                act.activation(h[n][0][:, c, :], h32[:, c, :], ACT.Copy).then_inc(h_hi, 1)

        over_tiles(act, step)

    def vector(dve):
        def step(f, n):
            for c in range(C):
                dve.wait_ge(gate_out, f * C + c + 1)
                dve.wait_ge(up_done, f * C + c + 1)
                if past(f, 1):
                    dve.wait_ge(h_lo, (f - 1) * C + c + 1)
                dve.tensor_tensor(h32[:, c, :], ps[2 * c + 1][:, :], act_gate[:, c, :], ALU.mult).then_inc(h_done, 1)
            if past(f, 1):
                add(f - 1)

        def add(f):
            for t in range(NT):
                dve.wait_ge(down_done, f * NT + t + 1)
                if past(f, 1):
                    dve.wait_ge(down_added, (f - 1) * NT + t + 1)
                dve.tensor_tensor(acc[:, t, :], acc[:, t, :], ps[4 + t % 4][:, :], ALU.add).then_inc(down_added, 1)

        dve.wait_ge(acc_zero, 2)
        over_tiles(dve, step)
        add(FT - 1)

    def split(pl, f, n, cols, hi, lo, used, count):
        if past(f, 2):
            pl.wait_ge(used, (f - 1) * count)
        stand_apart(pl)
        pl.tensor_scalar(w[n][0][:, cols], raw[n][:, cols], 1.0, 1.0, ALU.mult, ALU.mult).then_inc(hi, 1)
        pl.wait_ge(hi, f + 1)
        pl.tensor_tensor(w[n][1][:, cols], raw[n][:, cols], w[n][0][:, cols].bitcast(F32), ALU.subtract).then_inc(lo, 1)

    def split_gate_up(pl, f, n):
        pl.wait_ge(raw_in[n], (f - n) * 8 + 16)
        split(pl, f, n, slice(0, GU), gu_hi, gu_lo, up_done, C)

    def split_down(pl, f, n):
        split(pl, f, n, slice(GU, W), dw_hi, dw_lo, down_done, NT)

    def pool(pl):
        def step(f, n, ahead=True):
            for c in range(C):
                pl.wait_ge(h_hi, f * C + c + 1)
                pl.tensor_tensor(h[n][1][:, c, :], h32[:, c, :], h[n][0][:, c, :].bitcast(F32), ALU.subtract).then_inc(h_lo, 1)
            if ahead:
                split_down(pl, f + 1, 1 - n)
                split_gate_up(pl, f + 2, n)

        split_gate_up(pl, 0, 0)
        split_down(pl, 0, 0)
        split_gate_up(pl, 1, 1)
        for f in range(2):
            step(f, f)
        with pl.Fori(1, (FT - 3) // 2) as i:
            step(2 * i, 0)
            step(2 * i + 1, 1)
        step(FT - 3, (FT - 3) % 2)
        step(FT - 2, (FT - 2) % 2, False)
        split_down(pl, FT - 1, (FT - 1) % 2)
        step(FT - 1, (FT - 1) % 2, False)

    ctx.close()
    return {"sync": sync, "pool": pool, "scalar": scalar, "vector": vector, "tensor": tensor,
            "done": down_added, "done_count": FT * NT}


def host_layout(inp):
    c = np.ascontiguousarray
    wkv = np.asarray(inp["L0_attn_Wkv"])
    wk, wv = wkv[:, :HD0], wkv[:, HD0:]
    a = {
        "x": c(np.asarray(inp["L0_attn_hidden_states"]).reshape(NB * TB, D)),
        "wq0": c(inp["L0_attn_Wq"]),
        "wkv0": c(np.concatenate([np.tile(wk, (1, HPT)), wv], 1).reshape(KD, P, P + HD0).transpose(1, 0, 2)),
        "wo0": c(inp["L0_attn_Wo"]),
        "wf0": c(np.asarray(inp["L0_ffn_W"]).T),
        "bias0": c(inp["L0_ffn_bias"]),
        "a0": c(np.asarray(inp["L0_ffn_A"]).reshape(NEXP * RANK, D)),
        "bf0": c(np.asarray(inp["L0_ffn_Bf"]).transpose(0, 2, 1).reshape(NEXP * RANK, D)),
        "gate_w": c(np.stack([np.repeat(np.asarray(inp[n]), RANK).reshape(ER, P).T
                              for n in ("L0_ffn_coeffs", "L0_ffn_scales")], 1)),
    }
    columns = np.concatenate([np.asarray(inp["L1_attn_W" + n]).reshape(NG, -1, D) for n in "kvq"], 1)
    a["w1"] = c(columns.reshape(NG, GW, KD, P).transpose(0, 3, 2, 1))
    a["wo1"] = c(np.asarray(inp["L1_attn_Wo"]).T.reshape(NG, HG, P, D).transpose(0, 2, 1, 3))
    pad = ((0, FT * P - F), (0, 0))
    gate, up = (np.pad(np.asarray(inp["L1_ffn_W_" + n]), pad).reshape(FT, P, KD, P).transpose(0, 3, 2, 1)
                for n in ("gate", "up"))
    down = np.pad(np.asarray(inp["L1_ffn_W_down"]).T, pad).reshape(FT, P, D)
    a["ffn_w"] = c(np.concatenate([np.concatenate([gate, up], 3).reshape(FT, P, KD * 2 * P), down], 2))
    return a


def build(nc, dram, out):
    with ExitStack() as ctx:
        sb = lambda name, shape, dt: ctx.enter_context(nc.sbuf_tensor(name, shape, dt))
        sem = lambda name: nc.semaphore(name).__enter__()
        X = sb("X", [P, NT, D], F32)
        ident = sb("ident_sb", [P, P], F32)
        minus_half = sb("minus_half", [P, NT], F32)
        ps = [ctx.enter_context(nc.psum_tensor(f"bank{i}", [P, 512], F32)) for i in range(8)]
        ident_in, half_set, acc_zero, out_done = (sem(n) for n in ("ident_in", "half_set", "acc_zero", "out_done"))
        consts = {"ident": ident, "minus_half": minus_half, "in": ident_in}

        l0 = layer0(nc, dram, X, ps, consts)
        l0_over = (l0["done"], l0["done_count"])
        XT = [sb(f"XT_{x}", [P, KD, NB * TB], F32R) for x in ("hi", "lo")]
        acc = sb("acc", [P, NT, D], F32)
        norm = WideNorm(sb, sem)
        turn = Transposer(sb, sem, norm, X, XT, ps, ident)
        summed = sem("summed")
        attention = layer1_attention(nc, dram, XT, acc, ps, consts, acc_zero, (turn.lo_out, NT), l0_over)
        attention_over = (attention["done"], attention["done_count"])
        ffn = swiglu(nc, dram, XT, acc, ps, acc_zero, (turn.lo_out, 2 * NT), attention_over)
        ffn_over = (ffn["done"], ffn["done_count"])

        block = ctx.enter_context(nc.Block())

        @block.sync
        def _(sp):
            sp.dma_start(ident[:, :], dram["ident"]).then_inc(ident_in, 16)
            l0["sync"](sp)
            attention["sync"](sp)
            ffn["sync"](sp)
            rows = out.rearrange("(n p) d -> p n d", p=P)
            for t in range(NT):
                sp.wait_ge(summed, NT + t + 1)
                sp.dma_start(rows[:, t, :], X[:, t, :]).then_inc(out_done, 16)
            sp.wait_ge(out_done, NT * 16)

        @block.gpsimd
        def _(pl):
            pl.memset(minus_half[:, :], -0.5).then_inc(half_set, 1)
            pl.wait_ge(half_set, 1)
            l0["pool"](pl)
            pl.wait_ge(*l0_over)
            pl.memset(acc[:, :, :], 0.0).then_inc(acc_zero, 1)
            norm.inverse(pl, 0, minus_half[:, 0:NT])
            attention["pool"](pl)
            norm.inverse(pl, 1, minus_half[:, 0:NT])
            norm.inverse(pl, 2, minus_half[:, 0:NT])
            pl.memset(acc[:, :, :], 0.0).then_inc(acc_zero, 1)
            ffn["pool"](pl)
            norm.inverse(pl, 3, minus_half[:, 0:NT])

        @block.scalar
        def _(act):
            l0["scalar"](act)
            turn.scalar(act, 0)
            attention["scalar"](act)
            turn.scalar(act, 1)
            ffn["scalar"](act)

        @block.vector
        def _(dve):
            l0["vector"](dve)
            dve.wait_ge(*l0_over)
            turn.vector(dve, 0, 0)
            attention["vector"](dve)
            dve.wait_ge(*attention_over)
            finish_sublayer(dve, norm, 1, summed, X, acc)
            dve.wait_ge(summed, NT)
            turn.vector(dve, 1, 2)
            ffn["vector"](dve)
            dve.wait_ge(*ffn_over)
            finish_sublayer(dve, norm, 3, summed, X, acc)

        @block.tensor
        def _(pe):
            l0["tensor"](pe)
            turn.tensor(pe, 0, 0)
            attention["tensor"](pe)
            turn.tensor(pe, 1, 2)
            ffn["tensor"](pe)


def kernel(**inputs):
    import concourse.bacc as bacc
    from concourse.bass_utils import run_bass_kernel_spmd

    nc = bacc.Bacc("TRN2", target_bir_lowering=False, num_devices=1)
    arrays = {**host_layout(inputs), **constants()}
    dram = {name: nc.dram_tensor(f"in_{name}_dram", a.shape, mybir.dt.from_np(a.dtype), kind="ExternalInput").ap()
            for name, a in arrays.items()}
    out = nc.dram_tensor("out_dram", [NB * TB, D], F32, kind="ExternalOutput").ap()
    build(nc, dram, out)
    result = run_bass_kernel_spmd(nc, [{f"in_{name}_dram": a for name, a in arrays.items()}], core_ids=[0])
    return result.results[0]["out_dram"].reshape(NB, TB, D)
```

```python
from contextlib import ExitStack

import numpy as np

import concourse.bass as bass
from concourse import mybir

F32 = mybir.dt.float32
F32R = mybir.dt.float32r
F16 = mybir.dt.float16
BF16 = mybir.dt.bfloat16
ALU = mybir.AluOpType
ACT = mybir.ActivationFunctionType

P = 128
NB, TB = 4, 256
BT = TB // P
NT = NB * BT
D = 512
KD = D // P
EPS = 1e-5
MASKED = -1e32

H0, HD0 = 32, 16
HPT = P // HD0
SC0 = HD0 ** -0.5
SLOTS = 4
PROB_SCALE = 2.0 ** 15
NEXP, RANK = 16, 16
ER = NEXP * RANK // P

NG, HG, HD1 = 8, 4, 128
SC1 = HD1 ** -0.5
QW = HG * HD1
GW = QW + 2 * HD1

F = 1376
FT = (F + P - 1) // P

SW = P + 2 * P


def alibi_slopes(n):
    start = 2.0 ** (-2.0 ** (-(np.log2(n) - 3)))
    return np.array([start ** (i + 1) for i in range(n)], dtype=np.float32)


def rope_tables():
    theta, factor, high, low, orig = 500000.0, 8.0, 4.0, 1.0, 1024
    inv = 1.0 / theta ** (np.arange(0, HD1, 2, dtype=np.float32) / HD1)
    wavelen = 2.0 * np.pi / inv
    scaled = np.where(wavelen > orig / low, inv / factor, inv)
    smooth = (orig / wavelen - low) / (high - low)
    smoothed = (1.0 - smooth) / factor * inv + smooth * inv
    medium = (wavelen <= orig / low) & (wavelen >= orig / high)
    inv = np.where(medium, smoothed, scaled).astype(np.float32)
    freqs = (np.arange(TB, dtype=np.float32)[None, :] * inv[:, None]).astype(np.float32)
    cos, sin = np.cos(freqs), np.sin(freqs)
    return (np.concatenate([cos, cos]).astype(np.float32),
            np.concatenate([-sin, sin]).astype(np.float32))


def constants():
    q, c = np.arange(P)[:, None], np.arange(2 * P)[None, :]
    hidden = np.where(c - P > q, np.float32(MASKED), np.float32(0))
    cos, sin = rope_tables()
    return {
        "ident": np.eye(P, dtype=np.float32),
        "causal": hidden.astype(np.float32),
        "distance": (c - (2 * P - 1) + hidden).astype(np.float32),
        "slot_rows": (np.arange(P)[:, None] // HD0 % 2 == np.arange(2)[None, :]).astype(np.float32),
        "cos": cos, "sin": sin,
    }


def stand_apart(engine):
    engine.nop(nofuse=True)


class Norm:

    def __init__(self, name, sb, sem):
        self.six = sb(f"{name}_six", [P, BT, 6], F32)
        self.mv = sb(f"{name}_mv", [P, BT, 2], F32)
        self.var_eps = sb(f"{name}_var_eps", [P, BT], F32)
        self.rstd = sb(f"{name}_rstd", [P, BT], F32)
        self.stats_done = sem(f"{name}_stats_done")
        self.moments_done = sem(f"{name}_moments_done")
        self.var_ready = sem(f"{name}_var_ready")
        self.rstd_ready = sem(f"{name}_rstd_ready")
        self.normed = sem(f"{name}_normed")

    def moments(self, dve, b, source, apart=False):
        for t in range(BT):
            if apart and t == 0:
                stand_apart(dve)
            dve.bn_stats(self.six[:, t, :], source(t)).then_inc(self.stats_done, 1)
        dve.wait_ge(self.stats_done, b * BT + BT)
        stand_apart(dve)
        for t in range(BT):
            dve.bn_aggr(self.mv[:, t, :], self.six[:, t, :]).then_inc(self.moments_done, 1)
        dve.wait_ge(self.moments_done, b * BT + BT)
        dve.tensor_scalar(self.var_eps[:, :], self.mv[:, :, 1], EPS, None, ALU.add)\
           .then_inc(self.var_ready, 1)

    def inverse(self, pool, b, minus_half):
        pool.wait_ge(self.var_ready, b + 1)
        pool.tensor_tensor(self.rstd[:, :], self.var_eps[:, :], minus_half, ALU.pow)\
            .then_inc(self.rstd_ready, 1)

    def apply(self, dve, b, source, target):
        dve.wait_ge(self.rstd_ready, b + 1)
        for t in range(BT):
            dve.tensor_scalar(target(t), source(t), self.mv[:, t, 0:1], self.rstd[:, t:t + 1],
                              ALU.subtract, ALU.mult).then_inc(self.normed, 1)


def split_product(pe, out, left, right, first, last):
    (lh, ll), (rh, rl) = left, right
    pe.matmul(out, lh, rh, start=first, stop=False)
    pe.matmul(out, lh, rl, start=False, stop=False)
    return pe.matmul(out, ll, rh, start=False, stop=last)


def layer0(nc, dram, X, ps, consts):
    ident, minus_half, consts_in = consts["ident"], consts["minus_half"], consts["in"]
    ctx = ExitStack()
    sb = lambda name, shape, dt: ctx.enter_context(nc.sbuf_tensor(name, shape, dt))
    sem = lambda name: nc.semaphore(name).__enter__()
    pair = lambda name, shape: [sb(f"{name}_{x}", shape, F32R) for x in ("hi", "lo")]

    a_raw = sb("a_raw", [P, ER, D], F32)
    bf_raw = sb("bf_raw", [P, ER, D], F32)
    gate_w = sb("gate_w", [P, 2, ER], F32)
    gate_p = sb("gate_p", [P, ER], F32)
    bias_b = sb("bias_b", [P, D], F32)

    def weight(name, shape):
        hi = sb(f"{name}_hi", shape, F32R)
        with nc.sbuf_tensor(f"{name}_raw", shape, F32) as raw:
            pass
        return raw, (hi, sb(f"{name}_lo", shape, F32R))

    wq_raw, wq = weight("wq0", [P, KD, D])
    wo_raw, wo = weight("wo0", [P, KD, D])
    wkv_raw, wkv = weight("wkv0", [P, KD, P + HD0])
    wf_raw, wf = weight("wf0", [P, KD, D])
    distance = sb("distance", [P, 2 * P], F32)
    slot_rows = sb("slot_rows", [P, 2], F32)
    alibi = sb("alibi", [P, H0, 2 * P], F32)
    x_tok = sb("x_tok0", [P, BT, D], F32)
    tok = sb("tok0", [P, BT, D], F32)
    delta = sb("delta0", [P, BT, D], F32)
    xT = pair("xT0", [P, KD, TB])
    q_slots = sb("q_slots", [P, BT, H0, SLOTS, HD0], F32R)
    qT = sb("qT0", [P, H0 // 2, TB], F32R)
    k_rows = pair("k_rows", [P, TB])
    kT_half = sb("kT_half", [P, TB], F32)
    kT = sb("kT0", [P, TB], F32R)
    vT = sb("vT0", [HD0, TB], F32)
    v = sb("v0", [P, BT, HD0], F32)
    v_rest = sb("v_rest0", [P, 2, BT, HD0], F32)
    v_next = sb("v_next0", [P, 3, BT, HD0], BF16)
    v_parts = sb("v_parts0", [P, 3, BT, HD0], BF16)
    prob = sb("prob0", [P, 4, SW], F32)
    neg_max = sb("neg_max0", [P, 4, 2], F32)
    row_sum = sb("row_sum0", [P, H0, 2], F32)
    row_inv = sb("row_inv0", [P, H0, 2], F32)
    probT = [sb(f"probT0_{x}", [P, 4, SW], F16) for x in ("hi", "lo")]
    fT = pair("fT0", [P, KD, TB])

    ln1, ln2, ln3, ln4 = (Norm(f"ln{n}", sb, sem) for n in (1, 2, 3, 4))

    x_in = [sem(f"x_in{b}") for b in range(NB)]
    wq_in, kv_in, wo_in, wf_in, small_in = (sem(n) for n in ("wq_in", "kv_in", "wo_in", "wf_in", "small_in"))
    wq_hi, wq_lo, wkv_hi, wkv_lo = (sem(n) for n in ("wq_hi", "wq_lo", "wkv_hi", "wkv_lo"))
    wo_hi, wo_lo, wf_hi, wf_lo = (sem(n) for n in ("wo_hi", "wo_lo", "wf_hi", "wf_lo"))
    gate_done, bf_scaled, adapters_done, w_eff_done = (sem(n) for n in ("gate_done", "bf_scaled", "adapters_done", "w_eff_done"))
    alibi_done = sem("alibi_done")
    xT_done, xT_hi, xT_lo = (sem(n) for n in ("xT_done0", "xT_hi0", "xT_lo0"))
    kv_done, k_hi, k_lo, vT_out, v_turned, v_out = (sem(n) for n in ("kv_done0", "k_hi0", "k_lo0", "vT_out0", "v_turned0", "v_out0"))
    kT_halved, kT_out, v_split, v_copied = (sem(n) for n in ("kT_halved0", "kT_out0", "v_split0", "v_copied0"))
    q_done, q_hi, q_lo = (sem(n) for n in ("q_done0", "q_hi0", "q_lo0"))
    qT_done, qT_act, qT_dve = (sem(n) for n in ("qT_done0", "qT_act0", "qT_dve0"))
    s_done, masked, exp_done, pT_done, pT_hi, pv_done, pT_lo = (sem(n) for n in ("s_done0", "masked0", "exp_done0", "pT_done0", "pT_hi0", "pv_done0", "pT_lo0"))
    inv_done, o_out, oT_done, oT_hi, oT_lo = (sem(n) for n in ("inv_done0", "o_out0", "oT_done0", "oT_hi0", "oT_lo0"))
    wo_done, x1_done, x1T_done, x1T_hi, x1T_lo = (sem(n) for n in ("wo_done0", "x1_done0", "x1T_done0", "x1T_hi0", "x1T_lo0"))
    ffn_done, biased, x2_done = (sem(n) for n in ("ffn_done0", "biased0", "x2_done0"))

    slopes = alibi_slopes(H0)

    LAG_T, LAG_HI, LAG_LO, LAG_V = 2, 3, 4, 5
    QG = H0 // 4
    AT = {"out": LAG_V, "oT": 6, "oT_out": 7, "wo": 8, "n2": 12, "x1": 13, "n3": 14, "a3": 15, "x1T": 16,
          "x1T_out": 17, "ffn": 20, "n4": 24, "x2": 26,
          "n1": 8, "a1": 10, "xT": 14, "xT_out": 15, "kv": 18, "kv_out": 19, "v": 20, "q0": 24, "q0_out": 26, "q1": 26, "q1_out": 28,
          "qT": (29, 30, 31, 0), "qT_out": (30, 31, 0, 1)}
    CHUNKS = 4
    MERGE = (6, 8, 10, 12)

    def q_bank(t):
        return ps[6 + t][:, :].rearrange("p (h a d) -> p h a d", h=H0, a=1).to_broadcast([P, H0, 2, HD0])

    def turned(bank):
        return ps[bank][:, :].rearrange("p (k n) -> p k n", k=KD)

    def xrow(b, t):
        return X[:, b * BT + t, :]

    def sync(sp):
        tiled = lambda name: dram[name].rearrange("(k p) n -> p k n", p=P)
        for b in range(NB):
            sp.dma_start(X[:, b * BT:(b + 1) * BT, :], dram["x"].rearrange("(n p) d -> p n d", p=P)[:, b * BT:(b + 1) * BT, :])\
              .then_inc(x_in[b], 16)
            if b == 0:
                sp.dma_start(wkv_raw[:, :, :], dram["wkv0"]).then_inc(kv_in, 16)
                sp.dma_start(wq_raw[:, :, :], tiled("wq0")).then_inc(wq_in, 16)
        sp.dma_start(wf_raw[:, :, :], tiled("wf0")).then_inc(wf_in, 16)
        sp.dma_start(a_raw[:, :, :], tiled("a0")).then_inc(wf_in, 16)
        sp.dma_start(bf_raw[:, :, :], tiled("bf0")).then_inc(wf_in, 16)
        sp.dma_start(wo_raw[:, :, :], tiled("wo0")).then_inc(wo_in, 16)

    def sync_consts(act):
        act.dma_start(distance[:, :], dram["distance"]).then_inc(small_in, 16)
        act.dma_start(slot_rows[:, :], dram["slot_rows"]).then_inc(small_in, 16)
        act.dma_start(gate_w[:, :, :], dram["gate_w"]).then_inc(small_in, 16)
        act.dma_start(bias_b[:, :], dram["bias0"].partition_broadcast(P)).then_inc(small_in, 16)

    def split_in_place(pl, raw, parts, hi_done, lo_done):
        pl.tensor_scalar(parts[0][:, :, :], raw[:, :, :], 1.0, 1.0, ALU.mult, ALU.mult).then_inc(hi_done, 1)
        pl.wait_ge(hi_done, 1)
        pl.tensor_tensor(parts[1][:, :, :], raw[:, :, :], parts[0][:, :, :].bitcast(F32), ALU.subtract)\
          .then_inc(lo_done, 1)

    def pool(pl):
        pl.wait_ge(small_in, 64)
        ln1.inverse(pl, 0, minus_half[:, 0:BT])
        for h in range(H0):
            pl.tensor_scalar(alibi[:, h, :], distance[:, :], float(slopes[h]) / SC0, 1.0, ALU.mult, ALU.mult)\
              .then_inc(alibi_done, 1)
        split_v(pl, 0)
        copy_v(pl, 0)
        ln1.inverse(pl, 1, minus_half[:, 0:BT])
        pl.wait_ge(wo_in, 16)
        split_in_place(pl, wo_raw, wo, wo_hi, wo_lo)
        pl.wait_ge(w_eff_done, KD)
        split_in_place(pl, wf_raw, wf, wf_hi, wf_lo)
        split_v(pl, 1)
        with pl.Fori(1, NB - 1) as b:
            pool_batch(pl, b, True)
        pool_batch(pl, NB - 1, False)
        for norm in (ln2, ln3, ln4):
            norm.inverse(pl, NB - 1, minus_half[:, 0:BT])

    def split_v(pl, b):
        pl.wait_ge(v_out, b + 1)
        if past(b, 1):
            pl.wait_ge(v_copied, b)
        stand_apart(pl)
        pl.tensor_copy(v_next[:, 0, :, :], v[:, :, :]).then_inc(v_split, 1)
        for n, (left, rest) in enumerate(((v[:, :, :], v_rest[:, 0, :, :]), (v_rest[:, 0, :, :], v_rest[:, 1, :, :]))):
            pl.wait_ge(v_split, b * 5 + 2 * n + 1)
            pl.tensor_tensor(rest, left, v_next[:, n, :, :], ALU.subtract).then_inc(v_split, 1)
            pl.wait_ge(v_split, b * 5 + 2 * n + 2)
            stand_apart(pl)
            pl.tensor_copy(v_next[:, n + 1, :, :], rest).then_inc(v_split, 1)

    def copy_v(pl, b):
        if past(b, 1):
            pl.wait_ge(pv_done, b * H0)
        pl.wait_ge(v_split, b * 5 + 5)
        stand_apart(pl)
        pl.tensor_copy(v_parts[:, :, :, :], v_next[:, :, :, :]).then_inc(v_copied, 1)

    def pool_batch(pl, b, prologue):
        copy_v(pl, b)
        if prologue:
            ln1.inverse(pl, b + 1, minus_half[:, 0:BT])
        ln2.inverse(pl, b - 1, minus_half[:, 0:BT])
        ln3.inverse(pl, b - 1, minus_half[:, 0:BT])
        if prologue:
            split_v(pl, b + 1)
        ln4.inverse(pl, b - 1, minus_half[:, 0:BT])

    def scalar(act):
        sync_consts(act)
        act.wait_ge(kv_in, 16)
        act.activation(wkv[0][:, :, :], wkv_raw[:, :, :], ACT.Copy).then_inc(wkv_hi, 1)
        act.wait_ge(wq_in, 16)
        act.activation(wq[0][:, :, :], wq_raw[:, :, :], ACT.Copy).then_inc(wq_hi, 1)
        act_xT(act, 0)
        act_kv(act, 0)
        act_q(act, 0, 0)
        act_q(act, 0, 1)
        act_qT(act, 0, 0)
        act_qT(act, 0, 1)
        act_batch(act, 0, False, True)
        with act.Fori(1, NB - 1) as b:
            act_batch(act, b, True, True)
        act_batch(act, NB - 1, True, False)
        for step in range(LAG_V):
            act_probT(act, NB, step)
        act_turned(act, NB - 1, oT_done, oT_hi)
        act_turned(act, NB - 1, x1T_done, x1T_hi)

    def act_xT(act, b):
        for t in range(BT):
            act.wait_ge(xT_done, b * BT + t + 1)
            act.activation(xT[0][:, :, t * P:(t + 1) * P], turned(6 + t), ACT.Copy).then_inc(xT_hi, 1)

    def act_kv(act, b):
        act.wait_ge(kv_done, b + 1)
        act.activation(vT[:, :], ps[6][0:HD0, TB:2 * TB], ACT.Copy).then_inc(vT_out, 1)
        act.activation(k_rows[0][:, :], ps[6][:, 0:TB], ACT.Copy).then_inc(k_hi, 1)

    def act_q(act, b, t):
        act.wait_ge(q_done, b * BT + t + 1)
        act.activation(q_slots[:, t, :, 0:2, :], q_bank(t), ACT.Copy).then_inc(q_hi, 1)

    def act_qT(act, b, j):
        n = 2 * j
        act.wait_ge(qT_done, b * QG + n + 1)
        if past(b, 1):
            act.wait_ge(s_done, (b - 1) * H0 + 4 * n + 4)
        act.activation(qT[:, 2 * n:2 * n + 2, :], ps[6][:, :].rearrange("p (k n) -> p k n", k=2), ACT.Copy)\
           .then_inc(qT_act, 1)

    def act_turned(act, b, done, hi):
        for t in range(BT):
            act.wait_ge(done, b * BT + t + 1)
            act.activation(fT[0][:, :, t * P:(t + 1) * P], turned(6 + t), ACT.Copy).then_inc(hi, 1)

    def act_probT(act, b, step):
        h = step - LAG_HI
        g = b * H0 + h
        if under_way(b, step, LAG_HI):
            act.wait_ge(pT_done, g + 1)
            if past(g, 4):
                act.wait_ge(pv_done, g - 3)
            act.activation(probT[0][:, h % 4, :], ps[2 + h % 2][:, 0:SW], ACT.Copy, scale=PROB_SCALE).then_inc(pT_hi, 1)

    def act_exp(act, b, step):
        h = step
        g = b * H0 + h
        act.wait_ge(masked, 2 * g + 2)
        if h % (H0 // 2) == 0 and past(b, 1):
            act.wait_ge(inv_done, (b - 1) * 2 + h // (H0 // 2) + 1)
        for qb, (c0, c1) in enumerate(((0, P), (P, SW))):
            act.activation(prob[:, h % 4, c0:c1], prob[:, h % 4, c0:c1], ACT.Exp,
                           bias=neg_max[:, h % 4, qb:qb + 1], scale=-1.0,
                           accum_out=row_sum[:, h, qb:qb + 1]).then_inc(exp_done, 1)

    def act_batch(act, b, tail, prologue):
        for step in range(H0):
            act_probT(act, b, step)
            if tail and step == AT["oT_out"]:
                act_turned(act, b - 1, oT_done, oT_hi)
            if tail and step == AT["x1T_out"]:
                act_turned(act, b - 1, x1T_done, x1T_hi)
            if prologue and step == AT["xT_out"]:
                act_xT(act, b + 1)
            if prologue and step == AT["kv_out"]:
                act_kv(act, b + 1)
            if prologue and step == AT["q0_out"]:
                act_q(act, b + 1, 0)
            if prologue and step == AT["q1_out"]:
                act_q(act, b + 1, 1)
            for j, at in enumerate(AT["qT_out"]):
                if step == at and (j >= 2 or prologue):
                    act_qT(act, b if j >= 2 else b + 1, j)
            act_exp(act, b, step)

    def lo_part(dve, hi, lo, source, ready, count, done):
        dve.wait_ge(ready, count)
        dve.tensor_tensor(lo, source, hi.bitcast(F32), ALU.subtract).then_inc(done, 1)

    def lo_in_place(dve, raw, parts, hi_done, lo_done):
        lo_part(dve, parts[0][:, :, :], parts[1][:, :, :], raw[:, :, :], hi_done, 1, lo_done)

    def vector(dve):
        dve.wait_ge(x_in[0], 16)
        ln1.moments(dve, 0, lambda t: xrow(0, t))
        lo_in_place(dve, wkv_raw, wkv, wkv_hi, wkv_lo)
        ln1.apply(dve, 0, lambda t: xrow(0, t), lambda t: x_tok[:, t, :])
        lo_in_place(dve, wq_raw, wq, wq_hi, wq_lo)
        dve_xT(dve, 0)
        dve.wait_ge(small_in, 64)
        dve_k(dve, 0)
        dve_v(dve, 0, 0)
        dve_q(dve, 0, 0)
        dve_q(dve, 0, 1)
        dve_qT(dve, 0, 0)
        dve_qT(dve, 0, 1)
        dve.wait_ge(wf_in, 48)
        dve.tensor_tensor(gate_p[:, :], gate_w[:, 0, :], gate_w[:, 1, :], ALU.mult).then_inc(gate_done, 1)
        dve.wait_ge(gate_done, 1)
        for r in range(ER):
            dve.tensor_scalar(bf_raw[:, r, :], bf_raw[:, r, :], gate_p[:, r:r + 1], None, ALU.mult).then_inc(bf_scaled, 1)
        for b in range(1, NB):
            dve.wait_ge(x_in[b], 16)
        dve_batch(dve, 0, False, True)
        with dve.Fori(1, NB - 1) as b:
            dve_batch(dve, b, True, True)
        dve_batch(dve, NB - 1, True, False)
        for step in range(LAG_V):
            dve_probT(dve, NB, step)
        dve_inverse(dve, NB - 1, 1)
        dve_out(dve, NB - 1)
        dve_fT(dve, NB - 1, oT_hi, oT_lo)
        dve_n2(dve, NB - 1)
        dve_x1(dve, NB - 1)
        dve_n3(dve, NB - 1)
        dve_a3(dve, NB - 1)
        dve_fT(dve, NB - 1, x1T_hi, x1T_lo)
        dve_n4(dve, NB - 1)
        dve_x2(dve, NB - 1)

    def dve_n1(dve, b):
        ln1.moments(dve, b, lambda t: xrow(b, t), True)

    def dve_a1(dve, b):
        dve.wait_ge(xT_done, b * BT)
        ln1.apply(dve, b, lambda t: xrow(b, t), lambda t: x_tok[:, t, :])

    def dve_xT(dve, b):
        for t in range(BT):
            lo_part(dve, xT[0][:, :, t * P:(t + 1) * P], xT[1][:, :, t * P:(t + 1) * P], turned(6 + t),
                    xT_hi, b * BT + t + 1, xT_lo)

    def dve_k(dve, b):
        lo_part(dve, k_rows[0][:, :], k_rows[1][:, :], ps[6][:, 0:TB], k_hi, b + 1, k_lo)
        if past(b, 1):
            dve.wait_ge(kT_out, b)
        dve.tensor_scalar(kT_half[:, :], k_rows[0][:, :].bitcast(F32), slot_rows[:, 0:1], None, ALU.mult).then_inc(kT_halved, 1)

    def dve_v(dve, b, bank, scores=None):
        if scores is None:
            dve.wait_ge(v_turned, b + 1)
        else:
            dve.wait_ge(s_done, scores)
        if past(b, 1):
            dve.wait_ge(v_split, b * 5)
        dve.tensor_scalar(v[:, :, :], ps[bank][:, SW:SW + BT * HD0].rearrange("p (t n) -> p t n", t=BT), 1.0 / PROB_SCALE, None, ALU.mult)\
           .then_inc(v_out, 1)

    def dve_kT(dve, b):
        dve.wait_ge(kT_halved, b + 1)
        dve.wait_ge(k_lo, b + 1)
        if past(b, 1):
            dve.wait_ge(s_done, b * H0)
        dve.scalar_tensor_tensor(kT[:, :], k_rows[1][:, :].bitcast(F32), slot_rows[:, 1:2], kT_half[:, :],
                                 ALU.mult, ALU.add).then_inc(kT_out, 1)

    def dve_q(dve, b, t):
        lo_part(dve, q_slots[:, t, :, 0:2, :], q_slots[:, t, :, 2:4, :], q_bank(t), q_hi, b * BT + t + 1, q_lo)

    def dve_qT(dve, b, j):
        n = 2 * j + 1
        dve.wait_ge(qT_done, b * QG + n + 1)
        if past(b, 1):
            dve.wait_ge(s_done, (b - 1) * H0 + 4 * n + 4)
        dve.tensor_copy(qT[:, 2 * n:2 * n + 2, :], ps[7][:, :].rearrange("p (k n) -> p k n", k=2)).then_inc(qT_dve, 1)

    def dve_probT(dve, b, step):
        h = step - LAG_LO
        g = b * H0 + h
        if under_way(b, step, LAG_LO):
            dve.wait_ge(pT_hi, g + 1)
            dve.scalar_tensor_tensor(probT[1][:, h % 4, :], ps[2 + h % 2][:, 0:SW], PROB_SCALE, probT[0][:, h % 4, :],
                                     ALU.mult, ALU.subtract).then_inc(pT_lo, 1)

    def dve_mask(dve, b, step):
        h = step
        g = b * H0 + h
        dve.wait_ge(s_done, g + 1)
        if not past(b, 1):
            dve.wait_ge(alibi_done, h + 1)
        if past(g, 4):
            dve.wait_ge(pT_done, g - 3)
        stand_apart(dve)
        for qb, (c0, c1) in enumerate(((0, P), (P, SW))):
            dve.tensor_tensor_reduce(prob[:, h % 4, c0:c1], ps[h % 2][:, c0:c1], alibi[:, h, 2 * P - (c1 - c0):2 * P],
                                     -SC0, 3e38, ALU.add, ALU.min, neg_max[:, h % 4, qb:qb + 1]).then_inc(masked, 1)

    def dve_inverse(dve, b, part):
        hs = slice(part * (H0 // 2), (part + 1) * (H0 // 2))
        dve.wait_ge(exp_done, (b * 2 + part + 1) * H0)
        if part == 0 and past(b, 1):
            dve.wait_ge(o_out, b * BT)
        dve.reciprocal(row_inv[:, hs, :], row_sum[:, hs, :]).then_inc(inv_done, 1)

    def dve_out(dve, b):
        dve.wait_ge(inv_done, b * 2 + 2)
        dve.wait_ge(pv_done, b * H0 + H0)
        for t in range(BT):
            dve.tensor_tensor(tok[:, t, :].rearrange("p (h d) -> p h d", h=H0),
                              ps[4 + t][:, :].rearrange("p (h d) -> p h d", h=H0),
                              row_inv[:, :, t:t + 1].to_broadcast([P, H0, HD0]), ALU.mult).then_inc(o_out, 1)

    def dve_fT(dve, b, hi, lo):
        for t in range(BT):
            lo_part(dve, fT[0][:, :, t * P:(t + 1) * P], fT[1][:, :, t * P:(t + 1) * P], turned(6 + t), hi, b * BT + t + 1, lo)

    def add_delta(dve, b, norm, done):
        dve.wait_ge(norm.normed, b * BT + BT)
        for t in range(BT):
            dve.tensor_tensor(xrow(b, t), xrow(b, t), delta[:, t, :], ALU.add).then_inc(done, 1)

    def dve_n2(dve, b):
        dve.wait_ge(wo_done, b * BT + BT)
        ln2.moments(dve, b, lambda t: ps[6 + t][:, :], True)

    def dve_x1(dve, b):
        ln2.apply(dve, b, lambda t: ps[6 + t][:, :], lambda t: delta[:, t, :])
        add_delta(dve, b, ln2, x1_done)

    def dve_n3(dve, b):
        dve.wait_ge(x1_done, b * BT + BT)
        ln3.moments(dve, b, lambda t: xrow(b, t), True)

    def dve_a3(dve, b):
        dve.wait_ge(oT_done, b * BT + BT)
        ln3.apply(dve, b, lambda t: xrow(b, t), lambda t: tok[:, t, :])

    def dve_n4(dve, b):
        for t in range(BT):
            dve.wait_ge(ffn_done, b * BT + t + 1)
            dve.tensor_tensor(delta[:, t, :], ps[6 + t][:, :], bias_b[:, :], ALU.add).then_inc(biased, 1)
        dve.wait_ge(biased, b * BT + BT)
        ln4.moments(dve, b, lambda t: delta[:, t, :], True)

    def dve_x2(dve, b):
        ln4.apply(dve, b, lambda t: delta[:, t, :], lambda t: delta[:, t, :])
        add_delta(dve, b, ln4, x2_done)

    def dve_merge(dve, k):
        dve.wait_ge(adapters_done, k + 1)
        dve.tensor_tensor(wf_raw[:, k, :], ps[6 + k % 2][:, :], wf_raw[:, k, :], ALU.add).then_inc(w_eff_done, 1)

    def dve_batch(dve, b, tail, prologue):
        for step in range(H0):
            if step == 0:
                dve_kT(dve, b)
            dve_probT(dve, b, step)
            for j, at in enumerate(AT["qT_out"]):
                if step == at and (j >= 2 or prologue):
                    dve_qT(dve, b if j >= 2 else b + 1, j)
            if prologue and step == AT["v"]:
                dve_v(dve, b + 1, step % 2, b * H0 + step + 1)
            dve_mask(dve, b, step)
            if step == 1 and tail:
                dve_inverse(dve, b - 1, 1)
            if step == H0 // 2 + 1:
                dve_inverse(dve, b, 0)
            if not tail and step - 1 in MERGE:
                dve_merge(dve, MERGE.index(step - 1))
            if tail and step == AT["out"]:
                dve_out(dve, b - 1)
            if tail and step == AT["oT_out"]:
                dve_fT(dve, b - 1, oT_hi, oT_lo)
            if tail and step == AT["n2"]:
                dve_n2(dve, b - 1)
            if tail and step == AT["x1"]:
                dve_x1(dve, b - 1)
            if tail and step == AT["n3"]:
                dve_n3(dve, b - 1)
            if tail and step == AT["a3"]:
                dve_a3(dve, b - 1)
            if tail and step == AT["x1T_out"]:
                dve_fT(dve, b - 1, x1T_hi, x1T_lo)
            if prologue and step == AT["n1"]:
                dve_n1(dve, b + 1)
            if tail and step == AT["n4"]:
                dve_n4(dve, b - 1)
            if prologue and step == AT["a1"]:
                dve_a1(dve, b + 1)
            if tail and step == AT["x2"]:
                dve_x2(dve, b - 1)
            if prologue and step == AT["xT_out"]:
                dve_xT(dve, b + 1)
            if prologue and step == AT["kv_out"]:
                dve_k(dve, b + 1)
            if prologue and step == AT["q0_out"]:
                dve_q(dve, b + 1, 0)
            if prologue and step == AT["q1_out"]:
                dve_q(dve, b + 1, 1)

    def tensor(pe):
        pe.wait_ge(consts_in, 16)
        pe_xT(pe, 0)
        pe.wait_ge(wkv_lo, 1)
        pe_kv(pe, 0)
        pe_v(pe, 0, 0)
        pe.wait_ge(wq_lo, 1)
        for t in range(BT):
            for half in range(2):
                pe_q(pe, 0, t, half)
        for j in range(3):
            pe_qT(pe, 0, j)
        pe_batch(pe, 0, False, True)
        with pe.Fori(1, NB - 1) as b:
            pe_batch(pe, b, True, True)
        pe_batch(pe, NB - 1, True, False)
        for step in range(LAG_V):
            pe_head(pe, NB, step)
        pe_oT(pe, NB - 1, True)
        for chunk in range(CHUNKS):
            pe_linear(pe, NB - 1, wo, oT_lo, wo_done, chunk)
        pe_x1T(pe, NB - 1, False)
        for chunk in range(CHUNKS):
            pe_linear(pe, NB - 1, wf, x1T_lo, ffn_done, chunk)

    def transpose_tok(pe, source, t, done):
        for k in range(KD):
            last = pe.transpose(ps[6 + t][:, k * P:(k + 1) * P], source[:, t, k * P:(k + 1) * P], ident[:, :])
        last.then_inc(done, 1)

    def pe_xT(pe, b):
        for t in range(BT):
            pe.wait_ge(ln1.normed, b * BT + t + 1)
            if past(b, 2):
                pe.wait_ge(ln2.normed, (b - 1) * BT)
            elif b == 1:
                pe.wait_ge(w_eff_done, KD)
            transpose_tok(pe, x_tok, t, xT_done)

    def pe_kv(pe, b):
        pe.wait_ge(xT_lo, b * BT + BT)
        if past(b, 2):
            pe.wait_ge(x1T_lo, (b - 1) * BT)
        for k in range(KD):
            split_product(pe, ps[6][:, 0:TB], (wkv[0][:, k, 0:P], wkv[1][:, k, 0:P]),
                          (xT[0][:, k, :], xT[1][:, k, :]), k == 0, k == KD - 1)
        for k in range(KD):
            last = split_product(pe, ps[6][0:HD0, TB:2 * TB], (wkv[0][:, k, P:P + HD0], wkv[1][:, k, P:P + HD0]),
                                 (xT[0][:, k, :], xT[1][:, k, :]), k == 0, k == KD - 1)
        last.then_inc(kv_done, 1)

    def pe_v(pe, b, bank):
        pe.wait_ge(vT_out, b + 1)
        stand_apart(pe)
        for t in range(BT):
            last = pe.transpose(ps[bank][:, SW + t * HD0:SW + (t + 1) * HD0], vT[:, t * P:(t + 1) * P], ident[0:HD0, 0:HD0])
        last.then_inc(v_turned, 1)

    def pe_q(pe, b, t, half):
        if half == 0 and t == 0:
            pe.wait_ge(k_lo, b + 1)
            pe.wait_ge(vT_out, b + 1)
        if half == 0 and past(b, 2):
            pe.wait_ge(biased, (b - 1) * BT - 1 + t)
        for k in range(KD // 2 * half, KD // 2 * (half + 1)):
            last = split_product(pe, ps[6 + t][:, :], (xT[0][:, k, t * P:(t + 1) * P], xT[1][:, k, t * P:(t + 1) * P]),
                                 (wq[0][:, k, :], wq[1][:, k, :]), k == 0, k == KD - 1)
        if half == 1:
            last.then_inc(q_done, 1)

    def pe_qT(pe, b, j):
        if j == 0:
            pe.wait_ge(q_lo, b * BT + BT)
        else:
            pe.wait_ge(qT_act, b * (QG // 2) + j)
            pe.wait_ge(qT_dve, b * (QG // 2) + j)
        for n in (2 * j, 2 * j + 1):
            for c in range(4):
                two, t = 2 * n + c // 2, c % 2
                last = pe.transpose(ps[6 + n % 2][:, c * P:(c + 1) * P],
                                    q_slots[:, t, 2 * two:2 * two + 2, :, :].rearrange("p h s d -> p (h s d)").bitcast(F32),
                                    ident[:, :])
            last.then_inc(qT_done, 1)

    def pe_head(pe, b, step, v_too=False):
        h = step
        g = b * H0 + h
        if not past_end(b):
            rows = slice(64 * (h % 2), 64 * (h % 2) + 64)
            if h == 0:
                pe.wait_ge(kT_out, b + 1)
            if h % 8 == 0:
                pe.wait_ge(qT_act, b * (QG // 2) + h // 8 + 1)
            if h % 8 == 4:
                pe.wait_ge(qT_dve, b * (QG // 2) + h // 8 + 1)
            if past(g, 2):
                pe.wait_ge(masked, 2 * (g - 1))
            elif g == 0:
                pe.wait_ge(v_out, 1)
            if v_too:
                pe_v(pe, b + 1, h % 2)
            pe.matmul(ps[h % 2][:, 0:P], qT[rows, h // 2, 0:P], kT[rows, 0:P], start=True, stop=True)
            pe.matmul(ps[h % 2][:, P:SW], qT[rows, h // 2, P:TB], kT[rows, :], start=True, stop=True).then_inc(s_done, 1)
        h = step - LAG_T
        g = b * H0 + h
        if under_way(b, step, LAG_T):
            pe.wait_ge(exp_done, 2 * g + 2)
            if past(g, 2):
                pe.wait_ge(pT_lo, g - 1)
            for n in range(3):
                last = pe.transpose(ps[2 + h % 2][:, n * P:(n + 1) * P], prob[:, h % 4, n * P:(n + 1) * P], ident[:, :])
            last.then_inc(pT_done, 1)
        h = (step - LAG_V) % H0
        g = b * H0 + step - LAG_V
        if under_way(b, step, LAG_V):
            pe.wait_ge(pT_lo, g + 1)
            if h == 0:
                pe.wait_ge(v_copied, b + 1)
                if past(b, 1):
                    pe.wait_ge(o_out, b * BT)
            cols = slice(h * HD0, (h + 1) * HD0)
            for qb, kb, c in ((0, 0, 0), (1, 0, P), (1, 1, 2 * P)):
                for part in range(2):
                    for n in range(3):
                        last = pe.matmul(ps[4 + qb][:, cols], probT[part][:, h % 4, c:c + P], v_parts[:, n, kb, :],
                                         start=(kb == 0 and part == 0 and n == 0), stop=(kb == qb and part == 1 and n == 2))
            last.then_inc(pv_done, 1)

    def pe_merge(pe, k):
        pe.wait_ge(bf_scaled, ER)
        if k < 2:
            pe.wait_ge(qT_act, QG // 2)
            pe.wait_ge(qT_dve, QG // 2)
        else:
            pe.wait_ge(w_eff_done, k - 1)
        for r in range(ER):
            last = pe.matmul(ps[6 + k % 2][:, :], a_raw[:, r, k * P:(k + 1) * P], bf_raw[:, r, :],
                             start=(r == 0), stop=(r == ER - 1))
        last.then_inc(adapters_done, 1)

    def pe_oT(pe, b, last):
        for t in range(BT):
            pe.wait_ge(o_out, b * BT + t + 1)
            if last:
                pe.wait_ge(biased, b * BT)
            else:
                pe.wait_ge(qT_act, (b + 2) * (QG // 2))
                pe.wait_ge(qT_dve, (b + 2) * (QG // 2))
            transpose_tok(pe, tok, t, oT_done)

    def pe_linear(pe, b, weights, ready, done, chunk):
        t, half = divmod(chunk, 2)
        if chunk == 0:
            pe.wait_ge(ready, b * BT + BT)
        for k in range(KD // 2 * half, KD // 2 * (half + 1)):
            last = split_product(pe, ps[6 + t][:, :], (fT[0][:, k, t * P:(t + 1) * P], fT[1][:, k, t * P:(t + 1) * P]),
                                 (weights[0][:, k, :], weights[1][:, k, :]), k == 0, k == KD - 1)
        if half == 1:
            last.then_inc(done, 1)

    def pe_x1T(pe, b, shared):
        for t in range(BT):
            pe.wait_ge(ln3.normed, b * BT + t + 1)
            if shared:
                pe.wait_ge(xT_lo, (b + 3) * BT)
            transpose_tok(pe, tok, t, x1T_done)

    def pe_batch(pe, b, tail, prologue):
        for step in range(H0):
            pe_head(pe, b, step, prologue and step == AT["v"])
            if not tail and step in MERGE:
                pe_merge(pe, MERGE.index(step))
            if tail and step == AT["oT"]:
                pe_oT(pe, b - 1, False)
            if tail and 0 <= step - AT["wo"] < CHUNKS:
                pe.wait_ge(wo_lo, 1)
                pe_linear(pe, b - 1, wo, oT_lo, wo_done, step - AT["wo"])
            if prologue and step == AT["xT"]:
                pe_xT(pe, b + 1)
            if tail and step == AT["x1T"]:
                pe_x1T(pe, b - 1, prologue)
            if prologue and step == AT["kv"]:
                pe_kv(pe, b + 1)
            if tail and 0 <= step - AT["ffn"] < CHUNKS:
                pe.wait_ge(wf_lo, 1)
                if prologue:
                    pe.wait_ge(k_lo, b + 2)
                    pe.wait_ge(vT_out, b + 2)
                pe_linear(pe, b - 1, wf, x1T_lo, ffn_done, step - AT["ffn"])
            for t in range(BT):
                if prologue and 0 <= step - AT[f"q{t}"] < 2:
                    pe_q(pe, b + 1, t, step - AT[f"q{t}"])
            for j, at in enumerate(AT["qT"]):
                if step == at and (j == 3 or prologue):
                    pe_qT(pe, b if j == 3 else b + 1, j)

    ctx.close()
    return {"sync": sync, "pool": pool, "scalar": scalar, "vector": vector,
            "tensor": tensor, "done": x2_done, "done_count": NT}


def past(count, n):
    return not isinstance(count, int) or count >= n


def past_end(b):
    return isinstance(b, int) and b == NB


def under_way(b, step, lag):
    return past(b * H0 + step - lag, 0) and not (past_end(b) and step >= lag)


class BatchNorm:

    def __init__(self, name, sb, sem):
        self.six = sb(f"{name}_six", [P, 2, BT, 6], F32)
        self.mv = sb(f"{name}_mv", [P, 2, BT, 2], F32)
        self.var_eps = sb(f"{name}_var_eps", [P, 2, BT], F32)
        self.rstd = sb(f"{name}_rstd", [P, 2, BT], F32)
        self.stats_done = sem(f"{name}_stats_done")
        self.moments_done = sem(f"{name}_moments_done")
        self.var_ready = sem(f"{name}_var_ready")
        self.rstd_ready = sem(f"{name}_rstd_ready")
        self.normed = sem(f"{name}_normed")

    def moments(self, dve, use, source):
        n = use % 2
        if use >= 2:
            dve.wait_ge(self.normed, (use - 1) * BT)
        for t in range(BT):
            dve.bn_stats(self.six[:, n, t, :], source(t)).then_inc(self.stats_done, 1)
        for t in range(BT):
            dve.wait_ge(self.stats_done, use * BT + t + 1)
            dve.bn_aggr(self.mv[:, n, t, :], self.six[:, n, t, :]).then_inc(self.moments_done, 1)
        dve.wait_ge(self.moments_done, use * BT + BT)
        dve.tensor_scalar(self.var_eps[:, n, :], self.mv[:, n, :, 1], EPS, None, ALU.add).then_inc(self.var_ready, 1)

    def inverse(self, pool, use, minus_half):
        pool.wait_ge(self.var_ready, use + 1)
        pool.tensor_tensor(self.rstd[:, use % 2, :], self.var_eps[:, use % 2, :], minus_half[:, 0:BT], ALU.pow)\
            .then_inc(self.rstd_ready, 1)

    def apply(self, dve, use, source, target):
        n = use % 2
        dve.wait_ge(self.rstd_ready, use + 1)
        for t in range(BT):
            dve.tensor_scalar(target(t), source(t), self.mv[:, n, t, 0:1], self.rstd[:, n, t:t + 1],
                              ALU.subtract, ALU.mult).then_inc(self.normed, 1)


class Stream:

    def __init__(self, sb, sem, X, XT, acc, ps, ident, minus_half):
        self.X, self.XT, self.acc, self.ps, self.ident, self.minus_half = X, XT, acc, ps, ident, minus_half
        self.post = BatchNorm("post", sb, sem)
        self.pre = BatchNorm("pre", sb, sem)
        self.tok = sb("turn_tok", [P, 2 * BT, D], F32)
        self.summed = sem("summed")
        self.turned = sem("turned")
        self.hi_out = sem("turn_hi_out")
        self.lo_out = sem("turn_lo_out")

    def rows(self, what, b):
        return lambda t: what[:, b * BT + t, :]

    def post_moments(self, dve, rnd, b):
        self.post.moments(dve, rnd * NB + b, self.rows(self.acc, b))

    def post_apply(self, dve, rnd, b):
        self.post.apply(dve, rnd * NB + b, self.rows(self.acc, b), self.rows(self.acc, b))

    def add(self, engine, rnd, b):
        X, acc = self.X, self.acc
        for t in range(BT):
            n = b * BT + t
            engine.wait_ge(self.post.normed, rnd * NT + n + 1)
            engine.tensor_tensor(X[:, n, :], X[:, n, :], acc[:, n, :], ALU.add).then_inc(self.summed, 1)

    def pre_moments(self, dve, rnd, b):
        if rnd:
            dve.wait_ge(self.summed, b * BT + BT)
        self.pre.moments(dve, rnd * NB + b, self.rows(self.X, b))

    def pre_apply(self, dve, rnd, b):
        self.pre.apply(dve, rnd * NB + b, self.rows(self.X, b), lambda t: self.tok[:, b % 2 * BT + t, :])

    def turn(self, pe, rnd, n, bank):
        pe.wait_ge(self.pre.normed, rnd * NT + n + 1)
        for k in range(KD):
            last = pe.transpose(self.ps[bank][:, k * P:(k + 1) * P], self.tok[:, n % (2 * BT), k * P:(k + 1) * P],
                                self.ident[:, :])
        last.then_inc(self.turned, 1)

    def turned_tile(self, bank):
        return self.ps[bank][:, :].rearrange("p (k n) -> p k n", k=KD)

    def hi(self, act, rnd, n, bank):
        act.wait_ge(self.turned, rnd * NT + n + 1)
        act.activation(self.XT[0][:, :, n * P:(n + 1) * P], self.turned_tile(bank), ACT.Copy).then_inc(self.hi_out, 1)

    def lo(self, dve, rnd, n, bank):
        dve.wait_ge(self.hi_out, rnd * NT + n + 1)
        dve.tensor_tensor(self.XT[1][:, :, n * P:(n + 1) * P], self.turned_tile(bank),
                          self.XT[0][:, :, n * P:(n + 1) * P].bitcast(F32), ALU.subtract).then_inc(self.lo_out, 1)


def layer1_attention(nc, dram, stream, XT, acc, ps, consts, room):
    ident = consts["ident"]
    ctx = ExitStack()
    sb = lambda name, shape, dt: ctx.enter_context(nc.sbuf_tensor(name, shape, dt))
    sem = lambda name: nc.semaphore(name).__enter__()
    pair = lambda name, shape: [sb(f"{name}_{x}", shape, F32R) for x in ("hi", "lo")]

    w_raw = sb("w_raw1", [P, KD, GW], F32)
    w = pair("w1", [P, KD, GW])
    cos, sin = sb("cos1", [P, TB], F32), sb("sin1", [P, TB], F32)
    causal = sb("causal1", [P, 2 * P], F32)
    wo_raw = sb("wo_raw1", [P, HG, D], F32)
    wo = pair("wo1", [P, HG, D])
    prob = sb("prob1", [P, HG, SW], F32)
    neg_max = sb("neg_max1", [P, HG, 2], F32)
    row_sum = sb("row_sum1", [P, HG, 2], F32)
    row_inv = sb("row_inv1", [P, HG, 2], F32)
    pT = pair("pT1", [P, HG, SW])
    oT = pair("oT1", [P, HG, TB])
    k_sum, k_rot = sb("k_sum1", [P, TB], F32), sb("k_rot1", [P, TB], F32)
    q_sum, q_rot = sb("q_sum1", [P, 2, TB], F32), sb("q_rot1", [P, 2, TB], F32)
    vT = sb("vT1", [P, TB], F32)
    q = [pair(f"q1_{n}", [P, HG, TB]) for n in range(2)]
    k = [pair(f"k1_{n}", [P, TB]) for n in range(2)]
    v = [pair(f"v1_{n}", [P, BT, HD1]) for n in range(2)]

    acc_zero, tables_in, w_in, wo_in = sem("acc_zero"), sem("tables_in"), sem("w_in1"), sem("wo_in1")
    kvw_hi, qw_hi, kvw_lo, qw_lo, wo_hi, wo_lo = (sem(n) for n in ("kvw_hi", "qw_hi", "kvw_lo", "qw_lo", "wo_hi1", "wo_lo1"))
    s_done, masked, exp_done, inv_done, normed = (sem(n) for n in ("s_done1", "masked1", "exp_done1", "inv_done1", "normed1"))
    pT_done, pT_hi, pT_lo = (sem(n) for n in ("pT_done1", "pT_hi1", "pT_lo1"))
    kv_done, vT_out, v_turned, v_hi, v_lo = (sem(n) for n in ("kv_done1", "vT_out1", "v_turned1", "v_hi1", "v_lo1"))
    k_halves, k_sin, k_cos, k_added, k_hi, k_lo = (sem(n) for n in ("k_halves", "k_sin", "k_cos", "k_added", "k_hi1", "k_lo1"))
    q_done, q_halves, q_sin, q_cos, q_added, q_hi, q_lo = (sem(n) for n in ("q_done1", "q_halves", "q_sin", "q_cos", "q_added", "q_hi1", "q_lo1"))
    pv_done, o_hi, o_lo, wo_done, added = (sem(n) for n in ("pv_done1", "o_hi1", "o_lo1", "wo_done1", "added1"))

    BS, BP, BO, BM = (0, 1), (2, 3), 4, (5, 6, 7)
    KC, VC, QC = 0, HD1, 2 * HD1
    half = HD1 // 2

    def heads(bank):
        return ps[bank][:, :].rearrange("p (h n) -> p h n", h=2)

    def over_pair(table):
        return table[:, :].rearrange("p (a n) -> p a n", a=1).to_broadcast([P, 2, TB])

    def over_groups(engine, step):
        for b in range(NB):
            step(0, b, b > 0, True)
        with engine.Fori(1, NG - 1) as g:
            for b in range(NB):
                step(g, b, True, True)
        for b in range(NB):
            step(NG - 1, b, True, b < NB - 1)

    def sync(sp):
        sp.wait_ge(*room)
        sp.dma_start(cos[:, :], dram["cos"]).then_inc(tables_in, 16)
        sp.dma_start(sin[:, :], dram["sin"]).then_inc(tables_in, 16)
        sp.dma_start(causal[:, :], dram["causal"]).then_inc(tables_in, 16)
        sp.dma_start(w_raw[:, :, :], dram["w1"][0]).then_inc(w_in, 16)
        sp.dma_start(wo_raw[:, :, :], dram["wo1"][0]).then_inc(wo_in, 16)
        with sp.Fori(1, NG) as g:
            sp.wait_ge(kvw_lo, g)
            sp.wait_ge(qw_lo, g)
            sp.dma_start(w_raw[:, :, :], dram["w1"][g]).then_inc(w_in, 16)
            sp.wait_ge(wo_lo, g)
            sp.dma_start(wo_raw[:, :, :], dram["wo1"][g]).then_inc(wo_in, 16)

    def project_kv(pe, u, b):
        if past(u, 1):
            pe.wait_ge(v_lo, u)
        xs = slice(b * TB, (b + 1) * TB)
        for c0, o in ((KC, 0), (VC, TB)):
            for n in range(KD):
                last = split_product(pe, ps[BM[0]][:, o:o + TB], (w[0][:, n, c0:c0 + HD1], w[1][:, n, c0:c0 + HD1]),
                                     (XT[0][:, n, xs], XT[1][:, n, xs]), n == 0, n == KD - 1)
        last.then_inc(kv_done, 1)

    def project_q(pe, u, b, p):
        if past(u, 3):
            pe.wait_ge(added, (u - 3) * 2 + p + 1)
        elif u:
            pe.wait_ge(q_cos, (u - 1) * 2 + p + 1)
        xs = slice(b * TB, (b + 1) * TB)
        for h in (2 * p, 2 * p + 1):
            c0 = QC + h * HD1
            for n in range(KD):
                last = split_product(pe, ps[BM[1 + p]][:, (h % 2) * TB:(h % 2 + 1) * TB],
                                     (w[0][:, n, c0:c0 + HD1], w[1][:, n, c0:c0 + HD1]),
                                     (XT[0][:, n, xs], XT[1][:, n, xs]), n == 0, n == KD - 1)
        last.then_inc(q_done, 1)

    def turn_v(pe, u, b):
        pe.wait_ge(vT_out, u + 1)
        pe.wait_ge(k_cos, u + 1)
        for t in range(BT):
            last = pe.transpose(ps[BM[0]][:, t * P:(t + 1) * P], vT[:, t * P:(t + 1) * P], ident[:, :])
        last.then_inc(v_turned, 1)

    def scores(pe, u, b, h):
        n = b % 2
        if h == 0:
            pe.wait_ge(k_lo, u + 1)
        if h % 2 == 0:
            pe.wait_ge(q_lo, u * 2 + h // 2 + 1)
        if (h >= 2 or past(u, 1)):
            pe.wait_ge(masked, u * 8 + 2 * (h - 1))
        for qs, ks, cols in ((slice(0, P), slice(0, P), slice(0, P)), (slice(P, TB), slice(0, TB), slice(P, SW))):
            last = split_product(pe, ps[BS[h % 2]][:, cols], (q[n][0][:, h, qs], q[n][1][:, h, qs]),
                                 (k[n][0][:, ks], k[n][1][:, ks]), True, True)
        last.then_inc(s_done, 1)

    def turn_prob(pe, u, b, h):
        pe.wait_ge(normed, u * 8 + 2 * h + 2)
        if (h >= 2 or past(u, 1)):
            pe.wait_ge(pT_lo, u * HG + h - 1)
        for n in range(3):
            last = pe.transpose(ps[BP[h % 2]][:, n * P:(n + 1) * P], prob[:, h, n * P:(n + 1) * P], ident[:, :])
        last.then_inc(pT_done, 1)

    def prob_v(pe, u, b, p):
        n = b % 2
        pe.wait_ge(pT_lo, u * HG + 2 * p + 2)
        if p == 0:
            pe.wait_ge(v_lo, u + 1)
        if (p or past(u, 1)):
            pe.wait_ge(o_lo, u * 2 + p)
        hs = slice(2 * p, 2 * p + 2)
        for kb, cols, qs in ((0, slice(0, 2 * P), slice(0, TB)), (1, slice(2 * P, SW), slice(P, TB))):
            last = split_product(pe, heads(BO)[:, :, qs], (v[n][0][:, kb, :], v[n][1][:, kb, :]),
                                 (pT[0][:, hs, cols], pT[1][:, hs, cols]), kb == 0, kb == 1)
        last.then_inc(pv_done, 1)

    def project_out(pe, u, b, t):
        if t == 0:
            pe.wait_ge(o_lo, u * 2 + 2)
        for h in range(HG):
            last = split_product(pe, ps[BM[1 + t]][:, :], (oT[0][:, h, t * P:(t + 1) * P], oT[1][:, h, t * P:(t + 1) * P]),
                                 (wo[0][:, h, :], wo[1][:, h, :]), h == 0, h == HG - 1)
        last.then_inc(wo_done, 1)

    U = NG * NB

    def finishing(g, b):
        return b - 2 if isinstance(g, int) and g == NG - 1 and b >= 2 else None

    def tensor(pe):
        pe.wait_ge(stream.lo_out, NT)
        pe.wait_ge(kvw_lo, 1)
        project_kv(pe, 0, 0)
        pe.wait_ge(qw_lo, 1)
        project_q(pe, 0, 0, 0)
        project_q(pe, 0, 0, 1)
        turn_v(pe, 0, 0)

        def step(g, b, before, after):
            u, nb, pb = g * NB + b, (b + 1) % NB, (b - 1) % NB
            scores(pe, u, b, 0)
            scores(pe, u, b, 1)
            if before:
                prob_v(pe, u - 1, pb, 1)
            if after:
                if nb == 0:
                    pe.wait_ge(kvw_lo, g + 2)
                project_kv(pe, u + 1, nb)
            scores(pe, u, b, 2)
            scores(pe, u, b, 3)
            if after:
                if nb == 0:
                    pe.wait_ge(qw_lo, g + 2)
                project_q(pe, u + 1, nb, 0)
            turn_prob(pe, u, b, 0)
            turn_prob(pe, u, b, 1)
            if after:
                project_q(pe, u + 1, nb, 1)
                turn_v(pe, u + 1, nb)
            if before:
                wait_q_left(pe, u, after, 0)
                if pb == 0:
                    pe.wait_ge(wo_lo, g + 1)
                project_out(pe, u - 1, pb, 0)
            turn_prob(pe, u, b, 2)
            turn_prob(pe, u, b, 3)
            if before:
                wait_q_left(pe, u, after, 1)
                project_out(pe, u - 1, pb, 1)
            done = finishing(g, b)
            if done is not None:
                stream.turn(pe, 1, done * BT, BM[0])
            prob_v(pe, u, b, 0)
            if done is not None:
                pe.wait_ge(stream.lo_out, NT + done * BT + 1)
                stream.turn(pe, 1, done * BT + 1, BM[0])

        over_groups(pe, step)
        prob_v(pe, U - 1, NB - 1, 1)
        pe.wait_ge(added, U * 2 - 2)
        project_out(pe, U - 1, NB - 1, 0)
        project_out(pe, U - 1, NB - 1, 1)

    def wait_q_left(pe, u, after, t):
        pe.wait_ge(q_cos, u * 2 + 3 + t if after else u * 2 + 1 + t)

    def act_weights(act, g):
        act.wait_ge(w_in, g * 16 + 16)
        if past(g, 1):
            act.wait_ge(q_done, g * (2 * NB))
        act.activation(w[0][:, :, 0:QC], w_raw[:, :, 0:QC], ACT.Copy).then_inc(kvw_hi, 1)
        act.activation(w[0][:, :, QC:GW], w_raw[:, :, QC:GW], ACT.Copy).then_inc(qw_hi, 1)

    def act_wo(act, g):
        act.wait_ge(wo_in, g * 16 + 16)
        if past(g, 1):
            act.wait_ge(wo_done, g * (2 * NB))
        act.activation(wo[0][:, :, :], wo_raw[:, :, :], ACT.Copy).then_inc(wo_hi, 1)

    def swap_halves(act, target, source, done):
        act.activation(target[0:half], source[half:HD1], ACT.Copy).then_inc(done, 1)
        act.activation(target[half:HD1], source[0:half], ACT.Copy).then_inc(done, 1)

    def act_kv(act, u, b):
        act.wait_ge(kv_done, u + 1)
        if past(u, 1):
            act.wait_ge(k_added, u)
            act.wait_ge(v_turned, u)
        act.activation(vT[:, :], ps[BM[0]][:, TB:2 * TB], ACT.Copy).then_inc(vT_out, 1)
        swap_halves(act, k_rot, ps[BM[0]][:, 0:TB], k_halves)

    def act_k_hi(act, u, b):
        act.wait_ge(k_added, u + 1)
        act.activation(k[b % 2][0][:, :], k_sum[:, :], ACT.Copy).then_inc(k_hi, 1)

    def act_q(act, u, b, p):
        act.wait_ge(q_done, u * 2 + p + 1)
        if (p or past(u, 1)):
            act.wait_ge(q_added, u * 2 + p)
        swap_halves(act, q_rot, heads(BM[1 + p]), q_halves)

    def act_q_hi(act, u, b, p):
        act.wait_ge(q_added, u * 2 + p + 1)
        act.activation(q[b % 2][0][:, 2 * p:2 * p + 2, :], q_sum[:, :, :], ACT.Copy).then_inc(q_hi, 1)

    def act_v_hi(act, u, b):
        act.wait_ge(v_turned, u + 1)
        act.activation(v[b % 2][0][:, :, :], ps[BM[0]][:, 0:TB].rearrange("p (t n) -> p t n", t=BT), ACT.Copy).then_inc(v_hi, 1)

    def act_exp(act, u, b, h):
        act.wait_ge(masked, u * 8 + 2 * h + 2)
        if past(u, 1):
            act.wait_ge(inv_done, u * 2)
        for qb, (c0, c1) in enumerate(((0, P), (P, SW))):
            act.activation(prob[:, h, c0:c1], prob[:, h, c0:c1], ACT.Exp, bias=neg_max[:, h, qb:qb + 1], scale=-1.0,
                           accum_out=row_sum[:, h, qb:qb + 1]).then_inc(exp_done, 1)

    def act_pT(act, u, b, h):
        act.wait_ge(pT_done, u * HG + h + 1)
        act.activation(pT[0][:, h, :], ps[BP[h % 2]][:, 0:SW], ACT.Copy).then_inc(pT_hi, 1)

    def act_o(act, u, b, p):
        act.wait_ge(pv_done, u * 2 + p + 1)
        act.activation(oT[0][:, 2 * p:2 * p + 2, :], heads(BO), ACT.Copy).then_inc(o_hi, 1)

    def scalar(act):
        act_weights(act, 0)
        act_kv(act, 0, 0)
        act_k_hi(act, 0, 0)
        act_q(act, 0, 0, 0)
        act_q_hi(act, 0, 0, 0)
        act_q(act, 0, 0, 1)
        act_q_hi(act, 0, 0, 1)
        act_v_hi(act, 0, 0)
        act_wo(act, 0)

        def step(g, b, before, after):
            u, nb, pb = g * NB + b, (b + 1) % NB, (b - 1) % NB
            act_exp(act, u, b, 0)
            act_exp(act, u, b, 1)
            if before:
                act_o(act, u - 1, pb, 1)
            if b == 1 and past(g, 1):
                act_wo(act, g)
            if after:
                act_kv(act, u + 1, nb)
            act_exp(act, u, b, 2)
            act_exp(act, u, b, 3)
            if after:
                act_k_hi(act, u + 1, nb)
                act_q(act, u + 1, nb, 0)
            act_pT(act, u, b, 0)
            act_pT(act, u, b, 1)
            if after:
                act_q_hi(act, u + 1, nb, 0)
                act_q(act, u + 1, nb, 1)
                act_q_hi(act, u + 1, nb, 1)
                act_v_hi(act, u + 1, nb)
            act_pT(act, u, b, 2)
            act_pT(act, u, b, 3)
            done = finishing(g, b)
            if done is not None:
                stream.hi(act, 1, done * BT, BM[0])
            act_o(act, u, b, 0)
            if done is not None:
                stream.hi(act, 1, done * BT + 1, BM[0])
            if b == 2 and not (isinstance(g, int) and g == NG - 1):
                act_weights(act, g + 1)

        over_groups(act, step)
        act_o(act, U - 1, NB - 1, 1)

    def dve_kvw(dve, g):
        dve.wait_ge(kvw_hi, g + 1)
        dve.tensor_tensor(w[1][:, :, 0:QC], w_raw[:, :, 0:QC], w[0][:, :, 0:QC].bitcast(F32), ALU.subtract).then_inc(kvw_lo, 1)

    def dve_k_cos(dve, u, b):
        dve.wait_ge(k_halves, u * 2 + 2)
        if past(u, 1):
            dve.wait_ge(k_lo, u)
        dve.tensor_tensor(k_sum[:, :], ps[BM[0]][:, 0:TB], cos[:, :], ALU.mult).then_inc(k_cos, 1)

    def dve_k_add(dve, u, b):
        dve.wait_ge(k_sin, u + 1)
        dve.wait_ge(k_cos, u + 1)
        dve.tensor_tensor(k_sum[:, :], k_sum[:, :], k_rot[:, :], ALU.add).then_inc(k_added, 1)

    def dve_k_lo(dve, u, b):
        dve.wait_ge(k_hi, u + 1)
        dve.tensor_tensor(k[b % 2][1][:, :], k_sum[:, :], k[b % 2][0][:, :].bitcast(F32), ALU.subtract).then_inc(k_lo, 1)

    def dve_q_cos(dve, u, b, p):
        dve.wait_ge(q_halves, u * 4 + 2 * p + 2)
        if (p or past(u, 1)):
            dve.wait_ge(q_lo, u * 2 + p)
        dve.tensor_tensor(q_sum[:, :, :], heads(BM[1 + p]), over_pair(cos), ALU.mult).then_inc(q_cos, 1)

    def dve_q_add(dve, u, b, p):
        dve.wait_ge(q_sin, u * 2 + p + 1)
        dve.wait_ge(q_cos, u * 2 + p + 1)
        dve.tensor_tensor(q_sum[:, :, :], q_sum[:, :, :], q_rot[:, :, :], ALU.add).then_inc(q_added, 1)

    def dve_q_lo(dve, u, b, p):
        dve.wait_ge(q_hi, u * 2 + p + 1)
        dve.tensor_tensor(q[b % 2][1][:, 2 * p:2 * p + 2, :], q_sum[:, :, :],
                          q[b % 2][0][:, 2 * p:2 * p + 2, :].bitcast(F32), ALU.subtract).then_inc(q_lo, 1)

    def dve_v_lo(dve, u, b):
        dve.wait_ge(v_hi, u + 1)
        dve.tensor_tensor(v[b % 2][1][:, :, :], ps[BM[0]][:, 0:TB].rearrange("p (t n) -> p t n", t=BT),
                          v[b % 2][0][:, :, :].bitcast(F32), ALU.subtract).then_inc(v_lo, 1)

    def dve_mask(dve, u, b, h):
        dve.wait_ge(s_done, u * HG + h + 1)
        if past(u, 1):
            dve.wait_ge(pT_done, (u - 1) * HG + h + 1)
        stand_apart(dve)
        for qb, (c0, c1) in enumerate(((0, P), (P, SW))):
            dve.tensor_tensor_reduce(prob[:, h, c0:c1], ps[BS[h % 2]][:, c0:c1], causal[:, 2 * P - (c1 - c0):2 * P],
                                     -SC1, 3e38, ALU.add, ALU.min, neg_max[:, h, qb:qb + 1]).then_inc(masked, 1)

    def dve_inverse(dve, u, b, p):
        dve.wait_ge(exp_done, u * 8 + 4 * p + 4)
        if past(u, 1):
            dve.wait_ge(normed, (u - 1) * 8 + 4 * p + 4)
        stand_apart(dve)
        dve.reciprocal(row_inv[:, 2 * p:2 * p + 2, :], row_sum[:, 2 * p:2 * p + 2, :]).then_inc(inv_done, 1)

    def dve_pT(dve, u, b, h):
        dve.wait_ge(pT_hi, u * HG + h + 1)
        dve.tensor_tensor(pT[1][:, h, :], ps[BP[h % 2]][:, 0:SW], pT[0][:, h, :].bitcast(F32), ALU.subtract).then_inc(pT_lo, 1)

    def dve_o(dve, u, b, p):
        dve.wait_ge(o_hi, u * 2 + p + 1)
        dve.tensor_tensor(oT[1][:, 2 * p:2 * p + 2, :], heads(BO), oT[0][:, 2 * p:2 * p + 2, :].bitcast(F32),
                          ALU.subtract).then_inc(o_lo, 1)

    def dve_add(dve, u, b, t):
        dve.wait_ge(wo_done, u * 2 + t + 1)
        row = acc[:, b * BT + t, :]
        dve.tensor_tensor(row, row, ps[BM[1 + t]][:, :], ALU.add).then_inc(added, 1)

    def finish_moments(dve, b):
        dve.wait_ge(added, ((NG - 1) * NB + b + 1) * 2)
        stream.post_moments(dve, 0, b)

    def vector(dve):
        dve.wait_ge(tables_in, 48)
        dve.wait_ge(acc_zero, 1)
        dve_kvw(dve, 0)
        dve_k_cos(dve, 0, 0)
        dve_k_add(dve, 0, 0)
        dve_k_lo(dve, 0, 0)
        for p in range(2):
            dve_q_cos(dve, 0, 0, p)
            dve_q_add(dve, 0, 0, p)
            dve_q_lo(dve, 0, 0, p)
        dve_v_lo(dve, 0, 0)

        def step(g, b, before, after):
            u, nb, pb = g * NB + b, (b + 1) % NB, (b - 1) % NB
            done = finishing(g, b)
            if done is not None:
                finish_moments(dve, done)
            dve_mask(dve, u, b, 0)
            dve_mask(dve, u, b, 1)
            if done is not None:
                stream.post_apply(dve, 0, done)
                stream.add(dve, 0, done)
            if before:
                dve_o(dve, u - 1, pb, 1)
            if after:
                dve_k_cos(dve, u + 1, nb)
            dve_inverse(dve, u, b, 0)
            dve_mask(dve, u, b, 2)
            dve_mask(dve, u, b, 3)
            if after:
                dve_k_add(dve, u + 1, nb)
                dve_k_lo(dve, u + 1, nb)
            dve_inverse(dve, u, b, 1)
            if done is not None:
                stream.pre_moments(dve, 1, done)
            if after:
                dve_q_cos(dve, u + 1, nb, 0)
            dve_pT(dve, u, b, 0)
            dve_pT(dve, u, b, 1)
            if after:
                dve_q_add(dve, u + 1, nb, 0)
                dve_q_lo(dve, u + 1, nb, 0)
                dve_q_cos(dve, u + 1, nb, 1)
                dve_q_add(dve, u + 1, nb, 1)
            if before:
                dve_add(dve, u - 1, pb, 0)
            if after:
                dve_q_lo(dve, u + 1, nb, 1)
                dve_v_lo(dve, u + 1, nb)
            if done is not None:
                stream.pre_apply(dve, 1, done)
            dve_pT(dve, u, b, 2)
            dve_pT(dve, u, b, 3)
            if before:
                dve_add(dve, u - 1, pb, 1)
            if done is not None:
                stream.lo(dve, 1, done * BT, BM[0])
            dve_o(dve, u, b, 0)
            if done is not None:
                stream.lo(dve, 1, done * BT + 1, BM[0])
            if b == 2 and not (isinstance(g, int) and g == NG - 1):
                dve_kvw(dve, g + 1)

        over_groups(dve, step)
        b = NB - 2
        finish_moments(dve, b)
        dve_o(dve, U - 1, NB - 1, 1)
        stream.post_apply(dve, 0, b)
        stream.add(dve, 0, b)
        dve_add(dve, U - 1, NB - 1, 0)
        stream.pre_moments(dve, 1, b)
        dve_add(dve, U - 1, NB - 1, 1)
        finish_moments(dve, b + 1)
        stream.pre_apply(dve, 1, b)
        stream.post_apply(dve, 0, b + 1)
        stream.add(dve, 0, b + 1)
        stream.pre_moments(dve, 1, b + 1)
        stream.pre_apply(dve, 1, b + 1)

    def pool_qw(pl, g):
        pl.wait_ge(qw_hi, g + 1)
        pl.tensor_tensor(w[1][:, :, QC:GW], w_raw[:, :, QC:GW], w[0][:, :, QC:GW].bitcast(F32), ALU.subtract).then_inc(qw_lo, 1)

    def pool_wo(pl, g):
        pl.wait_ge(wo_hi, g + 1)
        pl.tensor_tensor(wo[1][:, :, :], wo_raw[:, :, :], wo[0][:, :, :].bitcast(F32), ALU.subtract).then_inc(wo_lo, 1)

    def pool_k(pl, u, b):
        pl.wait_ge(k_halves, u * 2 + 2)
        pl.tensor_tensor(k_rot[:, :], k_rot[:, :], sin[:, :], ALU.mult).then_inc(k_sin, 1)

    def pool_q(pl, u, b, p):
        pl.wait_ge(q_halves, u * 4 + 2 * p + 2)
        pl.tensor_tensor(q_rot[:, :, :], q_rot[:, :, :], over_pair(sin), ALU.mult).then_inc(q_sin, 1)

    def pool_norm(pl, u, b, p):
        pl.wait_ge(inv_done, u * 2 + p + 1)
        stand_apart(pl)
        for h in (2 * p, 2 * p + 1):
            for qb, (c0, c1) in enumerate(((0, P), (P, SW))):
                pl.tensor_scalar(prob[:, h, c0:c1], prob[:, h, c0:c1], row_inv[:, h, qb:qb + 1], 1.0, ALU.mult, ALU.mult)\
                  .then_inc(normed, 1)

    def pool(pl, next_weights):
        pl.memset(acc[:, :, :], 0.0).then_inc(acc_zero, 1)
        pl.wait_ge(tables_in, 48)
        pool_qw(pl, 0)
        pool_k(pl, 0, 0)
        pool_q(pl, 0, 0, 0)
        pool_q(pl, 0, 0, 1)
        pool_wo(pl, 0)

        def step(g, b, before, after):
            u, nb, pb = g * NB + b, (b + 1) % NB, (b - 1) % NB
            if b == 1 and past(g, 1):
                pool_wo(pl, g)
            done = finishing(g, b)
            if done is not None:
                stream.post.inverse(pl, done, stream.minus_half)
            if after:
                pool_k(pl, u + 1, nb)
            pool_norm(pl, u, b, 0)
            if after:
                pool_q(pl, u + 1, nb, 0)
            pool_norm(pl, u, b, 1)
            if done is not None:
                stream.pre.inverse(pl, NB + done, stream.minus_half)
            if after:
                pool_q(pl, u + 1, nb, 1)
            if b == 2 and not (isinstance(g, int) and g == NG - 1):
                pool_qw(pl, g + 1)

        over_groups(pl, step)
        next_weights(pl)
        for b in (NB - 2, NB - 1):
            stream.post.inverse(pl, b, stream.minus_half)
            stream.pre.inverse(pl, NB + b, stream.minus_half)

    ctx.close()
    return {"sync": sync, "pool": pool, "scalar": scalar, "vector": vector, "tensor": tensor,
            "weights_over": (q_done, U * 2)}


def swiglu(nc, dram, stream, XT, acc, ps, room):
    ctx = ExitStack()
    sb = lambda name, shape, dt: ctx.enter_context(nc.sbuf_tensor(name, shape, dt))
    sem = lambda name: nc.semaphore(name).__enter__()
    GU, W = KD * 2 * P, KD * 2 * P + D
    C = 2
    TC = NT // C * P

    raw = [sb(f"ffn_raw{n}", [P, W], F32) for n in range(2)]
    w = [[sb(f"ffn_w{n}_{x}", [P, W], F32R) for x in ("hi", "lo")] for n in range(2)]
    act_gate = sb("act_gate", [P, C, TC], F32)
    h32 = sb("h32", [P, C, TC], F32)
    h = [[sb(f"h{n}_{x}", [P, C, TC], F32R) for x in ("hi", "lo")] for n in range(2)]

    raw_in = [sem(f"ffn_raw_in{n}") for n in range(2)]
    gu_hi, gu_lo, dw_hi, dw_lo = (sem(n) for n in ("gu_hi", "gu_lo", "dw_hi", "dw_lo"))
    gate_done, up_done, gate_out, h_done, h_hi, h_lo = (sem("ffn_" + n) for n in ("gate_done", "up_done", "gate_out", "h_done", "h_hi", "h_lo"))
    down_done, down_added = sem("down_done"), sem("down_added")

    def over_tiles(engine, step):
        for f in range(3):
            step(f, f % 2)
        with engine.Fori(1, (FT - 1) // 2) as i:
            step(2 * i + 1, 1)
            step(2 * i + 2, 0)

    def sync(sp):
        sp.wait_ge(*room)
        for f in range(2):
            sp.dma_start(raw[f][:, :], dram["ffn_w"][f]).then_inc(raw_in[f], 16)
        with sp.Fori(1, (FT - 1) // 2) as i:
            for n in range(2):
                sp.wait_ge(dw_lo, 2 * i + n - 1)
                sp.dma_start(raw[n][:, :], dram["ffn_w"][2 * i + n]).then_inc(raw_in[n], 16)
        sp.wait_ge(dw_lo, FT - 2)
        sp.dma_start(raw[(FT - 1) % 2][:, :], dram["ffn_w"][FT - 1]).then_inc(raw_in[(FT - 1) % 2], 16)

    def tensor(pe):
        def step(f, n):
            pe.wait_ge(gu_lo, f + 1)
            for c in range(C):
                if isinstance(f, int) and f == 0:
                    if c == 1:
                        for t in range(NT // C, NT):
                            stream.turn(pe, 1, t, t)
                    pe.wait_ge(stream.lo_out, NT + (c + 1) * (NT // C))
                for up, done in ((0, gate_done), (1, up_done)):
                    if past(f, 1):
                        pe.wait_ge(h_done, (f - 1) * C + c + 1)
                    for k in range(KD):
                        cols = slice(k * 2 * P + up * P, k * 2 * P + up * P + P)
                        xs = slice(c * TC, (c + 1) * TC)
                        last = split_product(pe, ps[2 * c + up][:, :], (w[n][0][:, cols], w[n][1][:, cols]),
                                             (XT[0][:, k, xs], XT[1][:, k, xs]), k == 0, k == KD - 1)
                    last.then_inc(done, 1)
            if past(f, 1):
                down(f - 1, 1 - n)

        def down(f, n):
            pe.wait_ge(dw_lo, f + 1)
            for t in range(NT):
                c, ts = t // (NT // C), slice(t % (NT // C) * P, (t % (NT // C) + 1) * P)
                if t % (NT // C) == 0:
                    pe.wait_ge(h_lo, f * C + c + 1)
                if t >= 4 or past(f, 1):
                    pe.wait_ge(down_added, f * NT + t - 3)
                last = split_product(pe, ps[4 + t % 4][:, :], (h[n][0][:, c, ts], h[n][1][:, c, ts]),
                                     (w[n][0][:, GU:W], w[n][1][:, GU:W]), True, True)
                last.then_inc(down_done, 1)

        over_tiles(pe, step)
        down(FT - 1, (FT - 1) % 2)

    def scalar(act):
        def step(f, n):
            for c in range(C):
                act.wait_ge(gate_done, f * C + c + 1)
                if past(f, 1):
                    act.wait_ge(h_done, (f - 1) * C + c + 1)
                act.activation(act_gate[:, c, :], ps[2 * c][:, :], ACT.Silu).then_inc(gate_out, 1)
                if c == 0 and isinstance(f, int) and f == 0:
                    for t in range(NT // C, NT):
                        stream.hi(act, 1, t, t)
            for c in range(C):
                act.wait_ge(h_done, f * C + c + 1)
                act.activation(h[n][0][:, c, :], h32[:, c, :], ACT.Copy).then_inc(h_hi, 1)

        over_tiles(act, step)

    def vector(dve):
        def step(f, n):
            for c in range(C):
                dve.wait_ge(gate_out, f * C + c + 1)
                dve.wait_ge(up_done, f * C + c + 1)
                if past(f, 1):
                    dve.wait_ge(h_lo, (f - 1) * C + c + 1)
                dve.tensor_tensor(h32[:, c, :], ps[2 * c + 1][:, :], act_gate[:, c, :], ALU.mult).then_inc(h_done, 1)
                if c == 0 and isinstance(f, int) and f == 0:
                    for t in range(NT // C, NT):
                        stream.lo(dve, 1, t, t)
            if past(f, 1):
                add(f - 1)

        def add(f):
            for t in range(NT):
                dve.wait_ge(down_done, f * NT + t + 1)
                if past(f, 1):
                    dve.wait_ge(down_added, (f - 1) * NT + t + 1)
                    dve.tensor_tensor(acc[:, t, :], acc[:, t, :], ps[4 + t % 4][:, :], ALU.add).then_inc(down_added, 1)
                else:
                    dve.tensor_copy(acc[:, t, :], ps[4 + t % 4][:, :]).then_inc(down_added, 1)
                if isinstance(f, int) and f == FT - 1 and t % BT == BT - 1:
                    dve.wait_ge(down_added, f * NT + t + 1)
                    b = t // BT
                    stream.post_moments(dve, 1, b)
                    if b:
                        stream.post_apply(dve, 1, b - 1)
            if isinstance(f, int) and f == FT - 1:
                stream.post_apply(dve, 1, NB - 1)

        over_tiles(dve, step)
        add(FT - 1)

    def split(pl, f, n, cols, hi, lo, used, count):
        if past(f, 2):
            pl.wait_ge(used, (f - 1) * count)
        stand_apart(pl)
        pl.tensor_scalar(w[n][0][:, cols], raw[n][:, cols], 1.0, 1.0, ALU.mult, ALU.mult).then_inc(hi, 1)
        pl.wait_ge(hi, f + 1)
        pl.tensor_tensor(w[n][1][:, cols], raw[n][:, cols], w[n][0][:, cols].bitcast(F32), ALU.subtract).then_inc(lo, 1)

    def split_gate_up(pl, f, n):
        pl.wait_ge(raw_in[n], (f - n) * 8 + 16)
        split(pl, f, n, slice(0, GU), gu_hi, gu_lo, up_done, C)

    def split_down(pl, f, n):
        split(pl, f, n, slice(GU, W), dw_hi, dw_lo, down_done, NT)

    def first_weights(pl):
        split_gate_up(pl, 0, 0)

    def pool(pl):
        def step(f, n, ahead=True):
            for c in range(C):
                pl.wait_ge(h_hi, f * C + c + 1)
                pl.tensor_tensor(h[n][1][:, c, :], h32[:, c, :], h[n][0][:, c, :].bitcast(F32), ALU.subtract).then_inc(h_lo, 1)
            if ahead:
                split_down(pl, f + 1, 1 - n)
                split_gate_up(pl, f + 2, n)

        split_down(pl, 0, 0)
        split_gate_up(pl, 1, 1)
        for f in range(2):
            step(f, f)
        with pl.Fori(1, (FT - 3) // 2) as i:
            step(2 * i, 0)
            step(2 * i + 1, 1)
        step(FT - 3, (FT - 3) % 2)
        step(FT - 2, (FT - 2) % 2, False)
        split_down(pl, FT - 1, (FT - 1) % 2)
        step(FT - 1, (FT - 1) % 2, False)
        for b in range(NB + 1):
            if b < NB:
                stream.post.inverse(pl, NB + b, stream.minus_half)
            if b:
                stream.add(pl, 1, b - 1)

    ctx.close()
    return {"sync": sync, "first_weights": first_weights, "pool": pool, "scalar": scalar, "vector": vector,
            "tensor": tensor}


def host_layout(inp):
    c = np.ascontiguousarray
    wkv = np.asarray(inp["L0_attn_Wkv"])
    wk, wv = wkv[:, :HD0], wkv[:, HD0:]
    a = {
        "x": c(np.asarray(inp["L0_attn_hidden_states"]).reshape(NB * TB, D)),
        "wq0": c(inp["L0_attn_Wq"]),
        "wkv0": c(np.concatenate([np.tile(wk, (1, HPT)), wv], 1).reshape(KD, P, P + HD0).transpose(1, 0, 2)),
        "wo0": c(inp["L0_attn_Wo"]),
        "wf0": c(np.asarray(inp["L0_ffn_W"]).T),
        "bias0": c(inp["L0_ffn_bias"]),
        "a0": c(np.asarray(inp["L0_ffn_A"]).reshape(NEXP * RANK, D)),
        "bf0": c(np.asarray(inp["L0_ffn_Bf"]).transpose(0, 2, 1).reshape(NEXP * RANK, D)),
        "gate_w": c(np.stack([np.repeat(np.asarray(inp[n]), RANK).reshape(ER, P).T
                              for n in ("L0_ffn_coeffs", "L0_ffn_scales")], 1)),
    }
    columns = np.concatenate([np.asarray(inp["L1_attn_W" + n]).reshape(NG, -1, D) for n in "kvq"], 1)
    a["w1"] = c(columns.reshape(NG, GW, KD, P).transpose(0, 3, 2, 1))
    a["wo1"] = c(np.asarray(inp["L1_attn_Wo"]).T.reshape(NG, HG, P, D).transpose(0, 2, 1, 3))
    pad = ((0, FT * P - F), (0, 0))
    gate, up = (np.pad(np.asarray(inp["L1_ffn_W_" + n]), pad).reshape(FT, P, KD, P).transpose(0, 3, 2, 1)
                for n in ("gate", "up"))
    down = np.pad(np.asarray(inp["L1_ffn_W_down"]).T, pad).reshape(FT, P, D)
    a["ffn_w"] = c(np.concatenate([np.concatenate([gate, up], 3).reshape(FT, P, KD * 2 * P), down], 2))
    return a


def build(nc, dram, out):
    with ExitStack() as ctx:
        sb = lambda name, shape, dt: ctx.enter_context(nc.sbuf_tensor(name, shape, dt))
        sem = lambda name: nc.semaphore(name).__enter__()
        X = sb("X", [P, NT, D], F32)
        ident = sb("ident_sb", [P, P], F32)
        minus_half = sb("minus_half", [P, NT], F32)
        ps = [ctx.enter_context(nc.psum_tensor(f"bank{i}", [P, 512], F32)) for i in range(8)]
        ident_in, half_set, out_done = (sem(n) for n in ("ident_in", "half_set", "out_done"))
        consts = {"ident": ident, "minus_half": minus_half, "in": ident_in}

        l0 = layer0(nc, dram, X, ps, consts)
        l0_over = (l0["done"], l0["done_count"])
        XT = [sb(f"XT_{x}", [P, KD, NB * TB], F32R) for x in ("hi", "lo")]
        acc = sb("acc", [P, NT, D], F32)
        stream = Stream(sb, sem, X, XT, acc, ps, ident, minus_half)
        attention = layer1_attention(nc, dram, stream, XT, acc, ps, consts, l0_over)
        ffn = swiglu(nc, dram, stream, XT, acc, ps, attention["weights_over"])

        block = ctx.enter_context(nc.Block())

        @block.sync
        def _(sp):
            sp.dma_start(ident[:, :], dram["ident"]).then_inc(ident_in, 16)
            l0["sync"](sp)
            attention["sync"](sp)
            ffn["sync"](sp)
            rows = out.rearrange("(n p) d -> p n d", p=P)
            for t in range(NT):
                sp.wait_ge(stream.summed, NT + t + 1)
                sp.dma_start(rows[:, t, :], X[:, t, :]).then_inc(out_done, 16)
            sp.wait_ge(out_done, NT * 16)

        @block.gpsimd
        def _(pl):
            pl.memset(minus_half[:, :], -0.5).then_inc(half_set, 1)
            pl.wait_ge(half_set, 1)
            l0["pool"](pl)
            pl.wait_ge(*l0_over)
            for b in range(NB):
                stream.pre.inverse(pl, b, minus_half)
            attention["pool"](pl, ffn["first_weights"])
            ffn["pool"](pl)

        @block.scalar
        def _(act):
            l0["scalar"](act)
            for t in range(NT):
                stream.hi(act, 0, t, t)
            attention["scalar"](act)
            ffn["scalar"](act)

        @block.vector
        def _(dve):
            l0["vector"](dve)
            dve.wait_ge(*l0_over)
            stream.pre_moments(dve, 0, 0)
            for b in range(NB + 1):
                if b + 1 < NB:
                    stream.pre_moments(dve, 0, b + 1)
                if b < NB:
                    stream.pre_apply(dve, 0, b)
                if b:
                    for t in range((b - 1) * BT, b * BT):
                        stream.lo(dve, 0, t, t)
            attention["vector"](dve)
            ffn["vector"](dve)

        @block.tensor
        def _(pe):
            l0["tensor"](pe)
            for t in range(NT):
                stream.turn(pe, 0, t, t)
            attention["tensor"](pe)
            ffn["tensor"](pe)


def kernel(**inputs):
    import concourse.bacc as bacc
    from concourse.bass_utils import run_bass_kernel_spmd

    nc = bacc.Bacc("TRN2", target_bir_lowering=False, num_devices=1)
    arrays = {**host_layout(inputs), **constants()}
    dram = {name: nc.dram_tensor(f"in_{name}_dram", a.shape, mybir.dt.from_np(a.dtype), kind="ExternalInput").ap()
            for name, a in arrays.items()}
    out = nc.dram_tensor("out_dram", [NB * TB, D], F32, kind="ExternalOutput").ap()
    build(nc, dram, out)
    result = run_bass_kernel_spmd(nc, [{f"in_{name}_dram": a for name, a in arrays.items()}], core_ids=[0])
    return result.results[0]["out_dram"].reshape(NB, TB, D)
```

```python
from contextlib import ExitStack

import numpy as np

import concourse.bass as bass
from concourse import mybir

F32 = mybir.dt.float32
F32R = mybir.dt.float32r
F16 = mybir.dt.float16
BF16 = mybir.dt.bfloat16
ALU = mybir.AluOpType
ACT = mybir.ActivationFunctionType

P = 128
NB, TB = 4, 256
BT = TB // P
NT = NB * BT
D = 512
KD = D // P
EPS = 1e-5
MASKED = -1e32

H0, HD0 = 32, 16
HPT = P // HD0
SC0 = HD0 ** -0.5
SLOTS = 4
PROB_SCALE = 2.0 ** 15
NEXP, RANK = 16, 16
ER = NEXP * RANK // P

NG, HG, HD1 = 8, 4, 128
SC1 = HD1 ** -0.5
QW = HG * HD1
GW = QW + 2 * HD1

F = 1376
FT = (F + P - 1) // P

SW = P + 2 * P


def alibi_slopes(n):
    start = 2.0 ** (-2.0 ** (-(np.log2(n) - 3)))
    return np.array([start ** (i + 1) for i in range(n)], dtype=np.float32)


def rope_tables():
    theta, factor, high, low, orig = 500000.0, 8.0, 4.0, 1.0, 1024
    inv = 1.0 / theta ** (np.arange(0, HD1, 2, dtype=np.float32) / HD1)
    wavelen = 2.0 * np.pi / inv
    scaled = np.where(wavelen > orig / low, inv / factor, inv)
    smooth = (orig / wavelen - low) / (high - low)
    smoothed = (1.0 - smooth) / factor * inv + smooth * inv
    medium = (wavelen <= orig / low) & (wavelen >= orig / high)
    inv = np.where(medium, smoothed, scaled).astype(np.float32)
    freqs = (np.arange(TB, dtype=np.float32)[None, :] * inv[:, None]).astype(np.float32)
    cos, sin = np.cos(freqs), np.sin(freqs)
    return (np.concatenate([cos, cos]).astype(np.float32),
            np.concatenate([-sin, sin]).astype(np.float32))


def constants():
    q, c = np.arange(P)[:, None], np.arange(2 * P)[None, :]
    hidden = np.where(c - P > q, np.float32(MASKED), np.float32(0))
    cos, sin = rope_tables()
    return {
        "ident": np.eye(P, dtype=np.float32),
        "causal": hidden.astype(np.float32),
        "distance": (c - (2 * P - 1) + hidden).astype(np.float32),
        "slot_rows": (np.arange(P)[:, None] // HD0 % 2 == np.arange(2)[None, :]).astype(np.float32),
        "cos": cos, "sin": sin,
    }


def stand_apart(engine):
    engine.nop(nofuse=True)


class Norm:

    def __init__(self, name, sb, sem):
        self.six = sb(f"{name}_six", [P, BT, 6], F32)
        self.mv = sb(f"{name}_mv", [P, BT, 2], F32)
        self.var_eps = sb(f"{name}_var_eps", [P, BT], F32)
        self.rstd = sb(f"{name}_rstd", [P, BT], F32)
        self.stats_done = sem(f"{name}_stats_done")
        self.moments_done = sem(f"{name}_moments_done")
        self.var_ready = sem(f"{name}_var_ready")
        self.rstd_ready = sem(f"{name}_rstd_ready")
        self.normed = sem(f"{name}_normed")

    def moments(self, dve, b, source, apart=False):
        for t in range(BT):
            if apart and t == 0:
                stand_apart(dve)
            dve.bn_stats(self.six[:, t, :], source(t)).then_inc(self.stats_done, 1)
        dve.wait_ge(self.stats_done, b * BT + BT)
        stand_apart(dve)
        for t in range(BT):
            dve.bn_aggr(self.mv[:, t, :], self.six[:, t, :]).then_inc(self.moments_done, 1)
        dve.wait_ge(self.moments_done, b * BT + BT)
        dve.tensor_scalar(self.var_eps[:, :], self.mv[:, :, 1], EPS, None, ALU.add)\
           .then_inc(self.var_ready, 1)

    def inverse(self, pool, b, minus_half):
        pool.wait_ge(self.var_ready, b + 1)
        pool.tensor_tensor(self.rstd[:, :], self.var_eps[:, :], minus_half, ALU.pow)\
            .then_inc(self.rstd_ready, 1)

    def apply(self, dve, b, source, target):
        dve.wait_ge(self.rstd_ready, b + 1)
        for t in range(BT):
            dve.tensor_scalar(target(t), source(t), self.mv[:, t, 0:1], self.rstd[:, t:t + 1],
                              ALU.subtract, ALU.mult).then_inc(self.normed, 1)


def split_product(pe, out, left, right, first, last):
    (lh, ll), (rh, rl) = left, right
    pe.matmul(out, lh, rh, start=first, stop=False)
    pe.matmul(out, lh, rl, start=False, stop=False)
    return pe.matmul(out, ll, rh, start=False, stop=last)


def layer0(nc, dram, keep, X, ps, consts):
    ident, minus_half, consts_in = consts["ident"], consts["minus_half"], consts["in"]
    ctx = ExitStack()
    sb = lambda name, shape, dt: ctx.enter_context(nc.sbuf_tensor(name, shape, dt))
    sem = lambda name: nc.semaphore(name).__enter__()
    sems = lambda names: [sem(name) for name in names.split()]
    pair = lambda name, shape: [sb(f"{name}_{x}", shape, F32R) for x in ("hi", "lo")]

    tok = keep("tok0", [P, BT, D], F32)
    delta = keep("delta0", [P, BT, D], F32)
    bias_b = keep("bias_b", [P, D], F32)
    ln1, ln2, ln3, ln4 = (Norm(f"ln{n}", keep, sem) for n in (1, 2, 3, 4))

    def weight(name, shape):
        hi = sb(f"{name}_hi", shape, F32R)
        with nc.sbuf_tensor(f"{name}_raw", shape, F32) as raw:
            pass
        return raw, (hi, sb(f"{name}_lo", shape, F32R))

    wo_raw, wo = weight("wo0", [P, KD, D])
    wf_raw, wf = weight("wf0", [P, KD, D])
    fT = pair("fT0", [P, KD, TB])
    a_raw = sb("a_raw", [P, ER, D], F32)
    bf_raw = sb("bf_raw", [P, ER, D], F32)
    wq_raw, wq = weight("wq0", [P, KD, D])
    wkv_raw, wkv = weight("wkv0", [P, KD, P + HD0])
    gate_w = sb("gate_w", [P, 2, ER], F32)
    gate_p = sb("gate_p", [P, ER], F32)
    distance = sb("distance", [P, 2 * P], F32)
    slot_rows = sb("slot_rows", [P, 2], F32)
    alibi = sb("alibi", [P, H0, 2 * P], F32)
    x_tok = sb("x_tok0", [P, BT, D], F32)
    xT = pair("xT0", [P, KD, TB])
    q_slots = sb("q_slots", [P, BT, H0, SLOTS, HD0], F32R)
    qT = sb("qT0", [P, H0 // 2, TB], F32R)
    k_rows = pair("k_rows", [P, TB])
    kT_half = sb("kT_half", [P, TB], F32)
    kT = sb("kT0", [P, TB], F32R)
    vT = sb("vT0", [HD0, TB], F32)
    v = sb("v0", [P, BT, HD0], F32)
    v_rest = sb("v_rest0", [P, 2, BT, HD0], F32)
    v_next = sb("v_next0", [P, 3, BT, HD0], BF16)
    v_parts = sb("v_parts0", [P, 3, BT, HD0], BF16)
    prob = sb("prob0", [P, 4, SW], F32)
    neg_max = sb("neg_max0", [P, 4, 2], F32)
    row_sum = sb("row_sum0", [P, H0, 2], F32)
    row_inv = sb("row_inv0", [P, H0, 2], F32)
    probT = [sb(f"probT0_{x}", [P, 4, SW], F16) for x in ("hi", "lo")]


    x_in = [sem(f"x_in{b}") for b in range(NB)]
    wq_in, kv_in, wo_in, wf_in, small_in = sems("wq_in kv_in wo_in wf_in small_in")
    wq_hi, wq_lo, wkv_hi, wkv_lo = sems("wq_hi wq_lo wkv_hi wkv_lo")
    wo_hi, wo_lo, wf_hi, wf_lo = sems("wo_hi wo_lo wf_hi wf_lo")
    gate_done, bf_scaled, adapters_done, w_eff_done = sems("gate_done bf_scaled adapters_done w_eff_done")
    alibi_done = sem("alibi_done")
    xT_done, xT_hi, xT_lo = sems("xT_done0 xT_hi0 xT_lo0")
    kv_done, k_hi, k_lo, vT_out, v_turned, v_out = sems("kv_done0 k_hi0 k_lo0 vT_out0 v_turned0 v_out0")
    kT_halved, kT_out, v_split, v_copied = sems("kT_halved0 kT_out0 v_split0 v_copied0")
    q_done, q_hi, q_lo = sems("q_done0 q_hi0 q_lo0")
    qT_done, qT_act, qT_dve = sems("qT_done0 qT_act0 qT_dve0")
    s_done, masked, exp_done, pT_done, pT_hi, pv_done, pT_lo = sems("s_done0 masked0 exp_done0 pT_done0 pT_hi0 pv_done0 pT_lo0")
    inv_done, o_out, oT_done, oT_hi, oT_lo = sems("inv_done0 o_out0 oT_done0 oT_hi0 oT_lo0")
    wo_done, x1_done, x1T_done, x1T_hi, x1T_lo = sems("wo_done0 x1_done0 x1T_done0 x1T_hi0 x1T_lo0")
    ffn_done, biased, x2_done = sems("ffn_done0 biased0 x2_done0")

    slopes = alibi_slopes(H0)

    LAG_T, LAG_HI, LAG_LO, LAG_V = 2, 3, 3, 4
    QG = H0 // 4
    AT = {"out": LAG_V - 1, "oT": LAG_V, "oT_out": LAG_V + 1, "wo": LAG_V + 2, "n2": LAG_V + 6, "a2": 11, "x1": 12, "n3": 13,
          "a3": 14, "x1T": 16, "x1T_out": 17, "ffn": 20, "bias": (22, 24), "n4": 24, "a4": 26, "x2": 29,
          "n1": 7, "a1": 8, "xT": 14, "xT_out": 15, "kv": 18, "kv_out": 20, "v": 21, "q0": 24, "q0_out": 26, "q1": 26, "q1_out": 28,
          "qT": (29, 30, 31, 0), "qT_out": (30, 31, 0, 1)}
    FIRST_QT, FIRST_QT_OUT = (None, 0, 1, 2), (None, 1, 2, 3)
    CHUNKS = 4
    MERGE = (5, 7, 9, 11)

    def q_bank(t):
        return ps[6 + t][:, :].rearrange("p (h a d) -> p h a d", h=H0, a=1).to_broadcast([P, H0, 2, HD0])

    def turned(bank):
        return ps[bank][:, :].rearrange("p (k n) -> p k n", k=KD)

    def xrow(b, t):
        return X[:, b * BT + t, :]

    def sync(sp):
        tiled = lambda name: dram[name].rearrange("(k p) n -> p k n", p=P)
        for b in range(NB):
            sp.dma_start(X[:, b * BT:(b + 1) * BT, :], dram["x"].rearrange("(n p) d -> p n d", p=P)[:, b * BT:(b + 1) * BT, :])\
              .then_inc(x_in[b], 16)
            if b == 0:
                sp.dma_start(wkv_raw[:, :, :], dram["wkv0"]).then_inc(kv_in, 16)
                sp.dma_start(wq_raw[:, :, :], tiled("wq0")).then_inc(wq_in, 16)
        sp.dma_start(wf_raw[:, :, :], tiled("wf0")).then_inc(wf_in, 16)
        sp.dma_start(a_raw[:, :, :], tiled("a0")).then_inc(wf_in, 16)
        sp.dma_start(bf_raw[:, :, :], tiled("bf0")).then_inc(wf_in, 16)
        sp.dma_start(wo_raw[:, :, :], tiled("wo0")).then_inc(wo_in, 16)

    def sync_consts(act):
        act.dma_start(distance[:, :], dram["distance"]).then_inc(small_in, 16)
        act.dma_start(slot_rows[:, :], dram["slot_rows"]).then_inc(small_in, 16)
        act.dma_start(gate_w[:, :, :], dram["gate_w"]).then_inc(small_in, 16)
        act.dma_start(bias_b[:, :], dram["bias0"].partition_broadcast(P)).then_inc(small_in, 16)

    def split_in_place(pl, raw, parts, hi_done, lo_done):
        pl.tensor_scalar(parts[0][:, :, :], raw[:, :, :], 1.0, 1.0, ALU.mult, ALU.mult).then_inc(hi_done, 1)
        pl.wait_ge(hi_done, 1)
        pl.tensor_tensor(parts[1][:, :, :], raw[:, :, :], parts[0][:, :, :].bitcast(F32), ALU.subtract)\
          .then_inc(lo_done, 1)

    def pool(pl):
        ln1.inverse(pl, 0, minus_half[:, 0:BT])
        pl.wait_ge(small_in, 64)
        for h in range(H0):
            pl.tensor_scalar(alibi[:, h, :], distance[:, :], float(slopes[h]) / SC0, 1.0, ALU.mult, ALU.mult)\
              .then_inc(alibi_done, 1)
        split_v(pl, 0)
        copy_v(pl, 0)
        ln1.inverse(pl, 1, minus_half[:, 0:BT])
        pl.wait_ge(wo_in, 16)
        split_in_place(pl, wo_raw, wo, wo_hi, wo_lo)
        pl.wait_ge(w_eff_done, KD)
        split_in_place(pl, wf_raw, wf, wf_hi, wf_lo)
        split_v(pl, 1)
        with pl.Fori(1, NB - 1) as b:
            pool_batch(pl, b, True)
        pool_batch(pl, NB - 1, False)

    def split_v(pl, b):
        pl.wait_ge(v_out, b + 1)
        if past(b, 1):
            pl.wait_ge(v_copied, b)
        stand_apart(pl)
        pl.tensor_copy(v_next[:, 0, :, :], v[:, :, :]).then_inc(v_split, 1)
        for n, (left, rest) in enumerate(((v[:, :, :], v_rest[:, 0, :, :]), (v_rest[:, 0, :, :], v_rest[:, 1, :, :]))):
            pl.wait_ge(v_split, b * 5 + 2 * n + 1)
            pl.tensor_tensor(rest, left, v_next[:, n, :, :], ALU.subtract).then_inc(v_split, 1)
            pl.wait_ge(v_split, b * 5 + 2 * n + 2)
            stand_apart(pl)
            pl.tensor_copy(v_next[:, n + 1, :, :], rest).then_inc(v_split, 1)

    def copy_v(pl, b):
        if past(b, 1):
            pl.wait_ge(pv_done, b * H0)
        pl.wait_ge(v_split, b * 5 + 5)
        stand_apart(pl)
        pl.tensor_copy(v_parts[:, :, :, :], v_next[:, :, :, :]).then_inc(v_copied, 1)

    def pool_batch(pl, b, prologue):
        copy_v(pl, b)
        if prologue:
            ln1.inverse(pl, b + 1, minus_half[:, 0:BT])
        ln2.inverse(pl, b - 1, minus_half[:, 0:BT])
        ln3.inverse(pl, b - 1, minus_half[:, 0:BT])
        if prologue:
            split_v(pl, b + 1)
        ln4.inverse(pl, b - 1, minus_half[:, 0:BT])

    def scalar(act):
        sync_consts(act)
        act.wait_ge(kv_in, 16)
        act.activation(wkv[0][:, :, :], wkv_raw[:, :, :], ACT.Copy).then_inc(wkv_hi, 1)
        act.wait_ge(wq_in, 16)
        act.activation(wq[0][:, :, :], wq_raw[:, :, :], ACT.Copy).then_inc(wq_hi, 1)
        act_xT(act, 0)
        act_kv(act, 0)
        act_q(act, 0, 0)
        act_q(act, 0, 1)
        act_qT(act, 0, 0)
        act_batch(act, 0, False, True)
        with act.Fori(1, NB - 1) as b:
            act_batch(act, b, True, True)
        act_batch(act, NB - 1, True, False)
        for step in range(LAG_V):
            act_probT(act, NB, step)
        act_turned(act, NB - 1, oT_done, oT_hi)

    def act_xT(act, b):
        for t in range(BT):
            act.wait_ge(xT_done, b * BT + t + 1)
            act.activation(xT[0][:, :, t * P:(t + 1) * P], turned(6 + t), ACT.Copy).then_inc(xT_hi, 1)

    def act_kv(act, b):
        act.wait_ge(kv_done, b + 1)
        act.activation(vT[:, :], ps[7][0:HD0, TB:2 * TB], ACT.Copy).then_inc(vT_out, 1)
        act.activation(k_rows[0][:, :], ps[7][:, 0:TB], ACT.Copy).then_inc(k_hi, 1)

    def act_q(act, b, t):
        act.wait_ge(q_done, b * BT + t + 1)
        act.activation(q_slots[:, t, :, 0:2, :], q_bank(t), ACT.Copy).then_inc(q_hi, 1)

    def act_qT(act, b, j):
        n = 2 * j
        act.wait_ge(qT_done, b * QG + n + 1)
        if past(b, 1):
            act.wait_ge(s_done, (b - 1) * H0 + 4 * n + 4)
        act.activation(qT[:, 2 * n:2 * n + 2, :], ps[6][:, :].rearrange("p (k n) -> p k n", k=2), ACT.Copy)\
           .then_inc(qT_act, 1)

    def act_turned(act, b, done, hi):
        for t in range(BT):
            act.wait_ge(done, b * BT + t + 1)
            act.activation(fT[0][:, :, t * P:(t + 1) * P], turned(6 + t), ACT.Copy).then_inc(hi, 1)

    def act_probT(act, b, step):
        h = step - LAG_HI
        g = b * H0 + h
        if under_way(b, step, LAG_HI):
            act.wait_ge(pT_done, g + 1)
            if past(g, 4):
                act.wait_ge(pv_done, g - 3)
            act.activation(probT[0][:, h % 4, :], ps[2 + h % 2][:, 0:SW], ACT.Copy, scale=PROB_SCALE).then_inc(pT_hi, 1)

    def act_exp(act, b, step):
        h = step
        g = b * H0 + h
        act.wait_ge(masked, 2 * g + 2)
        if h % (H0 // 2) == 0 and past(b, 1):
            act.wait_ge(inv_done, (b - 1) * 2 + h // (H0 // 2) + 1)
        for qb, (c0, c1) in enumerate(((0, P), (P, SW))):
            act.activation(prob[:, h % 4, c0:c1], prob[:, h % 4, c0:c1], ACT.Exp,
                           bias=neg_max[:, h % 4, qb:qb + 1], scale=-1.0,
                           accum_out=row_sum[:, h, qb:qb + 1]).then_inc(exp_done, 1)

    def act_batch(act, b, tail, prologue):
        for step in range(H0):
            act_probT(act, b, step)
            if tail and step == AT["oT_out"]:
                act_turned(act, b - 1, oT_done, oT_hi)
            if tail and step == AT["x1T_out"]:
                act_turned(act, b - 1, x1T_done, x1T_hi)
            if prologue and step == AT["xT_out"]:
                act_xT(act, b + 1)
            if prologue and step == AT["kv_out"]:
                act_kv(act, b + 1)
            if prologue and step == AT["q0_out"]:
                act_q(act, b + 1, 0)
            if prologue and step == AT["q1_out"]:
                act_q(act, b + 1, 1)
            for j, at in enumerate(AT["qT_out"]):
                if step == at and (j < 2 and prologue or j >= 2 and tail):
                    act_qT(act, b if j >= 2 else b + 1, j)
                if not tail and step == FIRST_QT_OUT[j]:
                    act_qT(act, 0, j)
            act_exp(act, b, step)

    def lo_part(dve, hi, lo, source, ready, count, done):
        dve.wait_ge(ready, count)
        dve.tensor_tensor(lo, source, hi.bitcast(F32), ALU.subtract).then_inc(done, 1)

    def lo_in_place(dve, raw, parts, hi_done, lo_done):
        lo_part(dve, parts[0][:, :, :], parts[1][:, :, :], raw[:, :, :], hi_done, 1, lo_done)

    def vector(dve):
        dve.wait_ge(x_in[0], 16)
        ln1.moments(dve, 0, lambda t: xrow(0, t))
        lo_in_place(dve, wkv_raw, wkv, wkv_hi, wkv_lo)
        ln1.apply(dve, 0, lambda t: xrow(0, t), lambda t: x_tok[:, t, :])
        dve_xT(dve, 0)
        lo_in_place(dve, wq_raw, wq, wq_hi, wq_lo)
        dve.wait_ge(small_in, 64)
        dve_k(dve, 0)
        dve_v(dve, 0, 0)
        dve_q(dve, 0, 0)
        dve_q(dve, 0, 1)
        dve_qT(dve, 0, 0)
        for b in range(1, NB):
            dve.wait_ge(x_in[b], 16)
        dve_batch(dve, 0, False, True)
        with dve.Fori(1, NB - 1) as b:
            dve_batch(dve, b, True, True)
        dve_batch(dve, NB - 1, True, False)
        for step in range(LAG_V):
            dve_probT(dve, NB, step)
        dve_inverse(dve, NB - 1, 1)
        dve_out(dve, NB - 1)
        dve_fT(dve, NB - 1, oT_hi, oT_lo)

    def dve_n1(dve, b):
        ln1.moments(dve, b, lambda t: xrow(b, t), True)

    def dve_a1(dve, b):
        dve.wait_ge(xT_done, b * BT)
        ln1.apply(dve, b, lambda t: xrow(b, t), lambda t: x_tok[:, t, :])

    def dve_xT(dve, b):
        for t in range(BT):
            lo_part(dve, xT[0][:, :, t * P:(t + 1) * P], xT[1][:, :, t * P:(t + 1) * P], turned(6 + t),
                    xT_hi, b * BT + t + 1, xT_lo)

    def dve_k(dve, b):
        lo_part(dve, k_rows[0][:, :], k_rows[1][:, :], ps[7][:, 0:TB], k_hi, b + 1, k_lo)
        if past(b, 1):
            dve.wait_ge(kT_out, b)
        dve.tensor_scalar(kT_half[:, :], k_rows[0][:, :].bitcast(F32), slot_rows[:, 0:1], None, ALU.mult).then_inc(kT_halved, 1)

    def dve_v(dve, b, bank, scores=None):
        if scores is None:
            dve.wait_ge(v_turned, b + 1)
        else:
            dve.wait_ge(s_done, scores)
        if past(b, 1):
            dve.wait_ge(v_split, b * 5)
        beside = ps[bank][:, SW:SW + BT * HD0].rearrange("p (t n) -> p t n", t=BT)
        dve.tensor_scalar(v[:, :, :], beside, 1.0 / PROB_SCALE, None, ALU.mult)\
           .then_inc(v_out, 1)

    def dve_kT(dve, b):
        dve.wait_ge(kT_halved, b + 1)
        dve.wait_ge(k_lo, b + 1)
        if past(b, 1):
            dve.wait_ge(s_done, b * H0)
        dve.scalar_tensor_tensor(kT[:, :], k_rows[1][:, :].bitcast(F32), slot_rows[:, 1:2], kT_half[:, :],
                                 ALU.mult, ALU.add).then_inc(kT_out, 1)

    def dve_q(dve, b, t):
        lo_part(dve, q_slots[:, t, :, 0:2, :], q_slots[:, t, :, 2:4, :], q_bank(t), q_hi, b * BT + t + 1, q_lo)

    def dve_qT(dve, b, j):
        n = 2 * j + 1
        dve.wait_ge(qT_done, b * QG + n + 1)
        if past(b, 1):
            dve.wait_ge(s_done, (b - 1) * H0 + 4 * n + 4)
        dve.tensor_copy(qT[:, 2 * n:2 * n + 2, :], ps[7][:, :].rearrange("p (k n) -> p k n", k=2)).then_inc(qT_dve, 1)

    def dve_probT(dve, b, step):
        h = step - LAG_LO
        g = b * H0 + h
        if under_way(b, step, LAG_LO):
            dve.wait_ge(pT_hi, g + 1)
            dve.scalar_tensor_tensor(probT[1][:, h % 4, :], ps[2 + h % 2][:, 0:SW], PROB_SCALE, probT[0][:, h % 4, :],
                                     ALU.mult, ALU.subtract).then_inc(pT_lo, 1)

    def dve_mask(dve, b, step):
        h = step
        g = b * H0 + h
        dve.wait_ge(s_done, g + 1)
        if not past(b, 1):
            dve.wait_ge(alibi_done, h + 1)
        if past(g, 4):
            dve.wait_ge(pT_done, g - 3)
        stand_apart(dve)
        for qb, (c0, c1) in enumerate(((0, P), (P, SW))):
            dve.tensor_tensor_reduce(prob[:, h % 4, c0:c1], ps[h % 2][:, c0:c1], alibi[:, h, 2 * P - (c1 - c0):2 * P],
                                     -SC0, 3e38, ALU.add, ALU.min, neg_max[:, h % 4, qb:qb + 1]).then_inc(masked, 1)

    def dve_inverse(dve, b, part):
        hs = slice(part * (H0 // 2), (part + 1) * (H0 // 2))
        dve.wait_ge(exp_done, (b * 2 + part + 1) * H0)
        if part == 0 and past(b, 1):
            dve.wait_ge(o_out, b * BT)
        dve.reciprocal(row_inv[:, hs, :], row_sum[:, hs, :]).then_inc(inv_done, 1)

    def dve_out(dve, b):
        dve.wait_ge(inv_done, b * 2 + 2)
        dve.wait_ge(pv_done, b * H0 + H0)
        for t in range(BT):
            dve.tensor_tensor(tok[:, t, :].rearrange("p (h d) -> p h d", h=H0),
                              ps[4 + t][:, :].rearrange("p (h d) -> p h d", h=H0),
                              row_inv[:, :, t:t + 1].to_broadcast([P, H0, HD0]), ALU.mult).then_inc(o_out, 1)

    def dve_fT(dve, b, hi, lo):
        for t in range(BT):
            lo_part(dve, fT[0][:, :, t * P:(t + 1) * P], fT[1][:, :, t * P:(t + 1) * P], turned(6 + t), hi, b * BT + t + 1, lo)

    def add_delta(dve, b, norm, done):
        dve.wait_ge(norm.normed, b * BT + BT)
        for t in range(BT):
            dve.tensor_tensor(xrow(b, t), xrow(b, t), delta[:, t, :], ALU.add).then_inc(done, 1)

    def dve_n2(dve, b):
        dve.wait_ge(wo_done, b * BT + BT)
        ln2.moments(dve, b, lambda t: ps[6 + t][:, :], True)

    def dve_a2(dve, b):
        ln2.apply(dve, b, lambda t: ps[6 + t][:, :], lambda t: delta[:, t, :])

    def dve_x1(dve, b):
        add_delta(dve, b, ln2, x1_done)

    def dve_n3(dve, b):
        dve.wait_ge(x1_done, b * BT + BT)
        ln3.moments(dve, b, lambda t: xrow(b, t), True)

    def dve_a3(dve, b):
        dve.wait_ge(oT_done, b * BT + BT)
        ln3.apply(dve, b, lambda t: xrow(b, t), lambda t: tok[:, t, :])

    def dve_bias(dve, b, t):
        dve.wait_ge(ffn_done, b * BT + t + 1)
        dve.tensor_tensor(delta[:, t, :], ps[6 + t][:, :], bias_b[:, :], ALU.add).then_inc(biased, 1)

    def dve_n4(dve, b):
        dve.wait_ge(biased, b * BT + BT)
        ln4.moments(dve, b, lambda t: delta[:, t, :], True)

    def dve_a4(dve, b):
        ln4.apply(dve, b, lambda t: delta[:, t, :], lambda t: delta[:, t, :])

    def dve_x2(dve, b):
        add_delta(dve, b, ln4, x2_done)

    def dve_gates(dve):
        dve.wait_ge(wf_in, 48)
        dve.tensor_tensor(gate_p[:, :], gate_w[:, 0, :], gate_w[:, 1, :], ALU.mult).then_inc(gate_done, 1)
        dve.wait_ge(gate_done, 1)
        for r in range(ER):
            dve.tensor_scalar(bf_raw[:, r, :], bf_raw[:, r, :], gate_p[:, r:r + 1], None, ALU.mult).then_inc(bf_scaled, 1)

    def dve_merge(dve, k):
        dve.wait_ge(adapters_done, k + 1)
        dve.tensor_tensor(wf_raw[:, k, :], ps[6 + k % 2][:, :], wf_raw[:, k, :], ALU.add).then_inc(w_eff_done, 1)

    def dve_batch(dve, b, tail, prologue):
        for step in range(H0):
            if step == 0:
                dve_kT(dve, b)
            for j, at in enumerate(AT["qT_out"]):
                if step == at and (j < 2 and prologue or j >= 2 and tail):
                    dve_qT(dve, b if j >= 2 else b + 1, j)
                if not tail and step == FIRST_QT_OUT[j]:
                    dve_qT(dve, 0, j)
            if prologue and step == AT["v"]:
                dve_v(dve, b + 1, step % 2, b * H0 + step + 1)
            dve_mask(dve, b, step)
            dve_probT(dve, b, step)
            if step == 1 and tail:
                dve_inverse(dve, b - 1, 1)
            if step == H0 // 2 + 1:
                dve_inverse(dve, b, 0)
            if not tail and step == 4:
                dve_gates(dve)
            if not tail and step - ER in MERGE:
                dve_merge(dve, MERGE.index(step - ER))
            if tail and step == AT["out"]:
                dve_out(dve, b - 1)
            if tail and step == AT["oT_out"]:
                dve_fT(dve, b - 1, oT_hi, oT_lo)
            if tail and step == AT["n2"]:
                dve_n2(dve, b - 1)
            if tail and step == AT["a2"]:
                dve_a2(dve, b - 1)
            if tail and step == AT["x1"]:
                dve_x1(dve, b - 1)
            if tail and step == AT["n3"]:
                dve_n3(dve, b - 1)
            if tail and step == AT["a3"]:
                dve_a3(dve, b - 1)
            if tail and step == AT["x1T_out"]:
                dve_fT(dve, b - 1, x1T_hi, x1T_lo)
            if prologue and step == AT["n1"]:
                dve_n1(dve, b + 1)
            for t in range(BT):
                if tail and step == AT["bias"][t]:
                    dve_bias(dve, b - 1, t)
            if tail and step == AT["n4"]:
                dve_n4(dve, b - 1)
            if tail and step == AT["a4"]:
                dve_a4(dve, b - 1)
            if prologue and step == AT["a1"]:
                dve_a1(dve, b + 1)
            if tail and step == AT["x2"]:
                dve_x2(dve, b - 1)
            if prologue and step == AT["xT_out"]:
                dve_xT(dve, b + 1)
            if prologue and step == AT["kv_out"]:
                dve_k(dve, b + 1)
            if prologue and step == AT["q0_out"]:
                dve_q(dve, b + 1, 0)
            if prologue and step == AT["q1_out"]:
                dve_q(dve, b + 1, 1)

    def tensor(pe):
        pe.wait_ge(consts_in, 16)
        pe_xT(pe, 0)
        pe.wait_ge(wkv_lo, 1)
        pe_kv(pe, 0, 0)
        pe_kv(pe, 0, 1)
        pe_v(pe, 0, 0)
        pe.wait_ge(wq_lo, 1)
        for t in range(BT):
            for half in range(2):
                pe_q(pe, 0, t, half)
        pe_qT(pe, 0, 0)
        pe_batch(pe, 0, False, True)
        with pe.Fori(1, NB - 1) as b:
            pe_batch(pe, b, True, True)
        pe_batch(pe, NB - 1, True, False)
        for step in range(LAG_V):
            pe_head(pe, NB, step)
        pe_oT(pe, NB - 1, True)

    def transpose_tok(pe, source, t, done):
        for k in range(KD):
            last = pe.transpose(ps[6 + t][:, k * P:(k + 1) * P], source[:, t, k * P:(k + 1) * P], ident[:, :])
        last.then_inc(done, 1)

    def pe_xT(pe, b):
        for t in range(BT):
            pe.wait_ge(ln1.normed, b * BT + t + 1)
            if past(b, 2):
                pe.wait_ge(ln2.normed, (b - 1) * BT)
            elif b == 1:
                pe.wait_ge(w_eff_done, KD)
            transpose_tok(pe, x_tok, t, xT_done)

    def pe_kv(pe, b, part):
        rows, out, cols = ((slice(0, P), slice(0, TB), slice(0, P)), (slice(0, HD0), slice(TB, 2 * TB), slice(P, P + HD0)))[part]
        if part == 0:
            pe.wait_ge(xT_lo, b * BT + BT)
            if past(b, 2):
                pe.wait_ge(x1T_lo, (b - 1) * BT)
        for k in range(KD):
            last = split_product(pe, ps[7][rows, out], (wkv[0][:, k, cols], wkv[1][:, k, cols]),
                                 (xT[0][:, k, :], xT[1][:, k, :]), k == 0, k == KD - 1)
        if part == 1:
            last.then_inc(kv_done, 1)

    def pe_v(pe, b, bank):
        pe.wait_ge(vT_out, b + 1)
        stand_apart(pe)
        for t in range(BT):
            last = pe.transpose(ps[bank][:, SW + t * HD0:SW + (t + 1) * HD0], vT[:, t * P:(t + 1) * P], ident[0:HD0, 0:HD0])
        last.then_inc(v_turned, 1)

    def pe_q(pe, b, t, half):
        if half == 0 and t == 1:
            pe.wait_ge(k_lo, b + 1)
            pe.wait_ge(vT_out, b + 1)
        if half == 0 and past(b, 2):
            pe.wait_ge(biased, (b - 1) * BT - 1 + t)
        for k in range(KD // 2 * half, KD // 2 * (half + 1)):
            last = split_product(pe, ps[6 + t][:, :], (xT[0][:, k, t * P:(t + 1) * P], xT[1][:, k, t * P:(t + 1) * P]),
                                 (wq[0][:, k, :], wq[1][:, k, :]), k == 0, k == KD - 1)
        if half == 1:
            last.then_inc(q_done, 1)

    def pe_qT(pe, b, j):
        if j == 0:
            pe.wait_ge(q_lo, b * BT + BT)
        else:
            pe.wait_ge(qT_act, b * (QG // 2) + j)
            pe.wait_ge(qT_dve, b * (QG // 2) + j)
        for n in (2 * j, 2 * j + 1):
            for c in range(4):
                two, t = 2 * n + c // 2, c % 2
                last = pe.transpose(ps[6 + n % 2][:, c * P:(c + 1) * P],
                                    q_slots[:, t, 2 * two:2 * two + 2, :, :].rearrange("p h s d -> p (h s d)").bitcast(F32),
                                    ident[:, :])
            last.then_inc(qT_done, 1)

    def pe_head(pe, b, step, v_too=False):
        h = step
        g = b * H0 + h
        if not past_end(b):
            rows = slice(64 * (h % 2), 64 * (h % 2) + 64)
            if h == 0:
                pe.wait_ge(kT_out, b + 1)
            if h % 8 == 0:
                pe.wait_ge(qT_act, b * (QG // 2) + h // 8 + 1)
            if h % 8 == 4:
                pe.wait_ge(qT_dve, b * (QG // 2) + h // 8 + 1)
            if past(g, 2):
                pe.wait_ge(masked, 2 * (g - 1))
            elif g == 0:
                pe.wait_ge(v_out, 1)
            if v_too:
                pe_v(pe, b + 1, h % 2)
            pe.matmul(ps[h % 2][:, 0:P], qT[rows, h // 2, 0:P], kT[rows, 0:P], start=True, stop=True)
            pe.matmul(ps[h % 2][:, P:SW], qT[rows, h // 2, P:TB], kT[rows, :], start=True, stop=True).then_inc(s_done, 1)
        h = step - LAG_T
        g = b * H0 + h
        if under_way(b, step, LAG_T):
            pe.wait_ge(exp_done, 2 * g + 2)
            if past(g, 2):
                pe.wait_ge(pT_lo, g - 1)
            for n in range(3):
                last = pe.transpose(ps[2 + h % 2][:, n * P:(n + 1) * P], prob[:, h % 4, n * P:(n + 1) * P], ident[:, :])
            last.then_inc(pT_done, 1)
        h = (step - LAG_V) % H0
        g = b * H0 + step - LAG_V
        if under_way(b, step, LAG_V):
            pe.wait_ge(pT_lo, g + 1)
            if h == 0:
                pe.wait_ge(v_copied, b + 1)
                if past(b, 1):
                    pe.wait_ge(o_out, b * BT)
            cols = slice(h * HD0, (h + 1) * HD0)
            for qb, kb, c in ((0, 0, 0), (1, 0, P), (1, 1, 2 * P)):
                for part in range(2):
                    for n in range(3):
                        last = pe.matmul(ps[4 + qb][:, cols], probT[part][:, h % 4, c:c + P], v_parts[:, n, kb, :],
                                         start=(kb == 0 and part == 0 and n == 0), stop=(kb == qb and part == 1 and n == 2))
            last.then_inc(pv_done, 1)

    def pe_merge(pe, k, r):
        pe.wait_ge(bf_scaled, ER)
        if k < 2:
            pe.wait_ge(qT_act, QG // 2)
            pe.wait_ge(qT_dve, QG // 2)
        else:
            pe.wait_ge(w_eff_done, k - 1)
        last = pe.matmul(ps[6 + k % 2][:, :], a_raw[:, r, k * P:(k + 1) * P], bf_raw[:, r, :],
                         start=(r == 0), stop=(r == ER - 1))
        if r == ER - 1:
            last.then_inc(adapters_done, 1)

    def pe_oT(pe, b, last):
        for t in range(BT):
            pe.wait_ge(o_out, b * BT + t + 1)
            if last:
                pe.wait_ge(biased, b * BT)
            else:
                pe.wait_ge(qT_act, (b + 2) * (QG // 2))
                pe.wait_ge(qT_dve, (b + 2) * (QG // 2))
            transpose_tok(pe, tok, t, oT_done)

    def pe_linear(pe, b, weights, ready, done, chunk):
        t, half = divmod(chunk, 2)
        if chunk == 0:
            pe.wait_ge(ready, b * BT + BT)
        for k in range(KD // 2 * half, KD // 2 * (half + 1)):
            last = split_product(pe, ps[6 + t][:, :], (fT[0][:, k, t * P:(t + 1) * P], fT[1][:, k, t * P:(t + 1) * P]),
                                 (weights[0][:, k, :], weights[1][:, k, :]), k == 0, k == KD - 1)
        if half == 1:
            last.then_inc(done, 1)

    def pe_x1T(pe, b, shared):
        for t in range(BT):
            pe.wait_ge(ln3.normed, b * BT + t + 1)
            if shared:
                pe.wait_ge(xT_lo, (b + 3) * BT)
            transpose_tok(pe, tok, t, x1T_done)

    def pe_batch(pe, b, tail, prologue):
        for step in range(H0):
            pe_head(pe, b, step, prologue and step == AT["v"])
            for r in range(ER):
                if not tail and step - r in MERGE:
                    pe_merge(pe, MERGE.index(step - r), r)
            if tail and step == AT["oT"]:
                pe_oT(pe, b - 1, False)
            if tail and 0 <= step - AT["wo"] < CHUNKS:
                pe.wait_ge(wo_lo, 1)
                pe_linear(pe, b - 1, wo, oT_lo, wo_done, step - AT["wo"])
            if prologue and step == AT["xT"]:
                pe_xT(pe, b + 1)
            if tail and step == AT["x1T"]:
                pe_x1T(pe, b - 1, prologue)
            if prologue and 0 <= step - AT["kv"] < 2:
                pe_kv(pe, b + 1, step - AT["kv"])
            if tail and 0 <= step - AT["ffn"] < CHUNKS:
                pe.wait_ge(wf_lo, 1)
                if prologue and step == AT["ffn"] + 2:
                    pe.wait_ge(k_lo, b + 2)
                    pe.wait_ge(vT_out, b + 2)
                pe_linear(pe, b - 1, wf, x1T_lo, ffn_done, step - AT["ffn"])
            for t in range(BT):
                if prologue and 0 <= step - AT[f"q{t}"] < 2:
                    pe_q(pe, b + 1, t, step - AT[f"q{t}"])
            for j, at in enumerate(AT["qT"]):
                if step == at and (j < 3 and prologue or j == 3 and tail):
                    pe_qT(pe, b if j == 3 else b + 1, j)
                if not tail and step == FIRST_QT[j]:
                    pe_qT(pe, 0, j)

    last = NB - 1

    def inverse(norm):
        return lambda pl: norm.inverse(pl, last, minus_half[:, 0:BT])

    def all_chunks(weights, ready, done):
        def products(pe):
            for chunk in range(CHUNKS):
                pe_linear(pe, last, weights, ready, done, chunk)
        return products

    def bias(dve):
        for t in range(BT):
            dve_bias(dve, last, t)

    tail = {"pool_n2": inverse(ln2), "pool_n3": inverse(ln3), "pool_n4": inverse(ln4),
            "act_x1T": lambda act: act_turned(act, last, x1T_done, x1T_hi),
            "dve_n2": lambda dve: dve_n2(dve, last), "dve_a2": lambda dve: dve_a2(dve, last),
            "dve_x1": lambda dve: dve_x1(dve, last), "dve_n3": lambda dve: dve_n3(dve, last),
            "dve_a3": lambda dve: dve_a3(dve, last), "dve_x1T": lambda dve: dve_fT(dve, last, x1T_hi, x1T_lo),
            "dve_bias": bias, "dve_n4": lambda dve: dve_n4(dve, last), "dve_a4": lambda dve: dve_a4(dve, last),
            "dve_x2": lambda dve: dve_x2(dve, last),
            "pe_wo": all_chunks(wo, oT_lo, wo_done), "pe_x1T": lambda pe: pe_x1T(pe, last, False),
            "pe_ffn": all_chunks(wf, x1T_lo, ffn_done),
            "ffn_over": (ffn_done, NT), "biased": biased, "done": x2_done}

    ctx.close()
    return {"sync": sync, "pool": pool, "scalar": scalar, "vector": vector, "tensor": tensor, "tail": tail,
            "x2_done": x2_done, "heads_over": (o_out, NT)}


def past(count, n):
    return not isinstance(count, int) or count >= n


def past_end(b):
    return isinstance(b, int) and b == NB


def under_way(b, step, lag):
    return past(b * H0 + step - lag, 0) and not (past_end(b) and step >= lag)


class BatchNorm:

    def __init__(self, name, sb, sem):
        self.six = sb(f"{name}_six", [P, 2, BT, 6], F32)
        self.mv = sb(f"{name}_mv", [P, 2, BT, 2], F32)
        self.var_eps = sb(f"{name}_var_eps", [P, 2, BT], F32)
        self.rstd = sb(f"{name}_rstd", [P, 2, BT], F32)
        self.stats_done = sem(f"{name}_stats_done")
        self.moments_done = sem(f"{name}_moments_done")
        self.var_ready = sem(f"{name}_var_ready")
        self.rstd_ready = sem(f"{name}_rstd_ready")
        self.normed = sem(f"{name}_normed")

    def moments(self, dve, use, source):
        n = use % 2
        if use >= 2:
            dve.wait_ge(self.normed, (use - 1) * BT)
        for t in range(BT):
            dve.bn_stats(self.six[:, n, t, :], source(t)).then_inc(self.stats_done, 1)
        for t in range(BT):
            dve.wait_ge(self.stats_done, use * BT + t + 1)
            dve.bn_aggr(self.mv[:, n, t, :], self.six[:, n, t, :]).then_inc(self.moments_done, 1)
        dve.wait_ge(self.moments_done, use * BT + BT)
        dve.tensor_scalar(self.var_eps[:, n, :], self.mv[:, n, :, 1], EPS, None, ALU.add).then_inc(self.var_ready, 1)

    def inverse(self, pool, use, minus_half):
        pool.wait_ge(self.var_ready, use + 1)
        pool.tensor_tensor(self.rstd[:, use % 2, :], self.var_eps[:, use % 2, :], minus_half[:, 0:BT], ALU.pow)\
            .then_inc(self.rstd_ready, 1)

    def apply(self, dve, use, source, target):
        n = use % 2
        dve.wait_ge(self.rstd_ready, use + 1)
        for t in range(BT):
            dve.tensor_scalar(target(t), source(t), self.mv[:, n, t, 0:1], self.rstd[:, n, t:t + 1],
                              ALU.subtract, ALU.mult).then_inc(self.normed, 1)


class Stream:

    def __init__(self, sb, sem, X, XT, acc, ps, ident, minus_half, x2_done):
        self.x2_done = x2_done
        self.X, self.XT, self.acc, self.ps, self.ident, self.minus_half = X, XT, acc, ps, ident, minus_half
        self.post = BatchNorm("post", sb, sem)
        self.pre = BatchNorm("pre", sb, sem)
        self.tok = sb("turn_tok", [P, 2 * BT, D], F32)
        self.summed = sem("summed")
        self.last_summed = sem("last_summed")
        self.turned = sem("turned")
        self.hi_out = sem("turn_hi_out")
        self.lo_out = sem("turn_lo_out")

    def rows(self, what, b):
        return lambda t: what[:, b * BT + t, :]

    def post_moments(self, dve, rnd, b):
        self.post.moments(dve, rnd * NB + b, self.rows(self.acc, b))

    def post_apply(self, dve, rnd, b):
        self.post.apply(dve, rnd * NB + b, self.rows(self.acc, b), self.rows(self.acc, b))

    def add(self, engine, rnd, b):
        X, acc = self.X, self.acc
        for t in range(BT):
            n = b * BT + t
            engine.wait_ge(self.post.normed, rnd * NT + n + 1)
            done = self.last_summed if rnd == 1 and b == NB - 1 else self.summed
            engine.tensor_tensor(X[:, n, :], X[:, n, :], acc[:, n, :], ALU.add).then_inc(done, 1)

    def pre_moments(self, dve, rnd, b):
        if rnd:
            dve.wait_ge(self.summed, b * BT + BT)
        else:
            dve.wait_ge(self.x2_done, b * BT + BT)
        self.pre.moments(dve, rnd * NB + b, self.rows(self.X, b))

    def pre_apply(self, dve, rnd, b):
        self.pre.apply(dve, rnd * NB + b, self.rows(self.X, b), lambda t: self.tok[:, b % 2 * BT + t, :])

    def turn(self, pe, rnd, n, bank):
        pe.wait_ge(self.pre.normed, rnd * NT + n + 1)
        for k in range(KD):
            last = pe.transpose(self.ps[bank][:, k * P:(k + 1) * P], self.tok[:, n % (2 * BT), k * P:(k + 1) * P],
                                self.ident[:, :])
        last.then_inc(self.turned, 1)

    def turned_tile(self, bank):
        return self.ps[bank][:, :].rearrange("p (k n) -> p k n", k=KD)

    def hi(self, act, rnd, n, bank):
        act.wait_ge(self.turned, rnd * NT + n + 1)
        act.activation(self.XT[0][:, :, n * P:(n + 1) * P], self.turned_tile(bank), ACT.Copy).then_inc(self.hi_out, 1)

    def lo(self, dve, rnd, n, bank):
        dve.wait_ge(self.hi_out, rnd * NT + n + 1)
        dve.tensor_tensor(self.XT[1][:, :, n * P:(n + 1) * P], self.turned_tile(bank),
                          self.XT[0][:, :, n * P:(n + 1) * P].bitcast(F32), ALU.subtract).then_inc(self.lo_out, 1)


def layer1_attention(nc, dram, keep, stream, XT, acc, ps, consts, tail, room):
    ident = consts["ident"]
    ctx = ExitStack()
    sb = lambda name, shape, dt: ctx.enter_context(nc.sbuf_tensor(name, shape, dt))
    sem = lambda name: nc.semaphore(name).__enter__()
    sems = lambda names: [sem(name) for name in names.split()]
    pair = lambda name, shape: [sb(f"{name}_{x}", shape, F32R) for x in ("hi", "lo")]

    prob, pT, oT, wo = keep["prob"], keep["pT"], keep["oT"], keep["wo"]
    w_raw = sb("w_raw1", [P, KD, GW], F32)
    w = pair("w1", [P, KD, GW])
    wo_raw = sb("wo_raw1", [P, HG, D], F32)
    cos, sin = sb("cos1", [P, TB], F32), sb("sin1", [P, TB], F32)
    causal = sb("causal1", [P, 2 * P], F32)
    neg_max = sb("neg_max1", [P, HG, 2], F32)
    row_sum = sb("row_sum1", [P, HG, 2], F32)
    row_inv = sb("row_inv1", [P, HG, 2], F32)
    k_sum, k_rot = sb("k_sum1", [P, TB], F32), sb("k_rot1", [P, TB], F32)
    q_sum, q_rot = sb("q_sum1", [P, 2, TB], F32), sb("q_rot1", [P, 2, TB], F32)
    vT = sb("vT1", [P, TB], F32)
    q = [pair(f"q1_{n}", [P, HG, TB]) for n in range(2)]
    k = [pair(f"k1_{n}", [P, TB]) for n in range(2)]
    v = [pair(f"v1_{n}", [P, BT, HD1]) for n in range(2)]

    acc_zero, tables_in = sem("acc_zero"), sem("tables_in")
    kvw_in, qw_in, wo_in = sem("kvw_in1"), sem("qw_in1"), sem("wo_in1")
    kvw_hi, qw_hi, kvw_lo, qw_lo, wo_hi, wo_lo = sems("kvw_hi qw_hi kvw_lo qw_lo wo_hi1 wo_lo1")
    s_done, masked, exp_done, inv_done, normed = sems("s_done1 masked1 exp_done1 inv_done1 normed1")
    pT_done, pT_hi, pT_lo = sems("pT_done1 pT_hi1 pT_lo1")
    kv_done, vT_out, v_turned, v_hi, v_lo = sems("kv_done1 vT_out1 v_turned1 v_hi1 v_lo1")
    k_halves, k_sin, k_cos, k_added, k_hi, k_lo = sems("k_halves k_sin k_cos k_added k_hi1 k_lo1")
    q_done, q_halves, q_sin, q_cos, q_added, q_hi, q_lo = sems("q_done1 q_halves q_sin q_cos q_added q_hi1 q_lo1")
    pv_done, o_hi, o_lo, wo_done, added = sems("pv_done1 o_hi1 o_lo1 wo_done1 added1")

    FIRST_BANKS = (0, 1, 2, 3, 4, 0)
    BS, BP, BO, BM = (0, 1), (2, 3), 4, (5, 6, 7)
    KC, VC, QC = 0, HD1, 2 * HD1
    half = HD1 // 2

    def heads(bank):
        return ps[bank][:, :].rearrange("p (h n) -> p h n", h=2)

    def over_pair(table):
        return table[:, :].rearrange("p (a n) -> p a n", a=1).to_broadcast([P, 2, TB])

    def over_groups(engine, step):
        for b in range(NB):
            step(0, b, b > 0, True)
        with engine.Fori(1, NG - 1) as g:
            for b in range(NB):
                step(g, b, True, True)
        for b in range(NB):
            step(NG - 1, b, True, b < NB - 1)

    def sync(sp):
        sp.wait_ge(*room)
        sp.dma_start(w_raw[:, :, 0:QC], dram["w1"][0][:, :, 0:QC]).then_inc(kvw_in, 16)
        sp.dma_start(cos[:, :], dram["cos"]).then_inc(tables_in, 16)
        sp.dma_start(sin[:, :], dram["sin"]).then_inc(tables_in, 16)
        sp.dma_start(w_raw[:, :, QC:GW], dram["w1"][0][:, :, QC:GW]).then_inc(qw_in, 16)
        sp.dma_start(causal[:, :], dram["causal"]).then_inc(tables_in, 16)
        sp.dma_start(wo_raw[:, :, :], dram["wo1"][0]).then_inc(wo_in, 16)
        with sp.Fori(1, NG) as g:
            sp.wait_ge(qw_lo, g * 2)
            sp.wait_ge(kvw_lo, g)
            sp.dma_start(w_raw[:, :, 0:QC], dram["w1"][g][:, :, 0:QC]).then_inc(kvw_in, 16)
            sp.dma_start(w_raw[:, :, QC:GW], dram["w1"][g][:, :, QC:GW]).then_inc(qw_in, 16)
            sp.wait_ge(wo_lo, g)
            sp.dma_start(wo_raw[:, :, :], dram["wo1"][g]).then_inc(wo_in, 16)

    def project_kv(pe, u, b):
        if past(u, 1):
            pe.wait_ge(v_lo, u)
        xs = slice(b * TB, (b + 1) * TB)
        for c0, o in ((KC, 0), (VC, TB)):
            for n in range(KD):
                last = split_product(pe, ps[BM[0]][:, o:o + TB], (w[0][:, n, c0:c0 + HD1], w[1][:, n, c0:c0 + HD1]),
                                     (XT[0][:, n, xs], XT[1][:, n, xs]), n == 0, n == KD - 1)
        last.then_inc(kv_done, 1)

    def q_bank(u, p):
        return BP[p] if isinstance(u, int) and u == 0 else BM[1 + p]

    def project_q(pe, u, b, p):
        if past(u, 3):
            pe.wait_ge(added, (u - 3) * 2 + p + 1)
        elif u == 2:
            pe.wait_ge(q_cos, (u - 1) * 2 + p + 1)
        elif u == 1:
            pe.wait_ge(tail["biased"], NT - 1 + p)
        xs = slice(b * TB, (b + 1) * TB)
        for h in (2 * p, 2 * p + 1):
            c0 = QC + h * HD1
            for n in range(KD):
                last = split_product(pe, ps[q_bank(u, p)][:, (h % 2) * TB:(h % 2 + 1) * TB],
                                     (w[0][:, n, c0:c0 + HD1], w[1][:, n, c0:c0 + HD1]),
                                     (XT[0][:, n, xs], XT[1][:, n, xs]), n == 0, n == KD - 1)
        last.then_inc(q_done, 1)

    def turn_v(pe, u, b):
        pe.wait_ge(vT_out, u + 1)
        pe.wait_ge(k_cos, u + 1)
        for t in range(BT):
            last = pe.transpose(ps[BM[0]][:, t * P:(t + 1) * P], vT[:, t * P:(t + 1) * P], ident[:, :])
        last.then_inc(v_turned, 1)

    def scores(pe, u, b, h):
        n = b % 2
        if h == 0:
            pe.wait_ge(k_lo, u + 1)
        if h % 2 == 0:
            pe.wait_ge(q_lo, u * 2 + h // 2 + 1)
        if (h >= 2 or past(u, 1)):
            pe.wait_ge(masked, u * 8 + 2 * (h - 1))
        for qs, ks, cols in ((slice(0, P), slice(0, P), slice(0, P)), (slice(P, TB), slice(0, TB), slice(P, SW))):
            last = split_product(pe, ps[BS[h % 2]][:, cols], (q[n][0][:, h, qs], q[n][1][:, h, qs]),
                                 (k[n][0][:, ks], k[n][1][:, ks]), True, True)
        last.then_inc(s_done, 1)

    def turn_prob(pe, u, b, h):
        pe.wait_ge(normed, u * 8 + 2 * h + 2)
        if (h >= 2 or past(u, 1)):
            pe.wait_ge(pT_lo, u * HG + h - 1)
        for n in range(3):
            last = pe.transpose(ps[BP[h % 2]][:, n * P:(n + 1) * P], prob[:, h, n * P:(n + 1) * P], ident[:, :])
        last.then_inc(pT_done, 1)

    def prob_v(pe, u, b, p):
        n = b % 2
        pe.wait_ge(pT_lo, u * HG + 2 * p + 2)
        if p == 0:
            pe.wait_ge(v_lo, u + 1)
        if (p or past(u, 1)):
            pe.wait_ge(o_lo, u * 2 + p)
        hs = slice(2 * p, 2 * p + 2)
        for kb, cols, qs in ((0, slice(0, 2 * P), slice(0, TB)), (1, slice(2 * P, SW), slice(P, TB))):
            last = split_product(pe, heads(BO)[:, :, qs], (v[n][0][:, kb, :], v[n][1][:, kb, :]),
                                 (pT[0][:, hs, cols], pT[1][:, hs, cols]), kb == 0, kb == 1)
        last.then_inc(pv_done, 1)

    def project_out(pe, u, b, t):
        if t == 0:
            pe.wait_ge(o_lo, u * 2 + 2)
        for h in range(HG):
            last = split_product(pe, ps[BM[1 + t]][:, :], (oT[0][:, h, t * P:(t + 1) * P], oT[1][:, h, t * P:(t + 1) * P]),
                                 (wo[0][:, h, :], wo[1][:, h, :]), h == 0, h == HG - 1)
        last.then_inc(wo_done, 1)

    U = NG * NB

    def more(g):
        return not (isinstance(g, int) and g == NG - 1)

    def finishing(g, b):
        if isinstance(g, int) and g == NG - 1 and b >= 2:
            return b - 2, 1
        if isinstance(g, int) and g == 0 and b == 1:
            return NB - 1, 0
        return None, None

    def tensor(pe):
        tail["pe_wo"](pe)
        for t in range(2 * BT):
            stream.turn(pe, 0, t, FIRST_BANKS[t])
        pe.wait_ge(stream.lo_out, BT)
        pe.wait_ge(kvw_lo, 1)
        project_kv(pe, 0, 0)
        tail["pe_x1T"](pe)
        for t in range(2 * BT, NT - BT):
            stream.turn(pe, 0, t, FIRST_BANKS[t])
        pe.wait_ge(qw_lo, 2)
        pe.wait_ge(stream.lo_out, 2 * BT)
        project_q(pe, 0, 0, 0)
        project_q(pe, 0, 0, 1)
        tail["pe_ffn"](pe)
        turn_v(pe, 0, 0)
        pe.wait_ge(stream.lo_out, NT - BT)

        def step(g, b, before, after):
            u, nb, pb = g * NB + b, (b + 1) % NB, (b - 1) % NB
            scores(pe, u, b, 0)
            scores(pe, u, b, 1)
            if before:
                prob_v(pe, u - 1, pb, 1)
            if after:
                if nb == 0:
                    pe.wait_ge(kvw_lo, g + 2)
                if isinstance(g, int) and g == 0 and b == 2:
                    pe.wait_ge(stream.lo_out, NT)
                project_kv(pe, u + 1, nb)
            scores(pe, u, b, 2)
            scores(pe, u, b, 3)
            if after:
                if nb == 0:
                    pe.wait_ge(qw_lo, g * 2 + 3)
                project_q(pe, u + 1, nb, 0)
            turn_prob(pe, u, b, 0)
            turn_prob(pe, u, b, 1)
            if after:
                if nb == 0:
                    pe.wait_ge(qw_lo, g * 2 + 4)
                project_q(pe, u + 1, nb, 1)
                turn_v(pe, u + 1, nb)
            if before:
                wait_q_left(pe, u, after, 0)
                if pb == 0:
                    pe.wait_ge(wo_lo, g + 1)
                project_out(pe, u - 1, pb, 0)
            turn_prob(pe, u, b, 2)
            turn_prob(pe, u, b, 3)
            if before:
                wait_q_left(pe, u, after, 1)
                project_out(pe, u - 1, pb, 1)
            done, rnd = finishing(g, b)
            if done is not None:
                stream.turn(pe, rnd, done * BT, BM[0])
            prob_v(pe, u, b, 0)
            if done is not None:
                pe.wait_ge(stream.lo_out, rnd * NT + done * BT + 1)
                stream.turn(pe, rnd, done * BT + 1, BM[0])

        over_groups(pe, step)
        prob_v(pe, U - 1, NB - 1, 1)
        pe.wait_ge(added, U * 2 - 2)
        project_out(pe, U - 1, NB - 1, 0)
        project_out(pe, U - 1, NB - 1, 1)

    def wait_q_left(pe, u, after, t):
        pe.wait_ge(q_cos, u * 2 + 3 + t if after else u * 2 + 1 + t)

    def q_columns(p):
        return slice(QC + p * (QW // 2), QC + (p + 1) * (QW // 2))

    def act_kvw(act, g):
        act.wait_ge(kvw_in, g * 16 + 16)
        if past(g, 1):
            act.wait_ge(kv_done, g * NB)
        act.activation(w[0][:, :, 0:QC], w_raw[:, :, 0:QC], ACT.Copy).then_inc(kvw_hi, 1)

    def act_qw(act, g, p):
        if p == 0:
            act.wait_ge(qw_in, g * 16 + 16)
        if past(g, 1):
            act.wait_ge(q_done, g * (2 * NB) - 1 + p)
        act.activation(w[0][:, :, q_columns(p)], w_raw[:, :, q_columns(p)], ACT.Copy).then_inc(qw_hi, 1)

    def act_wo(act, g):
        act.wait_ge(wo_in, g * 16 + 16)
        if past(g, 1):
            act.wait_ge(wo_done, g * (2 * NB))
        act.activation(wo[0][:, :, :], wo_raw[:, :, :], ACT.Copy).then_inc(wo_hi, 1)

    def swap_halves(act, target, source, done):
        act.activation(target[0:half], source[half:HD1], ACT.Copy).then_inc(done, 1)
        act.activation(target[half:HD1], source[0:half], ACT.Copy).then_inc(done, 1)

    def act_kv(act, u, b):
        act.wait_ge(kv_done, u + 1)
        if past(u, 1):
            act.wait_ge(k_added, u)
            act.wait_ge(v_turned, u)
        act.activation(vT[:, :], ps[BM[0]][:, TB:2 * TB], ACT.Copy).then_inc(vT_out, 1)
        swap_halves(act, k_rot, ps[BM[0]][:, 0:TB], k_halves)

    def act_k_hi(act, u, b):
        act.wait_ge(k_added, u + 1)
        act.activation(k[b % 2][0][:, :], k_sum[:, :], ACT.Copy).then_inc(k_hi, 1)

    def act_q(act, u, b, p):
        act.wait_ge(q_done, u * 2 + p + 1)
        if (p or past(u, 1)):
            act.wait_ge(q_added, u * 2 + p)
        swap_halves(act, q_rot, heads(q_bank(u, p)), q_halves)

    def act_q_hi(act, u, b, p):
        act.wait_ge(q_added, u * 2 + p + 1)
        act.activation(q[b % 2][0][:, 2 * p:2 * p + 2, :], q_sum[:, :, :], ACT.Copy).then_inc(q_hi, 1)

    def act_v_hi(act, u, b):
        act.wait_ge(v_turned, u + 1)
        act.activation(v[b % 2][0][:, :, :], ps[BM[0]][:, 0:TB].rearrange("p (t n) -> p t n", t=BT), ACT.Copy).then_inc(v_hi, 1)

    def act_exp(act, u, b, h):
        act.wait_ge(masked, u * 8 + 2 * h + 2)
        if past(u, 1):
            act.wait_ge(inv_done, u * 2)
        for qb, (c0, c1) in enumerate(((0, P), (P, SW))):
            act.activation(prob[:, h, c0:c1], prob[:, h, c0:c1], ACT.Exp, bias=neg_max[:, h, qb:qb + 1], scale=-1.0,
                           accum_out=row_sum[:, h, qb:qb + 1]).then_inc(exp_done, 1)

    def act_pT(act, u, b, h):
        act.wait_ge(pT_done, u * HG + h + 1)
        act.activation(pT[0][:, h, :], ps[BP[h % 2]][:, 0:SW], ACT.Copy).then_inc(pT_hi, 1)

    def act_o(act, u, b, p):
        act.wait_ge(pv_done, u * 2 + p + 1)
        act.activation(oT[0][:, 2 * p:2 * p + 2, :], heads(BO), ACT.Copy).then_inc(o_hi, 1)

    def scalar(act):
        act_kvw(act, 0)
        for t in range(2 * BT):
            stream.hi(act, 0, t, FIRST_BANKS[t])
        act_qw(act, 0, 0)
        act_qw(act, 0, 1)
        tail["act_x1T"](act)
        for t in range(2 * BT, NT - BT):
            stream.hi(act, 0, t, FIRST_BANKS[t])
        act_kv(act, 0, 0)
        act_k_hi(act, 0, 0)
        act_q(act, 0, 0, 0)
        act_q_hi(act, 0, 0, 0)
        act_q(act, 0, 0, 1)
        act_q_hi(act, 0, 0, 1)
        act_v_hi(act, 0, 0)
        act.wait_ge(*tail["ffn_over"])
        act_wo(act, 0)

        def step(g, b, before, after):
            u, nb, pb = g * NB + b, (b + 1) % NB, (b - 1) % NB
            if b == 3 and more(g):
                act_qw(act, g + 1, 1)
            act_exp(act, u, b, 0)
            act_exp(act, u, b, 1)
            if before:
                act_o(act, u - 1, pb, 1)
            if after:
                act_kv(act, u + 1, nb)
            act_exp(act, u, b, 2)
            act_exp(act, u, b, 3)
            if after:
                act_k_hi(act, u + 1, nb)
                if b == 2 and more(g):
                    act_kvw(act, g + 1)
                act_q(act, u + 1, nb, 0)
            act_pT(act, u, b, 0)
            act_pT(act, u, b, 1)
            if after:
                act_q_hi(act, u + 1, nb, 0)
                act_q(act, u + 1, nb, 1)
                act_q_hi(act, u + 1, nb, 1)
                act_v_hi(act, u + 1, nb)
            act_pT(act, u, b, 2)
            act_pT(act, u, b, 3)
            done, rnd = finishing(g, b)
            if done is not None:
                stream.hi(act, rnd, done * BT, BM[0])
            act_o(act, u, b, 0)
            if done is not None:
                stream.hi(act, rnd, done * BT + 1, BM[0])
            if b == 0 and past(g, 1):
                act_wo(act, g)
            if b == 2 and more(g):
                act_qw(act, g + 1, 0)

        over_groups(act, step)
        act_o(act, U - 1, NB - 1, 1)

    def dve_kvw(dve, g):
        dve.wait_ge(kvw_hi, g + 1)
        dve.tensor_tensor(w[1][:, :, 0:QC], w_raw[:, :, 0:QC], w[0][:, :, 0:QC].bitcast(F32), ALU.subtract).then_inc(kvw_lo, 1)

    def dve_k_cos(dve, u, b):
        dve.wait_ge(k_halves, u * 2 + 2)
        if past(u, 1):
            dve.wait_ge(k_lo, u)
        dve.tensor_tensor(k_sum[:, :], ps[BM[0]][:, 0:TB], cos[:, :], ALU.mult).then_inc(k_cos, 1)

    def dve_k_add(dve, u, b):
        dve.wait_ge(k_sin, u + 1)
        dve.wait_ge(k_cos, u + 1)
        dve.tensor_tensor(k_sum[:, :], k_sum[:, :], k_rot[:, :], ALU.add).then_inc(k_added, 1)

    def dve_k_lo(dve, u, b):
        dve.wait_ge(k_hi, u + 1)
        dve.tensor_tensor(k[b % 2][1][:, :], k_sum[:, :], k[b % 2][0][:, :].bitcast(F32), ALU.subtract).then_inc(k_lo, 1)

    def dve_q_cos(dve, u, b, p):
        dve.wait_ge(q_halves, u * 4 + 2 * p + 2)
        if (p or past(u, 1)):
            dve.wait_ge(q_lo, u * 2 + p)
        dve.tensor_tensor(q_sum[:, :, :], heads(q_bank(u, p)), over_pair(cos), ALU.mult).then_inc(q_cos, 1)

    def dve_q_add(dve, u, b, p):
        dve.wait_ge(q_sin, u * 2 + p + 1)
        dve.wait_ge(q_cos, u * 2 + p + 1)
        dve.tensor_tensor(q_sum[:, :, :], q_sum[:, :, :], q_rot[:, :, :], ALU.add).then_inc(q_added, 1)

    def dve_q_lo(dve, u, b, p):
        dve.wait_ge(q_hi, u * 2 + p + 1)
        dve.tensor_tensor(q[b % 2][1][:, 2 * p:2 * p + 2, :], q_sum[:, :, :],
                          q[b % 2][0][:, 2 * p:2 * p + 2, :].bitcast(F32), ALU.subtract).then_inc(q_lo, 1)

    def dve_v_lo(dve, u, b):
        dve.wait_ge(v_hi, u + 1)
        dve.tensor_tensor(v[b % 2][1][:, :, :], ps[BM[0]][:, 0:TB].rearrange("p (t n) -> p t n", t=BT),
                          v[b % 2][0][:, :, :].bitcast(F32), ALU.subtract).then_inc(v_lo, 1)

    def dve_mask(dve, u, b, h):
        dve.wait_ge(s_done, u * HG + h + 1)
        if past(u, 1):
            dve.wait_ge(pT_done, (u - 1) * HG + h + 1)
        stand_apart(dve)
        for qb, (c0, c1) in enumerate(((0, P), (P, SW))):
            dve.tensor_tensor_reduce(prob[:, h, c0:c1], ps[BS[h % 2]][:, c0:c1], causal[:, 2 * P - (c1 - c0):2 * P],
                                     -SC1, 3e38, ALU.add, ALU.min, neg_max[:, h, qb:qb + 1]).then_inc(masked, 1)

    def dve_inverse(dve, u, b, p):
        dve.wait_ge(exp_done, u * 8 + 4 * p + 4)
        if past(u, 1):
            dve.wait_ge(normed, (u - 1) * 8 + 4 * p + 4)
        stand_apart(dve)
        dve.reciprocal(row_inv[:, 2 * p:2 * p + 2, :], row_sum[:, 2 * p:2 * p + 2, :]).then_inc(inv_done, 1)

    def dve_pT(dve, u, b, h):
        dve.wait_ge(pT_hi, u * HG + h + 1)
        dve.tensor_tensor(pT[1][:, h, :], ps[BP[h % 2]][:, 0:SW], pT[0][:, h, :].bitcast(F32), ALU.subtract).then_inc(pT_lo, 1)

    def dve_o(dve, u, b, p):
        dve.wait_ge(o_hi, u * 2 + p + 1)
        dve.tensor_tensor(oT[1][:, 2 * p:2 * p + 2, :], heads(BO), oT[0][:, 2 * p:2 * p + 2, :].bitcast(F32),
                          ALU.subtract).then_inc(o_lo, 1)

    def dve_add(dve, u, b, t):
        dve.wait_ge(wo_done, u * 2 + t + 1)
        row = acc[:, b * BT + t, :]
        if isinstance(u, int) and u == 0:
            dve.wait_ge(acc_zero, 1)
        dve.tensor_tensor(row, row, ps[BM[1 + t]][:, :], ALU.add).then_inc(added, 1)

    def finish_moments(dve, b):
        dve.wait_ge(added, ((NG - 1) * NB + b + 1) * 2)
        stream.post_moments(dve, 0, b)

    def vector(dve):
        for b in range(2):
            stream.pre_moments(dve, 0, b)
        for b in range(2):
            stream.pre_apply(dve, 0, b)
        dve_kvw(dve, 0)
        tail["dve_n2"](dve)
        for t in range(BT):
            stream.lo(dve, 0, t, FIRST_BANKS[t])
        tail["dve_a2"](dve)
        tail["dve_x1"](dve)
        stream.pre_moments(dve, 0, 2)
        tail["dve_n3"](dve)
        for t in range(BT, 2 * BT):
            stream.lo(dve, 0, t, FIRST_BANKS[t])
        stream.pre_apply(dve, 0, 2)
        tail["dve_a3"](dve)
        tail["dve_x1T"](dve)
        for t in range(2 * BT, NT - BT):
            stream.lo(dve, 0, t, FIRST_BANKS[t])
        dve.wait_ge(tables_in, 48)
        dve_k_cos(dve, 0, 0)
        dve_k_add(dve, 0, 0)
        dve_k_lo(dve, 0, 0)
        for p in range(2):
            dve_q_cos(dve, 0, 0, p)
            dve_q_add(dve, 0, 0, p)
            dve_q_lo(dve, 0, 0, p)
        tail["dve_bias"](dve)
        dve_v_lo(dve, 0, 0)

        def step(g, b, before, after):
            u, nb, pb = g * NB + b, (b + 1) % NB, (b - 1) % NB
            done, rnd = finishing(g, b)
            if rnd == 0:
                tail["dve_n4"](dve)
            if rnd == 1:
                finish_moments(dve, done)
            dve_mask(dve, u, b, 0)
            dve_mask(dve, u, b, 1)
            if rnd == 0:
                tail["dve_a4"](dve)
                tail["dve_x2"](dve)
            if rnd == 1:
                stream.post_apply(dve, 0, done)
                stream.add(dve, 0, done)
            if before:
                dve_o(dve, u - 1, pb, 1)
            if after:
                dve_k_cos(dve, u + 1, nb)
            dve_inverse(dve, u, b, 0)
            dve_mask(dve, u, b, 2)
            dve_mask(dve, u, b, 3)
            if after:
                dve_k_add(dve, u + 1, nb)
                dve_k_lo(dve, u + 1, nb)
            dve_inverse(dve, u, b, 1)
            if b == 2 and more(g):
                dve_kvw(dve, g + 1)
            if done is not None:
                stream.pre_moments(dve, rnd, done)
            if after:
                dve_q_cos(dve, u + 1, nb, 0)
            dve_pT(dve, u, b, 0)
            dve_pT(dve, u, b, 1)
            if after:
                dve_q_add(dve, u + 1, nb, 0)
                dve_q_lo(dve, u + 1, nb, 0)
                dve_q_cos(dve, u + 1, nb, 1)
                dve_q_add(dve, u + 1, nb, 1)
            if before:
                dve_add(dve, u - 1, pb, 0)
            if after:
                dve_q_lo(dve, u + 1, nb, 1)
                dve_v_lo(dve, u + 1, nb)
            if done is not None:
                stream.pre_apply(dve, rnd, done)
            dve_pT(dve, u, b, 2)
            dve_pT(dve, u, b, 3)
            if before:
                dve_add(dve, u - 1, pb, 1)
            if done is not None:
                stream.lo(dve, rnd, done * BT, BM[0])
            dve_o(dve, u, b, 0)
            if done is not None:
                stream.lo(dve, rnd, done * BT + 1, BM[0])

        over_groups(dve, step)
        b = NB - 2
        finish_moments(dve, b)
        dve_o(dve, U - 1, NB - 1, 1)
        stream.post_apply(dve, 0, b)
        stream.add(dve, 0, b)
        dve_add(dve, U - 1, NB - 1, 0)
        stream.pre_moments(dve, 1, b)
        dve_add(dve, U - 1, NB - 1, 1)
        finish_moments(dve, b + 1)
        stream.pre_apply(dve, 1, b)
        stream.post_apply(dve, 0, b + 1)
        stream.add(dve, 0, b + 1)
        stream.pre_moments(dve, 1, b + 1)
        stream.pre_apply(dve, 1, b + 1)

    def pool_qw(pl, g, p):
        cols = q_columns(p)
        pl.wait_ge(qw_hi, g * 2 + p + 1)
        pl.tensor_tensor(w[1][:, :, cols], w_raw[:, :, cols], w[0][:, :, cols].bitcast(F32), ALU.subtract).then_inc(qw_lo, 1)

    def pool_wo(pl, g):
        pl.wait_ge(wo_hi, g + 1)
        pl.tensor_tensor(wo[1][:, :, :], wo_raw[:, :, :], wo[0][:, :, :].bitcast(F32), ALU.subtract).then_inc(wo_lo, 1)

    def pool_k(pl, u, b):
        pl.wait_ge(k_halves, u * 2 + 2)
        pl.tensor_tensor(k_rot[:, :], k_rot[:, :], sin[:, :], ALU.mult).then_inc(k_sin, 1)

    def pool_q(pl, u, b, p):
        pl.wait_ge(q_halves, u * 4 + 2 * p + 2)
        pl.tensor_tensor(q_rot[:, :, :], q_rot[:, :, :], over_pair(sin), ALU.mult).then_inc(q_sin, 1)

    def pool_norm(pl, u, b, p):
        pl.wait_ge(inv_done, u * 2 + p + 1)
        stand_apart(pl)
        for h in (2 * p, 2 * p + 1):
            for qb, (c0, c1) in enumerate(((0, P), (P, SW))):
                pl.tensor_scalar(prob[:, h, c0:c1], prob[:, h, c0:c1], row_inv[:, h, qb:qb + 1], 1.0, ALU.mult, ALU.mult)\
                  .then_inc(normed, 1)

    def pool(pl, next_weights):
        stream.pre.inverse(pl, 0, stream.minus_half)
        stream.pre.inverse(pl, 1, stream.minus_half)
        tail["pool_n2"](pl)
        stream.pre.inverse(pl, 2, stream.minus_half)
        tail["pool_n3"](pl)
        pl.wait_ge(tables_in, 48)
        pool_qw(pl, 0, 0)
        pool_qw(pl, 0, 1)
        pool_k(pl, 0, 0)
        pool_q(pl, 0, 0, 0)
        pool_q(pl, 0, 0, 1)
        pl.memset(acc[:, :, :], 0.0).then_inc(acc_zero, 1)

        def step(g, b, before, after):
            u, nb, pb = g * NB + b, (b + 1) % NB, (b - 1) % NB
            done, rnd = finishing(g, b)
            if b == 3 and more(g):
                pool_qw(pl, g + 1, 1)
            if rnd == 0:
                tail["pool_n4"](pl)
            if rnd == 1:
                stream.post.inverse(pl, done, stream.minus_half)
            if after:
                pool_k(pl, u + 1, nb)
            pool_norm(pl, u, b, 0)
            if after:
                pool_q(pl, u + 1, nb, 0)
            pool_norm(pl, u, b, 1)
            if done is not None:
                stream.pre.inverse(pl, rnd * NB + done, stream.minus_half)
            if after:
                pool_q(pl, u + 1, nb, 1)
            if b == 0:
                pool_wo(pl, g)
            if b == 2 and more(g):
                pool_qw(pl, g + 1, 0)

        over_groups(pl, step)
        next_weights(pl)
        for b in (NB - 2, NB - 1):
            stream.post.inverse(pl, b, stream.minus_half)
            stream.pre.inverse(pl, NB + b, stream.minus_half)

    ctx.close()
    return {"sync": sync, "pool": pool, "scalar": scalar, "vector": vector, "tensor": tensor,
            "weights_over": (q_done, U * 2)}


def swiglu(nc, dram, stream, XT, acc, ps, room):
    ctx = ExitStack()
    sb = lambda name, shape, dt: ctx.enter_context(nc.sbuf_tensor(name, shape, dt))
    sem = lambda name: nc.semaphore(name).__enter__()
    sems = lambda names: [sem(name) for name in names.split()]
    GU, W = KD * 2 * P, KD * 2 * P + D
    C = 2
    TC = NT // C * P

    raw = [sb(f"ffn_raw{n}", [P, W], F32) for n in range(2)]
    w = [[sb(f"ffn_w{n}_{x}", [P, W], F32R) for x in ("hi", "lo")] for n in range(2)]
    act_gate = sb("act_gate", [P, C, TC], F32)
    h32 = sb("h32", [P, C, TC], F32)
    h = [[sb(f"h{n}_{x}", [P, C, TC], F32R) for x in ("hi", "lo")] for n in range(2)]

    raw_in = [sem(f"ffn_raw_in{n}") for n in range(2)]
    gu_hi, gu_lo, dw_hi, dw_lo = sems("gu_hi gu_lo dw_hi dw_lo")
    gate_done, up_done, gate_out, h_done, h_hi, h_lo = sems("ffn_gate_done ffn_up_done ffn_gate_out ffn_h_done ffn_h_hi ffn_h_lo")
    down_done, down_added = sem("down_done"), sem("down_added")

    def over_tiles(engine, step):
        for f in range(3):
            step(f, f % 2)
        with engine.Fori(1, (FT - 3) // 2) as i:
            step(2 * i + 1, 1)
            step(2 * i + 2, 0)
        for f in (FT - 2, FT - 1):
            step(f, f % 2)

    def ends(f):
        return isinstance(f, int) and f == FT - 1

    def sync(sp):
        sp.wait_ge(*room)
        for f in range(2):
            sp.dma_start(raw[f][:, :], dram["ffn_w"][f]).then_inc(raw_in[f], 16)
        with sp.Fori(1, (FT - 1) // 2) as i:
            for n in range(2):
                sp.wait_ge(dw_lo, 2 * i + n - 1)
                sp.dma_start(raw[n][:, :], dram["ffn_w"][2 * i + n]).then_inc(raw_in[n], 16)
        sp.wait_ge(dw_lo, FT - 2)
        sp.dma_start(raw[(FT - 1) % 2][:, :], dram["ffn_w"][FT - 1]).then_inc(raw_in[(FT - 1) % 2], 16)

    def tensor(pe):
        def step(f, n):
            pe.wait_ge(gu_lo, f + 1)
            for c in range(C):
                if isinstance(f, int) and f == 0:
                    if c == 1:
                        for t in range(NT // C, NT):
                            stream.turn(pe, 1, t, t)
                    pe.wait_ge(stream.lo_out, NT + (c + 1) * (NT // C))
                for up, done in ((0, gate_done), (1, up_done)):
                    if past(f, 1):
                        pe.wait_ge(h_done, (f - 1) * C + c + 1)
                    for k in range(KD):
                        cols = slice(k * 2 * P + up * P, k * 2 * P + up * P + P)
                        xs = slice(c * TC, (c + 1) * TC)
                        last = split_product(pe, ps[2 * c + up][:, :], (w[n][0][:, cols], w[n][1][:, cols]),
                                             (XT[0][:, k, xs], XT[1][:, k, xs]), k == 0, k == KD - 1)
                    last.then_inc(done, 1)
            if past(f, 1) and not ends(f):
                down((f - 1,), f - 1, 1 - n)

        def down(tiles, f, n):
            for t in range(NT):
                c, ts = t // (NT // C), slice(t % (NT // C) * P, (t % (NT // C) + 1) * P)
                if t >= 4 or past(f, 1):
                    pe.wait_ge(down_added, f * NT + t - 3)
                for number, tile in enumerate(tiles):
                    if t == 0:
                        pe.wait_ge(dw_lo, tile + 1)
                    if t % (NT // C) == 0:
                        pe.wait_ge(h_lo, tile * C + c + 1)
                    m = (n + number) % 2
                    last = split_product(pe, ps[4 + t % 4][:, :], (h[m][0][:, c, ts], h[m][1][:, c, ts]),
                                         (w[m][0][:, GU:W], w[m][1][:, GU:W]), number == 0, number == len(tiles) - 1)
                last.then_inc(down_done, 1)

        over_tiles(pe, step)
        down((FT - 2, FT - 1), FT - 2, (FT - 2) % 2)

    def scalar(act):
        def step(f, n):
            for c in range(C):
                act.wait_ge(gate_done, f * C + c + 1)
                if past(f, 1):
                    act.wait_ge(h_done, (f - 1) * C + c + 1)
                act.activation(act_gate[:, c, :], ps[2 * c][:, :], ACT.Silu).then_inc(gate_out, 1)
                if c == 0 and isinstance(f, int) and f == 0:
                    for t in range(NT // C, NT):
                        stream.hi(act, 1, t, t)
            for c in range(C):
                act.wait_ge(h_done, f * C + c + 1)
                act.activation(h[n][0][:, c, :], h32[:, c, :], ACT.Copy).then_inc(h_hi, 1)

        over_tiles(act, step)

    def vector(dve):
        def step(f, n):
            for c in range(C):
                dve.wait_ge(gate_out, f * C + c + 1)
                dve.wait_ge(up_done, f * C + c + 1)
                if past(f, 1):
                    dve.wait_ge(h_lo, (f - 1) * C + c + 1)
                dve.tensor_tensor(h32[:, c, :], ps[2 * c + 1][:, :], act_gate[:, c, :], ALU.mult).then_inc(h_done, 1)
                if c == 0 and isinstance(f, int) and f == 0:
                    for t in range(NT // C, NT):
                        stream.lo(dve, 1, t, t)
            if past(f, 1) and not ends(f):
                add(f - 1)

        def add(f):
            for t in range(NT):
                dve.wait_ge(down_done, f * NT + t + 1)
                if past(f, 1):
                    dve.wait_ge(down_added, (f - 1) * NT + t + 1)
                    dve.tensor_tensor(acc[:, t, :], acc[:, t, :], ps[4 + t % 4][:, :], ALU.add).then_inc(down_added, 1)
                else:
                    dve.tensor_copy(acc[:, t, :], ps[4 + t % 4][:, :]).then_inc(down_added, 1)
                if isinstance(f, int) and f == FT - 2 and t % BT == BT - 1:
                    dve.wait_ge(down_added, f * NT + t + 1)
                    b = t // BT
                    stream.post_moments(dve, 1, b)
                    if b:
                        stream.post_apply(dve, 1, b - 1)
            if isinstance(f, int) and f == FT - 2:
                stream.post_apply(dve, 1, NB - 1)
                stream.add(dve, 1, NB - 1)

        over_tiles(dve, step)
        add(FT - 2)

    def split(pl, f, n, cols, hi, lo, used, count):
        if past(f, 2):
            pl.wait_ge(used, (f - 1) * count)
        stand_apart(pl)
        pl.tensor_scalar(w[n][0][:, cols], raw[n][:, cols], 1.0, 1.0, ALU.mult, ALU.mult).then_inc(hi, 1)
        pl.wait_ge(hi, f + 1)
        pl.tensor_tensor(w[n][1][:, cols], raw[n][:, cols], w[n][0][:, cols].bitcast(F32), ALU.subtract).then_inc(lo, 1)

    def split_gate_up(pl, f, n):
        pl.wait_ge(raw_in[n], (f - n) * 8 + 16)
        split(pl, f, n, slice(0, GU), gu_hi, gu_lo, up_done, C)

    def split_down(pl, f, n):
        split(pl, f, n, slice(GU, W), dw_hi, dw_lo, down_done, NT)

    def first_weights(pl):
        split_gate_up(pl, 0, 0)

    def pool(pl):
        def step(f, n, ahead=True):
            for c in range(C):
                pl.wait_ge(h_hi, f * C + c + 1)
                pl.tensor_tensor(h[n][1][:, c, :], h32[:, c, :], h[n][0][:, c, :].bitcast(F32), ALU.subtract).then_inc(h_lo, 1)
            if ahead:
                split_down(pl, f + 1, 1 - n)
                split_gate_up(pl, f + 2, n)

        split_down(pl, 0, 0)
        split_gate_up(pl, 1, 1)
        for f in range(2):
            step(f, f)
        with pl.Fori(1, (FT - 3) // 2) as i:
            step(2 * i, 0)
            step(2 * i + 1, 1)
        step(FT - 3, (FT - 3) % 2)
        step(FT - 2, (FT - 2) % 2, False)
        split_down(pl, FT - 1, (FT - 1) % 2)
        step(FT - 1, (FT - 1) % 2, False)
        for b in range(NB):
            stream.post.inverse(pl, NB + b, stream.minus_half)
            if b:
                stream.add(pl, 1, b - 1)

    ctx.close()
    return {"sync": sync, "first_weights": first_weights, "pool": pool, "scalar": scalar, "vector": vector,
            "tensor": tensor}


def host_layout(inp):
    c = np.ascontiguousarray
    wkv = np.asarray(inp["L0_attn_Wkv"])
    wk, wv = wkv[:, :HD0], wkv[:, HD0:]
    a = {
        "x": c(np.asarray(inp["L0_attn_hidden_states"]).reshape(NB * TB, D)),
        "wq0": c(inp["L0_attn_Wq"]),
        "wkv0": c(np.concatenate([np.tile(wk, (1, HPT)), wv], 1).reshape(KD, P, P + HD0).transpose(1, 0, 2)),
        "wo0": c(inp["L0_attn_Wo"]),
        "wf0": c(np.asarray(inp["L0_ffn_W"]).T),
        "bias0": c(inp["L0_ffn_bias"]),
        "a0": c(np.asarray(inp["L0_ffn_A"]).reshape(NEXP * RANK, D)),
        "bf0": c(np.asarray(inp["L0_ffn_Bf"]).transpose(0, 2, 1).reshape(NEXP * RANK, D)),
        "gate_w": c(np.stack([np.repeat(np.asarray(inp[n]), RANK).reshape(ER, P).T
                              for n in ("L0_ffn_coeffs", "L0_ffn_scales")], 1)),
    }
    columns = np.concatenate([np.asarray(inp["L1_attn_W" + n]).reshape(NG, -1, D) for n in "kvq"], 1)
    a["w1"] = c(columns.reshape(NG, GW, KD, P).transpose(0, 3, 2, 1))
    a["wo1"] = c(np.asarray(inp["L1_attn_Wo"]).T.reshape(NG, HG, P, D).transpose(0, 2, 1, 3))
    pad = ((0, FT * P - F), (0, 0))
    gate, up = (np.pad(np.asarray(inp["L1_ffn_W_" + n]), pad).reshape(FT, P, KD, P).transpose(0, 3, 2, 1)
                for n in ("gate", "up"))
    down = np.pad(np.asarray(inp["L1_ffn_W_down"]).T, pad).reshape(FT, P, D)
    a["ffn_w"] = c(np.concatenate([np.concatenate([gate, up], 3).reshape(FT, P, KD * 2 * P), down], 2))
    return a


def build(nc, dram, out):
    with ExitStack() as ctx:
        sb = lambda name, shape, dt: ctx.enter_context(nc.sbuf_tensor(name, shape, dt))
        sem = lambda name: nc.semaphore(name).__enter__()
        sems = lambda names: [sem(name) for name in names.split()]
        X = sb("X", [P, NT, D], F32)
        ident = sb("ident_sb", [P, P], F32)
        minus_half = sb("minus_half", [P, NT], F32)
        ps = [ctx.enter_context(nc.psum_tensor(f"bank{i}", [P, 512], F32)) for i in range(8)]
        ident_in, half_set, out_done = sems("ident_in half_set out_done")
        consts = {"ident": ident, "minus_half": minus_half, "in": ident_in}

        l0 = layer0(nc, dram, sb, X, ps, consts)
        split = lambda name, shape: [sb(f"{name}_{x}", shape, F32R) for x in ("hi", "lo")]
        early = {"pT": split("pT1", [P, HG, SW]), "oT": split("oT1", [P, HG, TB]), "wo": split("wo1", [P, HG, D]),
                 "prob": sb("prob1", [P, HG, SW], F32)}
        XT = [sb(f"XT_{x}", [P, KD, NB * TB], F32R) for x in ("hi", "lo")]
        acc = sb("acc", [P, NT, D], F32)
        stream = Stream(sb, sem, X, XT, acc, ps, ident, minus_half, l0["x2_done"])
        attention = layer1_attention(nc, dram, early, stream, XT, acc, ps, consts, l0["tail"], l0["heads_over"])
        ffn = swiglu(nc, dram, stream, XT, acc, ps, attention["weights_over"])

        block = ctx.enter_context(nc.Block())

        @block.sync
        def _(sp):
            sp.dma_start(ident[:, :], dram["ident"]).then_inc(ident_in, 16)
            l0["sync"](sp)
            attention["sync"](sp)
            ffn["sync"](sp)
            rows = out.rearrange("(n p) d -> p n d", p=P)
            for t in range(NT):
                if t < NT - BT:
                    sp.wait_ge(stream.summed, NT + t + 1)
                else:
                    sp.wait_ge(stream.last_summed, t - (NT - BT) + 1)
                sp.dma_start(rows[:, t, :], X[:, t, :]).then_inc(out_done, 16)
            sp.wait_ge(out_done, NT * 16)

        @block.gpsimd
        def _(pl):
            pl.memset(minus_half[:, :], -0.5).then_inc(half_set, 1)
            pl.wait_ge(half_set, 1)
            l0["pool"](pl)
            attention["pool"](pl, ffn["first_weights"])
            ffn["pool"](pl)

        @block.scalar
        def _(act):
            l0["scalar"](act)
            attention["scalar"](act)
            ffn["scalar"](act)

        @block.vector
        def _(dve):
            l0["vector"](dve)
            attention["vector"](dve)
            ffn["vector"](dve)

        @block.tensor
        def _(pe):
            l0["tensor"](pe)
            attention["tensor"](pe)
            ffn["tensor"](pe)


def kernel(**inputs):
    import concourse.bacc as bacc
    from concourse.bass_utils import run_bass_kernel_spmd

    nc = bacc.Bacc("TRN2", target_bir_lowering=False, num_devices=1)
    arrays = {**host_layout(inputs), **constants()}
    dram = {name: nc.dram_tensor(f"in_{name}_dram", a.shape, mybir.dt.from_np(a.dtype), kind="ExternalInput").ap()
            for name, a in arrays.items()}
    out = nc.dram_tensor("out_dram", [NB * TB, D], F32, kind="ExternalOutput").ap()
    build(nc, dram, out)
    result = run_bass_kernel_spmd(nc, [{f"in_{name}_dram": a for name, a in arrays.items()}], core_ids=[0])
    return result.results[0]["out_dram"].reshape(NB, TB, D)
```
